# Optimizing a Trainium2 kernel written in Bass

```python
import numpy as np
import jax
import jax.numpy as jnp

def _softmax(x, axis=-1):
    return jax.nn.softmax(x, axis=axis)

def _gelu(x):
    return jax.nn.gelu(x, approximate=True)

def _silu(x):
    return jax.nn.silu(x)

def _sigmoid(x):
    return jax.nn.sigmoid(x)

def _layernorm(x, axis=-1, eps=1e-05):
    m = jnp.mean(x, axis=axis, keepdims=True)
    v = jnp.var(x, axis=axis, keepdims=True)
    return (x - m) / jnp.sqrt(v + eps)

def _scatter_add(tgt, idx, src, axis=0):
    return tgt.at[idx].add(src)

def _segment_sum(src, seg, n):
    return jax.ops.segment_sum(src, seg, n)
kernel_name = 'mk_adj_resnorm_d4_adj_r2_143cbc'

def setup_inputs(seed: int=0):
    np.random.seed(seed)
    _w = jnp.asarray

    def _rec_inputs():
        import jax
        import jax.numpy as jnp
        _gk = jax.random.key(seed)
        x = -0.0005207 + 1.001 * jax.random.normal(jax.random.fold_in(_gk, 1), (8, 1024, 128), jnp.float32)
        _a = jax.random.bernoulli(jax.random.fold_in(_gk, 2), 0.00390625, (8, 1024, 1024))
        _a = jnp.logical_or(_a, jnp.swapaxes(_a, -1, -2))
        _a = jnp.logical_or(_a, jnp.eye(1024, dtype=bool))
        _af = _a.astype(jnp.float32)
        adj = _af
        _nm = jnp.ones((8, 1024), dtype=bool)
        nodemask = jnp.where(_nm, 1.0, 0.0).astype(jnp.float32)
        return (x, adj, nodemask)
    x, adj, nodemask = _rec_inputs()

    def _L0_gnn_setup():
        import jax, jax.numpy as jnp
        import numpy as np
        B, N, IN_DIM, OUT_DIM, H = (8, 512, 128, 128, 4)
        D = OUT_DIM // H
        NEG_INF = -9000000000000000.0
        LRELU_SLOPE = 0.2
        key = jax.random.key(seed)
        k1, k2, k3, k4 = jax.random.split(key, 4)
        x = jax.random.normal(k1, (B, N, IN_DIM), dtype=jnp.float32)
        adj = jax.random.randint(k2, (B, N, N), 0, 2).astype(jnp.float32)
        W = jax.random.normal(k3, (IN_DIM, H * D), dtype=jnp.float32) * jnp.sqrt(2.0 / (IN_DIM + H * D))
        a = jax.random.normal(k4, (H, 2 * D), dtype=jnp.float32) * jnp.sqrt(2.0 / (H + 2 * D))
        return {'x': x, 'adj': adj, 'W': W, 'a': a}
    _L0_gnn_all = _L0_gnn_setup()
    _L0_gnn_in = {k: v for k, v in _L0_gnn_all.items() if k in ('W', 'a')}
    del _L0_gnn_all

    def _L1_gnn_setup():
        import jax, jax.numpy as jnp
        import numpy as np
        B, N, IN_DIM, OUT_DIM = (8, 1024, 128, 128)
        EDGE_P = 0.02
        MASK_P = 0.9
        key = jax.random.key(seed)
        ks = jax.random.split(key, 8)
        x = jax.random.normal(ks[0], (B, N, IN_DIM), dtype=jnp.float32)
        adj = (jax.random.uniform(ks[1], (B, N, N)) < EDGE_P).astype(jnp.float32)
        mask = (jax.random.uniform(ks[2], (B, N)) < MASK_P).astype(jnp.float32)
        lim1 = 1.0 / np.sqrt(IN_DIM)
        W = jax.random.uniform(ks[3], (OUT_DIM, IN_DIM), minval=-lim1, maxval=lim1, dtype=jnp.float32)
        b = jax.random.uniform(ks[4], (OUT_DIM,), minval=-lim1, maxval=lim1, dtype=jnp.float32)
        lim2 = 1.0 / np.sqrt(2 * OUT_DIM)
        a1 = jax.random.uniform(ks[5], (OUT_DIM,), minval=-lim2, maxval=lim2, dtype=jnp.float32)
        a2 = jax.random.uniform(ks[6], (OUT_DIM,), minval=-lim2, maxval=lim2, dtype=jnp.float32)
        att_b = jax.random.uniform(ks[7], (), minval=-lim2, maxval=lim2, dtype=jnp.float32)
        return {'x': x, 'adj': adj, 'mask': mask, 'W': W, 'b': b, 'a1': a1, 'a2': a2, 'att_b': att_b}
    _L1_gnn_all = _L1_gnn_setup()
    _L1_gnn_in = {k: v for k, v in _L1_gnn_all.items() if k in ('W', 'b', 'a1', 'a2', 'att_b')}
    del _L1_gnn_all

    def _L2_gnn_setup():
        import jax, jax.numpy as jnp
        import numpy as np
        GROUPS = [list(range(25)), [0, 1, 2, 3, 4, 5, 6, 7, 8], [0, 9, 10, 11, 12, 13, 14], [6, 7, 8, 12, 13, 14], [3, 4, 5, 9, 10, 11]]
        B, N, D_IN, D_HID = (4096, 25, 128, 256)

        def _graph_conv(x, adj, W, b):
            n = adj.shape[-1]
            A = adj + jnp.eye(n, dtype=adj.dtype)
            deg = jnp.sum(A, axis=-1)
            deg_safe = jnp.where(deg == 0, 1.0, deg)
            dinv = jnp.where(deg == 0, 0.0, deg_safe ** (-0.5))
            norm_adj = dinv[:, :, None] * A * dinv[:, None, :]
            support = jnp.einsum('bnd,de->bne', x, W)
            out = jnp.einsum('bnm,bme->bne', norm_adj, support) + b
            return jax.nn.relu(out)
        key = jax.random.key(seed)
        ks = jax.random.split(key, 7)
        s1 = float(np.sqrt(6.0 / (D_IN + D_HID)))
        s2 = float(np.sqrt(6.0 / (D_HID + D_IN)))
        return {'x': jax.random.normal(ks[0], (B, N, D_IN), dtype=jnp.float32), 'adj': jax.random.uniform(ks[1], (B, N, N), dtype=jnp.float32), 'W1': jax.random.uniform(ks[2], (5, D_IN, D_HID), jnp.float32, -s1, s1), 'b1': jnp.zeros((5, D_HID), dtype=jnp.float32), 'W2': jax.random.uniform(ks[3], (5, D_HID, D_IN), jnp.float32, -s2, s2), 'b2': jnp.zeros((5, D_IN), dtype=jnp.float32), 'fusion_w': jnp.ones((5,), dtype=jnp.float32)}
    _L2_gnn_all = _L2_gnn_setup()
    _L2_gnn_in = {k: v for k, v in _L2_gnn_all.items() if k in ('W1', 'b1', 'W2', 'b2', 'fusion_w')}
    del _L2_gnn_all

    def _L3_gnn_setup():
        import math
        import jax, jax.numpy as jnp
        import numpy as np
        B, N, D, H = (32, 256, 128, 8)
        HD = D // H
        key = jax.random.key(seed)
        ks = jax.random.split(key, 9)
        h = jax.random.normal(ks[0], (B, N, D), dtype=jnp.float32)
        edge = jax.random.normal(ks[1], (B, N, N), dtype=jnp.float32)
        adj = jax.random.uniform(ks[2], (B, N, N)) < 0.5
        adj_mask = adj | jnp.eye(N, dtype=bool)[None]
        s = 1.0 / math.sqrt(D)
        W_q = jax.random.normal(ks[3], (D, D), dtype=jnp.float32) * s
        W_k = jax.random.normal(ks[4], (D, D), dtype=jnp.float32) * s
        W_v = jax.random.normal(ks[5], (D, D), dtype=jnp.float32) * s
        W_e = jax.random.normal(ks[6], (H, 1), dtype=jnp.float32)
        W_o = jax.random.normal(ks[7], (D, D), dtype=jnp.float32) * s
        return {'h': h, 'edge': edge, 'adj_mask': adj_mask, 'W_q': W_q, 'W_k': W_k, 'W_v': W_v, 'W_e': W_e, 'W_o': W_o}
    _L3_gnn_all = _L3_gnn_setup()
    _L3_gnn_in = {k: v for k, v in _L3_gnn_all.items() if k in ('W_q', 'W_k', 'W_v', 'W_e', 'W_o')}
    del _L3_gnn_all
    return {'x': x, 'adj': adj, 'nodemask': nodemask, 'L0_gnn_W': _L0_gnn_in['W'], 'L0_gnn_a': _L0_gnn_in['a'], 'L1_gnn_W': _L1_gnn_in['W'], 'L1_gnn_b': _L1_gnn_in['b'], 'L1_gnn_a1': _L1_gnn_in['a1'], 'L1_gnn_a2': _L1_gnn_in['a2'], 'L1_gnn_att_b': _L1_gnn_in['att_b'], 'L2_gnn_W1': _L2_gnn_in['W1'], 'L2_gnn_b1': _L2_gnn_in['b1'], 'L2_gnn_W2': _L2_gnn_in['W2'], 'L2_gnn_b2': _L2_gnn_in['b2'], 'L2_gnn_fusion_w': _L2_gnn_in['fusion_w'], 'L3_gnn_W_q': _L3_gnn_in['W_q'], 'L3_gnn_W_k': _L3_gnn_in['W_k'], 'L3_gnn_W_v': _L3_gnn_in['W_v'], 'L3_gnn_W_e': _L3_gnn_in['W_e'], 'L3_gnn_W_o': _L3_gnn_in['W_o']}

def reference(x, adj, nodemask, L0_gnn_W, L0_gnn_a, L1_gnn_W, L1_gnn_b, L1_gnn_a1, L1_gnn_a2, L1_gnn_att_b, L2_gnn_W1, L2_gnn_b1, L2_gnn_W2, L2_gnn_b2, L2_gnn_fusion_w, L3_gnn_W_q, L3_gnn_W_k, L3_gnn_W_v, L3_gnn_W_e, L3_gnn_W_o):
    import jax
    import jax.numpy as jnp

    def _L0_gnn_ref(x, adj, W, a):
        import jax, jax.numpy as jnp
        import numpy as np
        B, N, IN_DIM, OUT_DIM, H = (8, 512, 128, 128, 4)
        D = OUT_DIM // H
        NEG_INF = -9000000000000000.0
        LRELU_SLOPE = 0.2
        h = jnp.einsum('bni,io->bno', x, W).reshape(x.shape[0], x.shape[1], H, D)
        h = h.transpose(0, 2, 1, 3)
        a1, a2 = (a[:, :D], a[:, D:])
        e_i = jnp.einsum('bhnd,hd->bhn', h, a1)
        e_j = jnp.einsum('bhmd,hd->bhm', h, a2)
        e = e_i[:, :, :, None] + e_j[:, :, None, :]
        e = jnp.where(e > 0, e, LRELU_SLOPE * e)
        e = jnp.where(adj[:, None, :, :] > 0, e, NEG_INF)
        attn = jax.nn.softmax(e, axis=-1)
        out = jnp.einsum('bhnm,bhmd->bhnd', attn, h)
        out = out.transpose(0, 2, 1, 3).reshape(x.shape[0], x.shape[1], H * D)
        return out

    def _L1_gnn_ref(x, adj, mask, W, b, a1, a2, att_b):
        import jax, jax.numpy as jnp
        import numpy as np
        B, N, IN_DIM, OUT_DIM = (8, 1024, 128, 128)
        EDGE_P = 0.02
        MASK_P = 0.9
        h = jnp.einsum('bni,di->bnd', x, W) + b
        s1 = h @ a1
        s2 = h @ a2
        logits = s1[:, :, None] + s2[:, None, :] + att_b
        att = jax.nn.sigmoid(logits) * adj
        att = att * mask[:, :, None] * mask[:, None, :]
        att = att / (jnp.sum(att, axis=-1, keepdims=True) + 1e-08)
        h_new = jnp.einsum('bij,bjd->bid', att, h)
        return h_new * mask[:, :, None]

    def _L2_gnn_ref(x, adj, W1, b1, W2, b2, fusion_w):
        import jax, jax.numpy as jnp
        import numpy as np
        GROUPS = [list(range(25)), [0, 1, 2, 3, 4, 5, 6, 7, 8], [0, 9, 10, 11, 12, 13, 14], [6, 7, 8, 12, 13, 14], [3, 4, 5, 9, 10, 11]]
        B, N, D_IN, D_HID = (4096, 25, 128, 256)

        def _graph_conv(x, adj, W, b):
            n = adj.shape[-1]
            A = adj + jnp.eye(n, dtype=adj.dtype)
            deg = jnp.sum(A, axis=-1)
            deg_safe = jnp.where(deg == 0, 1.0, deg)
            dinv = jnp.where(deg == 0, 0.0, deg_safe ** (-0.5))
            norm_adj = dinv[:, :, None] * A * dinv[:, None, :]
            support = jnp.einsum('bnd,de->bne', x, W)
            out = jnp.einsum('bnm,bme->bne', norm_adj, support) + b
            return jax.nn.relu(out)
        norm_w = jax.nn.softmax(fusion_w)
        fused = jnp.zeros_like(x)
        for g, idx_list in enumerate(GROUPS):
            idx = jnp.asarray(idx_list)
            x_g = x[:, idx, :]
            adj_g = adj[:, idx][:, :, idx]
            h = _graph_conv(x_g, adj_g, W1[g], b1[g])
            out_g = _graph_conv(h, adj_g, W2[g], b2[g])
            fused = fused.at[:, idx, :].add(norm_w[g] * out_g)
        return fused

    def _L3_gnn_ref(h, edge, adj_mask, W_q, W_k, W_v, W_e, W_o):
        import math
        import jax, jax.numpy as jnp
        import numpy as np
        B, N, D, H = (32, 256, 128, 8)
        HD = D // H
        b, n, _ = h.shape
        q = (h @ W_q.T).reshape(b, n, H, HD).transpose(0, 2, 1, 3)
        k = (h @ W_k.T).reshape(b, n, H, HD).transpose(0, 2, 1, 3)
        v = (h @ W_v.T).reshape(b, n, H, HD).transpose(0, 2, 1, 3)
        edge_bias = jnp.einsum('bij,h->bhij', edge, W_e[:, 0])
        scores = jnp.einsum('bhid,bhjd->bhij', q, k) / math.sqrt(HD) + edge_bias
        scores = jnp.where(adj_mask[:, None], scores, -jnp.inf)
        attn = jax.nn.softmax(scores, axis=-1)
        out = jnp.einsum('bhij,bhjd->bhid', attn, v)
        out = out.transpose(0, 2, 1, 3).reshape(b, n, D)
        return out @ W_o.T
    x = _layernorm(x + _L0_gnn_ref(x, adj, L0_gnn_W, L0_gnn_a), axis=-1)
    x = _layernorm(x + _L1_gnn_ref(x, adj, nodemask, L1_gnn_W, L1_gnn_b, L1_gnn_a1, L1_gnn_a2, L1_gnn_att_b), axis=-1)
    x = _layernorm(x + _L2_gnn_ref(x, adj, L2_gnn_W1, L2_gnn_b1, L2_gnn_W2, L2_gnn_b2, L2_gnn_fusion_w), axis=-1)
    x = _layernorm(x + _L3_gnn_ref(x, adj, adj, L3_gnn_W_q, L3_gnn_W_k, L3_gnn_W_v, L3_gnn_W_e, L3_gnn_W_o), axis=-1)
    return x

_drawn_inputs = setup_inputs


def setup_inputs(seed=0):
    import zlib

    import numpy as np

    out = dict(_drawn_inputs(seed))
    spreads = {'L2_gnn_b1': (0.0, 0.8), 'L2_gnn_b2': (0.0, 2.0), 'L2_gnn_fusion_w': (1.0, 0.6)}
    factors = {'L1_gnn_a1': 26.092, 'L2_gnn_W1': 3.874, 'L2_gnn_W2': 3.347, 'L3_gnn_W_e': 64.0}
    for name, (base, spread) in spreads.items():
        noise = np.random.default_rng([zlib.crc32(name.encode()), seed]).standard_normal(out[name].shape)
        drawn = base * np.exp(spread * noise) if base else spread * noise
        out[name] = jnp.asarray(drawn.astype(out[name].dtype))
    for name, factor in factors.items():
        out[name] = (out[name] * factor).astype(out[name].dtype)
    return out
```

```python
from contextlib import ExitStack

import concourse.bass as bass
import numpy as np
from concourse import mybir

ALU = mybir.AluOpType
ACT = mybir.ActivationFunctionType
F32 = mybir.dt.float32
BF16 = mybir.dt.bfloat16
AX_X = mybir.AxisListType.X
RMAX = bass.bass_isa.ReduceOp.max

P = 128
B, N, D = 8, 1024, 128
NT = N // P
HALF = 512
H0, D0 = 4, 32
C0 = 64
H3, D3 = 8, 16
C3 = 32
G, GN, DH = 5, 25, 256
GROUPS = [list(range(25)), [0, 1, 2, 3, 4, 5, 6, 7, 8], [0, 9, 10, 11, 12, 13, 14],
          [6, 7, 8, 12, 13, 14], [3, 4, 5, 9, 10, 11]]
SETUP_V = 24
BIG = float(2.0 ** 100)
EPS = 1e-5
TERMS = [(0, 0), (0, 1), (1, 0), (1, 1), (0, 2), (2, 0)]
KQ = D3 * len(TERMS)


def build(nc, a):
    with ExitStack() as ctx:
        def sb(name, shape, dt=F32):
            return ctx.enter_context(nc.sbuf_tensor(name, shape, dt))

        def sem(name):
            return ctx.enter_context(nc.semaphore(name))

        ps = ctx.enter_context(nc.psum_tensor("ps", [P, 8, 512], F32))

        def banks(first, count):
            return ps[:, first:first + count, :].rearrange("p b n -> p (b n)")

        ident = sb("ident", [P, P])
        identb = sb("identb", [P, P], BF16)
        ones = sb("ones", [P, P])
        w0x = sb("w0x", [P, D + H0])
        w0s = sb("w0s", [P, H0, P])
        w1x = sb("w1x", [P, D + 1])
        w1s = sb("w1s", [P, P])
        b1x = sb("b1x", [1, D + 1])
        w2a = sb("w2a", [P, G * DH])
        b2a = sb("b2a", [P, G * 2])
        w2b = sb("w2b", [P, G * 2, D])
        b2b = sb("b2b", [1, G * D])
        gpair = sb("gpair", [GN, G, GN])
        grow = sb("grow", [GN, G])
        gw = sb("gw", [GN, G])
        wT = sb("wT", [P, 4, P])
        web = sb("web", [P, H3])
        maskall = sb("maskall", [P, B * NT])
        ablk = sb("ablk", [P, 2 * H0])
        acol = sb("acol", [P, 3])
        attb = sb("attb", [1, 1])
        fus = sb("fus", [GN, G])
        small = sb("small", [P, 8])
        epst = sb("epst", [P, 1])

        adj = sb("adj", [P, NT, N])
        adjT = sb("adjT", [P, NT, N], BF16)
        neg = sb("neg", [P, NT, N], BF16)
        xr = sb("xr", [P, NT, D])
        yr = sb("yr", [P, NT, D])
        tmp = sb("tmp", [P, NT, D])
        xT = sb("xT", [P, N])
        ring = sb("ring", [P, 8, N])
        oT = sb("oT", [P, 2, N])
        v0 = sb("v0", [P, NT, H0, C0])
        hx = sb("hx", [P, NT, D + 1])
        tt = sb("tt", [P, NT, H0])
        tB = sb("tB", [P, NT, H0])
        tE = sb("tE", [P, NT, H0])
        tmx = sb("tmx", [P, H0])
        tall = sb("tall", [P, H0])
        den = sb("den", [P, NT, H3])
        emp = sb("emp", [P, NT, H0])
        hsum = sb("hsum", [P, D])
        s2 = sb("s2", [P, NT])
        msk = sb("msk", [P, NT])
        fac = sb("fac", [P, NT])
        stats = sb("stats", [P, NT, 6])
        mv = sb("mv", [P, NT, 2])
        sd = sb("sd", [P, NT])
        a25 = sb("a25", [GN, GN])
        agr = sb("agr", [GN, G, GN])
        nT = sb("nT", [GN, G, GN])
        deg = sb("deg", [GN, 4, G])
        nadj = sb("nadj", [GN, G, GN])
        x25T = sb("x25T", [P, GN])
        h25 = sb("h25", [P, G * 2, GN])
        f25 = sb("f25", [GN, D])
        qk_all = sb("qk", [P, 2, H3 * N], BF16)
        qk = qk_all[0:KQ + 1].rearrange("p s (h n) -> p s h n", h=H3)
        v3 = sb("v3", [P, NT, H3, C3])
        mx = sb("mx", [P, H3, NT])
        sh = sb("sh", [P, H3, NT])
        shT = sb("shT", [H3 * NT, P], BF16)
        qs, ks = qk[:, 0], qk[:, 1]

        negT = adjT
        cs = qk_all[:, 0, :].bitcast(F32).rearrange("p (h n) -> p h n", h=H0)
        flat = ring[:].rearrange("p a n -> p (a n)")
        raw = ring[:, 6].rearrange("p (w n) -> p w n", w=NT)
        mrow = ring[0:B * NT, 7, 0:P]
        w0t = ring[:, 7, P:2 * P]
        sup1 = flat[0:GN, 0:G * DH]
        sup2 = flat[0:GN, 2 * N:2 * N + G * D]
        o25 = flat[0:GN, 3 * N:3 * N + G * D].rearrange("p (g d) -> p g d", g=G)
        parts = flat[:, 0:3 * N].bitcast(BF16).rearrange("p (s c n) -> p s c n", s=2, c=3)
        rest = ring[:, 3:5]
        junk = ring[:, 5:7]

        PER, HEAD = {}, {}

        def signal(name, per=1, head=0):
            s = sem(name)
            PER[s], HEAD[s] = per, head
            return s

        weights_in = sem("weights_in")
        waits_alone = sem("waits_alone")
        setup_t = sem("setup_t")
        setup_v = sem("setup_v")
        setup_a = sem("setup_a")
        setup_g = sem("setup_g")
        adj_in = signal("adj_in", 16)
        x_in = signal("x_in", 16)
        stack_in = signal("stack_in", 16 * 2 * len(TERMS) * H3)
        shift_in = signal("shift_in", 16)
        stored = signal("stored", 16, head=1)
        adjT_ps = signal("adjT_ps", NT)
        adjT_ok = signal("adjT_ok", NT)
        neg_ok = signal("neg_ok", NT)
        negT_ok = signal("negT_ok")
        mask_ok = signal("mask_ok")
        agr_ok = signal("agr_ok", 2)
        deg_ok = signal("deg_ok", 3)
        degroot_ok = signal("degroot_ok")
        dinv_ok = signal("dinv_ok", 3)
        nadj_ok = signal("nadj_ok")
        nadjT_ps = signal("nadjT_ps")
        nadjT_ok = signal("nadjT_ok")
        xT_ps = signal("xT_ps", 3)
        xT_ok = signal("xT_ok", 3)
        h0_ps = signal("h0_ps")
        h0_ok = signal("h0_ok", 3)
        t_ok = signal("t_ok", 3)
        tmax_ok = signal("tmax_ok")
        tall_ok = signal("tall_ok")
        td_ok = signal("td_ok")
        tBE_ok = signal("tBE_ok", 2)
        v0_ok = signal("v0_ok", 2)
        hsum_ps = signal("hsum_ps")
        hsum_ok = signal("hsum_ok")
        s0_ps = signal("s0_ps", H0)
        c_relu = signal("c_relu", H0)
        c_ok = signal("c_ok", H0)
        p0_ok = signal("p0_ok", H0 * NT)
        pv0 = signal("pv0", 2 * NT)
        oT0_ok = signal("oT0_ok", 2)
        o0_ps = signal("o0_ps")
        emp_ok = signal("emp_ok")
        den0_ok = signal("den0_ok", 2)
        eh_ok = signal("eh_ok")
        y_ok = signal("y_ok", 6, head=1)
        ln_stats = signal("ln_stats", 4 * NT)
        ln_aggr = signal("ln_aggr", 4 * NT)
        ln_root = signal("ln_root", 4)
        ln_rec = signal("ln_rec", 4)
        ln_ok = signal("ln_ok", 4 * NT)
        h1_ps = signal("h1_ps")
        h1_ok = signal("h1_ok", 3)
        s2_ok = signal("s2_ok", 3)
        s1_ps = signal("s1_ps")
        sig_ok = signal("sig_ok", NT)
        p1_ok = signal("p1_ok", NT)
        pv1 = signal("pv1")
        fac_ok = signal("fac_ok", 5)
        x25_ps = signal("x25_ps")
        x25_ok = signal("x25_ok")
        sup1_ps = signal("sup1_ps")
        sup1_ok = signal("sup1_ok")
        h25_ps = signal("h25_ps")
        h25_ok = signal("h25_ok", 2)
        sup2_ps = signal("sup2_ps")
        sup2_ok = signal("sup2_ok")
        o25_ps = signal("o25_ps")
        o25_ok = signal("o25_ok", G + 2)
        qk_ps = signal("qk_ps", 2)
        v_ps = signal("v_ps")
        v3_ok = signal("v3_ok")
        part1_ok = signal("part1_ok", 2)
        rest_ok = signal("rest_ok", 2)
        part2_ok = signal("part2_ok", 2)
        part3_ok = signal("part3_ok", 2)
        mxs_ps = signal("mxs_ps", H3 * NT)
        mx_ok = signal("mx_ok", H3 * NT, head=1)
        sh_ok = signal("sh_ok", 2)
        shT_ps = signal("shT_ps")
        shT_ok = signal("shT_ok")
        sc_ps = signal("sc_ps", H3 * NT)
        p3_ok = signal("p3_ok", H3 * NT)
        pv3 = signal("pv3", 2 * NT)
        oT3_ok = signal("oT3_ok", 2)
        o3_ps = signal("o3_ps")
        den3_ok = signal("den3_ok")
        on_ok = signal("on_ok")
        onT_ps = signal("onT_ps")
        onT_ok = signal("onT_ok")
        z_ps = signal("z_ps")

        def at(eng, b, s, k):
            if isinstance(b, int):
                return PER[s] * b + k + HEAD[s]
            value = registers[eng]
            eng.reg_mul(value, b, PER[s])
            eng.reg_add(value, value, k + HEAD[s])
            return value

        adj_d = a["adj"].rearrange("b (t p) j -> b p t j", p=P)
        x_d = a["x"].rearrange("b (t p) d -> b p t d", p=P)
        out_d = a["out"].rearrange("b (t p) d -> b p t d", p=P)
        names = ["L0_gnn_W", "L1_gnn_W", "L3_gnn_W_q", "L3_gnn_W_k", "L3_gnn_W_v", "L3_gnn_W_o"]
        T4 = banks(0, 4).rearrange("p (t n) -> p t n", t=NT)
        O0 = T4.rearrange("p t (h c) -> p t h c", c=C0)
        O3 = T4.rearrange("p t (h c) -> p t h c", c=C3)

        def threes(first):
            for n in range(3):
                yield n, ps[:, first + n, :], 3 * n, min(3, NT - 3 * n)

        registers = {eng: ctx.enter_context(eng.register(f"wait_value_{n}"))
                     for n, eng in enumerate([nc.sync, nc.gpsimd, nc.scalar, nc.vector, nc.tensor])}
        block = ctx.enter_context(nc.Block())

        @block.sync
        def _(sp):
            def load(dst, src, **how):
                sp.dma_start(dst, src, **how).then_inc(weights_in, 16)

            for n, name in enumerate(names):
                load(raw[:, n, :], a[name])
            load(ident[:], a["ident"])
            load(gpair[:], a["gpair"])
            load(grow[:], a["grow"])
            sp.wait_ge(setup_g, 1)
            for h in range(H0):
                for half in range(2):
                    load(ablk[D0 * h:D0 * h + D0, H0 * half + h:H0 * half + h + 1],
                         a["L0_gnn_a"][h, D0 * half:D0 * half + D0].rearrange("(d o) -> d o", o=1))
            for n, name in enumerate(["L1_gnn_a1", "L1_gnn_a2", "L1_gnn_b"]):
                load(acol[:, n:n + 1], a[name].rearrange("(d o) -> d o", o=1))
            load(b1x[:, 0:D], a["L1_gnn_b"].rearrange("(o d) -> o d", o=1))
            load(attb[:], a["L1_gnn_att_b"].rearrange("(o d) -> o d", o=1))
            load(w2a[:].rearrange("p (g e) -> p g e", g=G), a["L2_gnn_W1"].rearrange("g d e -> d g e"))
            load(b2a[:], a["L2_gnn_b1"].rearrange("g (c e) -> e (g c)", e=P), allow_slow_non_contiguous=True)
            load(w2b[:].rearrange("p (g c) d -> p g c d", g=G), a["L2_gnn_W2"].rearrange("g (c e) d -> e g c d", e=P))
            load(b2b[:], a["L2_gnn_b2"].rearrange("(o g) d -> o (g d)", o=1))
            load(fus[:], a["L2_gnn_fusion_w"].rearrange("(o g) -> o g", o=1).broadcast_to([GN, G]))
            load(web[:], a["L3_gnn_W_e"].rearrange("h o -> o h").broadcast_to([P, H3]))
            load(mrow[:], a["nodemask"].rearrange("b (t p) -> (b t) p", p=P))
            sp.dma_start(adj[:], adj_d[0]).then_inc(adj_in, 16)

            def turn(b, last):
                sp.wait_ge(y_ok, at(sp, b, y_ok, 0))
                sp.dma_start(xr[:], x_d[b]).then_inc(x_in, 16)
                if not last:
                    sp.wait_ge(adjT_ps, at(sp, b, adjT_ps, NT))
                    sp.wait_ge(neg_ok, at(sp, b, neg_ok, NT))
                    sp.wait_ge(agr_ok, at(sp, b, agr_ok, 1))
                    sp.dma_start(adj[:], adj_d[b + 1]).then_inc(adj_in, 16)
                for side in range(2):
                    for t, pair in enumerate(TERMS):
                        part = pair[side]
                        if part == 0:
                            sp.wait_ge(part1_ok, at(sp, b, part1_ok, side + 1))
                        elif part == 1:
                            sp.wait_ge(part2_ok, at(sp, b, part2_ok, side + 1))
                        else:
                            sp.wait_ge(part3_ok, at(sp, b, part3_ok, side + 1))
                        for h in range(H3):
                            sp.dma_start(qk[D3 * t:D3 * t + D3, side, h, :],
                                         parts[D3 * h:D3 * h + D3, side, part, :]).then_inc(stack_in, 16)
                sp.wait_ge(shT_ok, at(sp, b, shT_ok, 1))
                sp.dma_start(qs[KQ:KQ + 1].rearrange("o h (t n) -> o (h t) n", n=P), shT[:]).then_inc(shift_in, 16)
                sp.wait_ge(ln_ok, at(sp, b, ln_ok, 4 * NT))
                sp.dma_start(out_d[b], tmp[:]).then_inc(stored, 16)

            with sp.Fori(0, B - 1) as b:
                turn(b, False)
            turn(B - 1, True)
            sp.wait_ge(stored, at(sp, B, stored, 0))

        W_ALL = 16 * (len(names) + 3 + 2 * H0 + 3 + 1 + 1 + 4 + 2 + 1)

        @block.gpsimd
        def _(pool):
            pool.memset(ablk[:], 0.0).then_inc(setup_g, 1)
            pool.memset(ones[:], 1.0).then_inc(setup_g, 1)
            pool.memset(v0[:], 0.0).then_inc(setup_g, 1)
            pool.memset(v3[:], 0.0).then_inc(setup_g, 1)
            pool.memset(epst[:], EPS).then_inc(setup_g, 1)
            pool.memset(hx[:], 1.0).then_inc(setup_g, 1)
            pool.wait_ge(setup_g, 6)
            pool.memset(v3[:, :, :, D3:D3 + 1], 1.0).then_inc(setup_g, 1)
            for s in (y_ok, mx_ok, stored):
                pool.wait_ge(setup_v, SETUP_V).then_inc(s, HEAD[s])
            with pool.Fori(0, B) as b:
                pool.wait_ge(adj_in, at(pool, b, adj_in, 16))
                pool.wait_ge(mx_ok, at(pool, b, mx_ok, 0)).then_inc(waits_alone, 1)
                for t in range(NT):
                    pool.tensor_scalar(neg[:, t], adj[:, t], -1.0, BIG, ALU.add, ALU.mult).then_inc(neg_ok, 1)
                pool.tensor_copy(msk[:], maskall[:, bass.ds(b * NT, NT)]).then_inc(mask_ok, 1)
                pool.tensor_tensor(a25[:], adj[0:GN, 0, 0:GN], ident[0:GN, 0:GN], ALU.add).then_inc(agr_ok, 1)
                pool.wait_ge(agr_ok, at(pool, b, agr_ok, 1))
                pool.tensor_tensor(agr[:], a25[:].unsqueeze(1).broadcast_to([GN, G, GN]), gpair[:], ALU.mult)\
                    .then_inc(agr_ok, 1)
                pool.wait_ge(tmax_ok, at(pool, b, tmax_ok, 1)).then_inc(waits_alone, 1)
                pool.partition_all_reduce(tall[:], tmx[:], P, RMAX).then_inc(tall_ok, 1)
                pool.wait_ge(tBE_ok, at(pool, b, tBE_ok, 2))
                pool.wait_ge(h0_ok, at(pool, b, h0_ok, 3))
                pool.tensor_tensor(v0[:, :, :, 0:D0], hx[:, :, 0:D].rearrange("p t (h d) -> p t h d", h=H0),
                                   tB[:].unsqueeze(3).broadcast_to([P, NT, H0, D0]), ALU.mult).then_inc(v0_ok, 1)
                pool.tensor_copy(v0[:, :, :, D0:D0 + 1], tB[:].unsqueeze(3)).then_inc(v0_ok, 1)
                pool.wait_ge(emp_ok, at(pool, b, emp_ok, 1))
                pool.wait_ge(hsum_ok, at(pool, b, hsum_ok, 1))
                pool.wait_ge(stored, at(pool, b, stored, 0))
                pool.tensor_tensor(tmp[:].rearrange("p t (h d) -> p t h d", h=H0),
                                   emp[:].unsqueeze(3).broadcast_to([P, NT, H0, D0]),
                                   hsum[:].rearrange("p (h d) -> p h d", h=H0).unsqueeze(1).broadcast_to([P, NT, H0, D0]),
                                   ALU.mult).then_inc(eh_ok, 1)
                for side in range(2):
                    pool.wait_ge(part2_ok, at(pool, b, part2_ok, side + 1))
                    pool.tensor_tensor(parts[:, side, 2], rest[:, side], parts[:, side, 1], ALU.subtract)\
                        .then_inc(part3_ok, 1)

        @block.scalar
        def _(act):
            act.wait_ge(setup_v, 5)
            nc.scalar.activation(gw[:], gw[:], ACT.Exp).then_inc(setup_a, 1)
            act.wait_ge(setup_v, SETUP_V)
            with act.Fori(0, B) as b:
                def copy(out, in_, s, scale=1.0):
                    nc.scalar.activation(out, in_, ACT.Copy, scale=scale).then_inc(s, 1)

                def root(layer):
                    act.wait_ge(ln_aggr, at(act, b, ln_aggr, NT * (layer + 1)))
                    nc.scalar.activation(sd[:], mv[:, :, 1], ACT.Sqrt, bias=epst[:, 0:1]).then_inc(ln_root, 1)

                for t in range(NT):
                    act.wait_ge(adjT_ps, at(act, b, adjT_ps, t + 1))
                    copy(adjT[:, t], banks(2 * (t % 2), 2), adjT_ok)
                act.wait_ge(xT_ps, at(act, b, xT_ps, 1))
                copy(xT[:], banks(4, 2), xT_ok)
                act.wait_ge(t_ok, at(act, b, t_ok, 3))
                for _, bank, t, k in threes(4):
                    copy(hx[:, t:t + k, 0:D], bank[:, 0:k * (D + H0)].rearrange("p (t n) -> p t n", t=k)[:, :, 0:D], h0_ok)
                act.wait_ge(deg_ok, at(act, b, deg_ok, 3))
                nc.scalar.activation(deg[:, 3], deg[:, 2], ACT.Sqrt).then_inc(degroot_ok, 1)
                act.wait_ge(hsum_ps, at(act, b, hsum_ps, 1))
                copy(hsum[:], banks(7, 1)[:, 0:D], hsum_ok)
                act.wait_ge(td_ok, at(act, b, td_ok, 1))
                nc.scalar.activation(tB[:], tt[:], ACT.Exp, scale=0.2).then_inc(tBE_ok, 1)
                nc.scalar.activation(tE[:], tt[:], ACT.Exp, scale=0.8).then_inc(tBE_ok, 1)
                for h in range(H0):
                    act.wait_ge(c_relu, at(act, b, c_relu, h + 1))
                    nc.scalar.activation(cs[:, h], cs[:, h], ACT.Exp, scale=-0.8).then_inc(c_ok, 1)
                for g in range(2):
                    act.wait_ge(pv0, at(act, b, pv0, NT * (g + 1)))
                    copy(oT[:, g], banks(4 + 2 * g, 2), oT0_ok)
                root(0)
                act.wait_ge(xT_ps, at(act, b, xT_ps, 2))
                copy(xT[:], banks(4, 2), xT_ok)
                act.wait_ge(s2_ok, at(act, b, s2_ok, 3))
                for _, bank, t, k in threes(0):
                    copy(hx[:, t:t + k, 0:D], bank[:, 0:k * (D + 1)].rearrange("p (t n) -> p t n", t=k)[:, :, 0:D], h1_ok)
                act.wait_ge(s1_ps, at(act, b, s1_ps, 1))
                for t in range(NT):
                    if t >= 2:
                        act.wait_ge(p1_ok, at(act, b, p1_ok, t - 1))
                    nc.scalar.activation(oT[:, t % 2], banks(6, 2), ACT.Sigmoid, bias=s2[:, t:t + 1])\
                        .then_inc(sig_ok, 1)
                root(1)
                act.wait_ge(x25_ps, at(act, b, x25_ps, 1))
                copy(x25T[:], banks(5, 1)[:, 0:GN], x25_ok)
                act.wait_ge(sup1_ps, at(act, b, sup1_ps, 1))
                copy(sup1, banks(0, 3)[0:GN, 0:G * DH], sup1_ok)
                act.wait_ge(sup2_ps, at(act, b, sup2_ps, 1))
                copy(sup2, banks(6, 2)[0:GN, 0:G * D], sup2_ok)
                root(2)
                act.wait_ge(xT_ps, at(act, b, xT_ps, 3))
                copy(xT[:], banks(4, 2), xT_ok)
                for side, scale in enumerate([0.25, 1.0]):
                    act.wait_ge(qk_ps, at(act, b, qk_ps, side + 1))
                    copy(parts[:, side, 0], banks(2 * side, 2), part1_ok, scale)
                act.wait_ge(v_ps, at(act, b, v_ps, 1))
                copy(v3[:, :, :, 0:D3], banks(6, 2).rearrange("p (t h d) -> p t h d", t=NT, h=H3), v3_ok)
                for side in range(2):
                    act.wait_ge(rest_ok, at(act, b, rest_ok, side + 1))
                    copy(parts[:, side, 1], rest[:, side], part2_ok)
                act.wait_ge(shT_ps, at(act, b, shT_ps, 1))
                copy(shT[:], banks(6, 1)[0:H3 * NT, 0:P], shT_ok)
                for n in range(H3 * NT):
                    act.wait_ge(sc_ps, at(act, b, sc_ps, n + 1))
                    if n >= 8:
                        act.wait_ge(pv3, at(act, b, pv3, n // 4 - 1))
                    nc.scalar.activation(ring[:, n % 8], banks(2 * (n % 2), 2), ACT.Exp).then_inc(p3_ok, 1)
                    if n == H3 * NT // 2 + 3:
                        act.wait_ge(pv3, at(act, b, pv3, NT))
                        copy(oT[:, 0], banks(4, 2), oT3_ok)
                act.wait_ge(pv3, at(act, b, pv3, 2 * NT))
                copy(oT[:, 1], banks(6, 2), oT3_ok)
                act.wait_ge(onT_ps, at(act, b, onT_ps, 1))
                copy(xT[:], banks(4, 2), onT_ok)
                root(3)

        @block.vector
        def _(dve):
            steps = [0]

            def step(ins):
                ins.then_inc(setup_v, 1)
                steps[0] += 1
                dve.wait_ge(setup_v, steps[0])

            dve.wait_ge(weights_in, W_ALL)
            step(nc.vector.tensor_copy(identb[:], ident[:]))
            step(nc.vector.tensor_copy(w0x[:, 0:D], raw[:, 0]))
            step(nc.vector.tensor_copy(gw[:], fus[:]))
            step(nc.vector.reduce_max(small[0:GN, 0:1], gw[:], AX_X))
            step(nc.vector.tensor_scalar(gw[:], gw[:], small[0:GN, 0:1], None, ALU.subtract))
            dve.wait_ge(setup_t, 1)
            step(nc.vector.tensor_copy(w0t[:], banks(0, 1)[:, 0:P]))
            step(nc.vector.tensor_copy(w1x[:, 0:D], banks(0, 1)[:, P:2 * P]))
            step(nc.vector.tensor_copy(wT[:], banks(0, 2)[:, 2 * P:6 * P].rearrange("p (w n) -> p w n", w=4)))
            step(nc.vector.tensor_copy(maskall[:], banks(2, 1)[:, 0:B * NT]))
            dve.wait_ge(setup_t, 2)
            step(nc.vector.tensor_copy(w0x[:, D:D + H0], banks(3, 1)[:, H0:2 * H0]))
            step(nc.vector.tensor_copy(small[:, 0:H0], banks(3, 1)[:, 0:H0]))
            step(nc.vector.tensor_copy(small[:, H0:H0 + 2], banks(3, 1)[:, 16:18]))
            dve.wait_ge(setup_g, 7)
            for h in range(H0):
                step(nc.vector.tensor_scalar(w0s[:, h], ones[:], small[:, h:h + 1], None, ALU.mult))
            step(nc.vector.tensor_scalar(w1s[:], ones[:], small[:, H0:H0 + 1], None, ALU.mult))
            step(nc.vector.tensor_copy(w1x[:, D:D + 1], small[:, H0 + 1:H0 + 2]))
            step(nc.vector.reduce_sum(b1x[:, D:D + 1], banks(3, 1)[0:1, 32:34], AX_X))
            step(nc.vector.tensor_tensor(b1x[:, D:D + 1], b1x[:, D:D + 1], attb[:], ALU.add))
            dve.wait_ge(setup_a, 1)
            step(nc.vector.reduce_sum(small[0:GN, 6:7], gw[:], AX_X))
            step(nc.vector.reciprocal(small[0:GN, 7:8], small[0:GN, 6:7]))
            step(nc.vector.scalar_tensor_tensor(out=gw[:], in0=gw[:], scalar=small[0:GN, 7:8], in1=grow[:],
                                                op0=ALU.mult, op1=ALU.mult))
            step(nc.vector.memset(qk[KQ:KQ + 1, :], 1.0))
            assert steps[0] == SETUP_V
            with dve.Fori(0, B) as b:
                def norm(layer, src, out):
                    for t in range(NT):
                        nc.vector.bn_stats(stats[:, t], src[:, t]).then_inc(ln_stats, 1)
                    dve.wait_ge(ln_stats, at(dve, b, ln_stats, NT * (layer + 1))).then_inc(waits_alone, 1)
                    for t in range(NT):
                        nc.vector.bn_aggr(mv[:, t], stats[:, t]).then_inc(ln_aggr, 1)
                    dve.wait_ge(ln_root, at(dve, b, ln_root, layer + 1))
                    nc.vector.reciprocal(sd[:], sd[:]).then_inc(ln_rec, 1)
                    dve.wait_ge(ln_rec, at(dve, b, ln_rec, layer + 1))
                    for t in range(NT):
                        nc.vector.tensor_scalar(out[:, t], src[:, t], mv[:, t, 0:1], sd[:, t:t + 1],
                                                ALU.subtract, ALU.mult).then_inc(ln_ok, 1)

                dve.wait_ge(agr_ok, at(dve, b, agr_ok, 2))
                nc.vector.reduce_sum(deg[:, 0], agr[:], AX_X).then_inc(deg_ok, 1)
                dve.wait_ge(deg_ok, at(dve, b, deg_ok, 1))
                nc.vector.tensor_scalar(deg[:, 1], deg[:, 0], 0.0, None, ALU.is_equal).then_inc(deg_ok, 1)
                dve.wait_ge(deg_ok, at(dve, b, deg_ok, 2))
                nc.vector.tensor_tensor(deg[:, 2], deg[:, 0], deg[:, 1], ALU.add).then_inc(deg_ok, 1)
                dve.wait_ge(h0_ps, at(dve, b, h0_ps, 1))
                for _, bank, t, k in threes(4):
                    nc.vector.tensor_copy(tt[:, t:t + k], bank[:, 0:k * (D + H0)].rearrange(
                        "p (t n) -> p t n", t=k)[:, :, D:D + H0]).then_inc(t_ok, 1)
                dve.wait_ge(t_ok, at(dve, b, t_ok, 3))
                nc.vector.reduce_max(tmx[:], tt[:].rearrange("p t h -> p h t"), AX_X).then_inc(tmax_ok, 1)
                dve.wait_ge(tall_ok, at(dve, b, tall_ok, 1))
                nc.vector.tensor_tensor(tt[:], tt[:], tall[:].unsqueeze(1).broadcast_to([P, NT, H0]), ALU.subtract)\
                    .then_inc(td_ok, 1)
                for h in range(H0):
                    dve.wait_ge(s0_ps, at(dve, b, s0_ps, h + 1))
                    nc.vector.tensor_scalar(cs[:, h], banks(2 * (h % 2), 2), tall[:, h:h + 1], 0.0, ALU.add, ALU.max)\
                        .then_inc(c_relu, 1)
                dve.wait_ge(degroot_ok, at(dve, b, degroot_ok, 1))
                nc.vector.reciprocal(deg[:, 2], deg[:, 3]).then_inc(dinv_ok, 1)
                nc.vector.tensor_scalar(deg[:, 0], deg[:, 1], -1.0, 1.0, ALU.mult, ALU.add).then_inc(dinv_ok, 1)
                dve.wait_ge(dinv_ok, at(dve, b, dinv_ok, 2))
                nc.vector.tensor_tensor(deg[:, 3], deg[:, 2], deg[:, 0], ALU.mult).then_inc(dinv_ok, 1)
                dve.wait_ge(dinv_ok, at(dve, b, dinv_ok, 3))
                dinv = deg[:, 3].unsqueeze(2).broadcast_to([GN, G, GN])
                nc.vector.tensor_tensor(nadj[:], agr[:], dinv, ALU.mult).then_inc(nadj_ok, 1)
                dve.wait_ge(tBE_ok, at(dve, b, tBE_ok, 2))
                for n in range(H0 * NT):
                    g, t, q = n // (2 * NT), n // 2 % NT, n % 2
                    h = 2 * g + q
                    dve.wait_ge(c_ok, at(dve, b, c_ok, h + 1))
                    if n >= 8:
                        dve.wait_ge(pv0, at(dve, b, pv0, n // 2 - 3))
                    nc.vector.scalar_tensor_tensor(out=ring[:, n % 8], in0=cs[:, h], scalar=tE[:, t, h:h + 1],
                                                   in1=adjT[:, t], op0=ALU.max, op1=ALU.mult).then_inc(p0_ok, 1)
                dve.wait_ge(o0_ps, at(dve, b, o0_ps, 1))
                nc.vector.tensor_scalar(emp[:], O0[:, :, :, D0], 0.0, None, ALU.is_equal).then_inc(emp_ok, 1)
                dve.wait_ge(emp_ok, at(dve, b, emp_ok, 1))
                nc.vector.scalar_tensor_tensor(out=den[:, :, 0:H0], in0=emp[:], scalar=float(N), in1=O0[:, :, :, D0],
                                               op0=ALU.mult, op1=ALU.add).then_inc(den0_ok, 1)
                dve.wait_ge(den0_ok, at(dve, b, den0_ok, 1))
                nc.vector.reciprocal(den[:, :, 0:H0], den[:, :, 0:H0]).then_inc(den0_ok, 1)
                y4 = yr[:].rearrange("p t (h d) -> p t h d", h=H0)
                dve.wait_ge(eh_ok, at(dve, b, eh_ok, 1))
                nc.vector.tensor_tensor(y4, O0[:, :, :, 0:D0], tmp[:].rearrange("p t (h d) -> p t h d", h=H0), ALU.add)\
                    .then_inc(y_ok, 1)
                dve.wait_ge(den0_ok, at(dve, b, den0_ok, 2))
                dve.wait_ge(y_ok, at(dve, b, y_ok, 1))
                nc.vector.tensor_tensor(y4, y4, den[:, :, 0:H0].unsqueeze(3).broadcast_to([P, NT, H0, D0]), ALU.mult)\
                    .then_inc(y_ok, 1)
                dve.wait_ge(y_ok, at(dve, b, y_ok, 2))
                nc.vector.tensor_tensor(yr[:], yr[:], xr[:], ALU.add).then_inc(y_ok, 1)
                dve.wait_ge(y_ok, at(dve, b, y_ok, 3))
                norm(0, yr, xr)
                dve.wait_ge(h1_ps, at(dve, b, h1_ps, 1))
                for _, bank, t, k in threes(0):
                    nc.vector.tensor_copy(s2[:, t:t + k], bank[:, 0:k * (D + 1)].rearrange(
                        "p (t n) -> p t n", t=k)[:, :, D]).then_inc(s2_ok, 1)
                dve.wait_ge(mask_ok, at(dve, b, mask_ok, 1))
                for t in range(NT):
                    dve.wait_ge(sig_ok, at(dve, b, sig_ok, t + 1))
                    nc.vector.scalar_tensor_tensor(out=ring[:, t], in0=oT[:, t % 2], scalar=msk[:, t:t + 1],
                                                   in1=adjT[:, t], op0=ALU.mult, op1=ALU.mult).then_inc(p1_ok, 1)
                dve.wait_ge(p1_ok, at(dve, b, p1_ok, NT))
                nc.vector.tensor_scalar(negT[:], adjT[:], -1.0, BIG, ALU.add, ALU.mult).then_inc(negT_ok, 1)
                dve.wait_ge(pv1, at(dve, b, pv1, 1))
                nc.vector.tensor_tensor(fac[:], T4[:, :, D], msk[:], ALU.mult).then_inc(fac_ok, 1)
                dve.wait_ge(fac_ok, at(dve, b, fac_ok, 1))
                nc.vector.tensor_scalar(fac[:], fac[:], 1e-8, None, ALU.add).then_inc(fac_ok, 1)
                dve.wait_ge(fac_ok, at(dve, b, fac_ok, 2))
                nc.vector.reciprocal(fac[:], fac[:]).then_inc(fac_ok, 1)
                dve.wait_ge(fac_ok, at(dve, b, fac_ok, 3))
                nc.vector.tensor_tensor(fac[:], fac[:], msk[:], ALU.mult).then_inc(fac_ok, 1)
                dve.wait_ge(fac_ok, at(dve, b, fac_ok, 4))
                nc.vector.tensor_tensor(fac[:], fac[:], msk[:], ALU.mult).then_inc(fac_ok, 1)
                dve.wait_ge(fac_ok, at(dve, b, fac_ok, 5))
                nc.vector.tensor_tensor(yr[:], T4[:, :, 0:D], fac[:].unsqueeze(2).broadcast_to([P, NT, D]), ALU.mult)\
                    .then_inc(y_ok, 1)
                dve.wait_ge(y_ok, at(dve, b, y_ok, 4))
                nc.vector.tensor_tensor(yr[:], yr[:], xr[:], ALU.add).then_inc(y_ok, 1)
                dve.wait_ge(y_ok, at(dve, b, y_ok, 5))
                norm(1, yr, xr)
                dve.wait_ge(nadjT_ps, at(dve, b, nadjT_ps, 1))
                nc.vector.tensor_tensor(nT[:], banks(4, 1)[0:GN, 0:G * GN].rearrange("p (g n) -> p g n", g=G), dinv,
                                        ALU.mult).then_inc(nadjT_ok, 1)
                dve.wait_ge(h25_ps, at(dve, b, h25_ps, 1))
                nc.vector.tensor_tensor(h25[:], banks(3, 1)[:, 0:2 * G * GN].rearrange("p (g n) -> p g n", n=GN),
                                        b2a[:].unsqueeze(2).broadcast_to([P, 2 * G, GN]), ALU.add).then_inc(h25_ok, 1)
                dve.wait_ge(h25_ok, at(dve, b, h25_ok, 1))
                nc.vector.tensor_scalar(h25[:], h25[:], 0.0, None, ALU.max).then_inc(h25_ok, 1)
                dve.wait_ge(o25_ps, at(dve, b, o25_ps, 1))
                for g in range(G):
                    nc.vector.tensor_scalar(o25[:, g], banks(0, 2)[0:GN, g * D:(g + 1) * D], 0.0, gw[:, g:g + 1],
                                            ALU.max, ALU.mult).then_inc(o25_ok, 1)
                dve.wait_ge(o25_ok, at(dve, b, o25_ok, G))
                nc.vector.tensor_reduce(f25[:], o25[:].rearrange("p g d -> p d g"), AX_X, ALU.add).then_inc(o25_ok, 1)
                dve.wait_ge(o25_ok, at(dve, b, o25_ok, G + 1))
                nc.vector.tensor_tensor(xr[0:GN, 0], xr[0:GN, 0], f25[:], ALU.add).then_inc(o25_ok, 1)
                dve.wait_ge(o25_ok, at(dve, b, o25_ok, G + 2))
                norm(2, xr, xr)
                for side, scale in enumerate([0.25, 1.0]):
                    dve.wait_ge(part1_ok, at(dve, b, part1_ok, side + 1))
                    nc.vector.scalar_tensor_tensor(out=rest[:, side], in0=banks(2 * side, 2), scalar=scale,
                                                   in1=parts[:, side, 0], op0=ALU.mult, op1=ALU.subtract)\
                        .then_inc(rest_ok, 1)
                dve.wait_ge(neg_ok, at(dve, b, neg_ok, NT))
                for n in range(H3 * NT):
                    h, t = n // NT, n % NT
                    if n >= 2:
                        dve.wait_ge(mx_ok, at(dve, b, mx_ok, n - 1))
                    dve.wait_ge(mxs_ps, at(dve, b, mxs_ps, n + 1)).then_inc(waits_alone, 1)
                    nc.vector.tensor_tensor_reduce(out=junk[:, n % 2], in0=banks(2 * (n % 3), 2), in1=neg[:, t],
                                                   scale=1.0, scalar=-3e38, op0=ALU.add, op1=ALU.max,
                                                   accum_out=mx[:, h, t:t + 1]).then_inc(mx_ok, 1)
                dve.wait_ge(mx_ok, at(dve, b, mx_ok, H3 * NT))
                wb = web[:].unsqueeze(2).broadcast_to([P, H3, NT])
                nc.vector.tensor_tensor(sh[:], mx[:], wb, ALU.add).then_inc(sh_ok, 1)
                dve.wait_ge(sh_ok, at(dve, b, sh_ok, 1))
                nc.vector.tensor_tensor(sh[:], wb, sh[:], ALU.subtract).then_inc(sh_ok, 1)
                dve.wait_ge(o3_ps, at(dve, b, o3_ps, 1))
                nc.vector.reciprocal(den[:], O3[:, :, :, D3]).then_inc(den3_ok, 1)
                dve.wait_ge(den3_ok, at(dve, b, den3_ok, 1))
                nc.vector.tensor_tensor(yr[:].rearrange("p t (h d) -> p t h d", h=H3), O3[:, :, :, 0:D3],
                                        den[:].unsqueeze(3).broadcast_to([P, NT, H3, D3]), ALU.mult)\
                    .then_inc(on_ok, 1)
                dve.wait_ge(z_ps, at(dve, b, z_ps, 1))
                nc.vector.tensor_tensor(yr[:], banks(6, 2).rearrange("p (t d) -> p t d", t=NT), xr[:], ALU.add)\
                    .then_inc(y_ok, 1)
                dve.wait_ge(y_ok, at(dve, b, y_ok, 6))
                norm(3, yr, tmp)

        @block.tensor
        def _(pe):
            mm, tr = nc.tensor.matmul, nc.tensor.transpose
            pe.wait_ge(weights_in, W_ALL)
            for n in range(len(names)):
                tr(banks(0, 2)[:, n * P:(n + 1) * P], raw[:, n], ident[:])
            tr(banks(2, 1)[:, 0:B * NT], mrow[:], ident[0:B * NT, 0:B * NT]).then_inc(setup_t, 1)
            pe.wait_ge(setup_v, 6)
            mm(banks(3, 1)[:, 0:2 * H0], w0t[:], ablk[:], start=True, stop=True)
            mm(banks(3, 1)[:, 16:18], raw[:, 1], acol[:, 0:2], start=True, stop=True)
            mm(banks(3, 1)[0:1, 32:34], acol[:, 2:3], acol[:, 0:2], start=True, stop=True).then_inc(setup_t, 1)
            pe.wait_ge(setup_v, SETUP_V)
            pe.wait_ge(setup_g, 7)
            with pe.Fori(0, B) as b:
                def turn_x(s):
                    for t in range(NT):
                        last = tr(banks(4, 2)[:, t * P:(t + 1) * P], xr[:, t], ident[:])
                    last.then_inc(s, 1)

                pe.wait_ge(adj_in, at(pe, b, adj_in, 16))
                for j in range(NT):
                    if j >= 2:
                        pe.wait_ge(adjT_ok, at(pe, b, adjT_ok, j - 1))
                    for i in range(NT):
                        last = tr(banks(2 * (j % 2), 2)[:, i * P:(i + 1) * P], adj[:, i, j * P:(j + 1) * P], ident[:])
                    last.then_inc(adjT_ps, 1)
                pe.wait_ge(x_in, at(pe, b, x_in, 16))
                turn_x(xT_ps)
                pe.wait_ge(xT_ok, at(pe, b, xT_ok, 1))
                pe.wait_ge(y_ok, at(pe, b, y_ok, 0))
                for n, bank, t, k in threes(4):
                    for i in range(k):
                        last = mm(bank[:, i * (D + H0):(i + 1) * (D + H0)], xT[:, (t + i) * P:(t + i + 1) * P], w0x[:],
                                  start=True, stop=True)
                last.then_inc(h0_ps, 1)
                pe.wait_ge(adjT_ok, at(pe, b, adjT_ok, NT))
                for h in range(H0):
                    if h >= 2:
                        pe.wait_ge(c_relu, at(pe, b, c_relu, h - 1))
                    for half in range(2):
                        last = mm(banks(2 * (h % 2) + half, 1), w0s[:, h], xT[:, half * HALF:(half + 1) * HALF],
                                  start=True, stop=True)
                    last.then_inc(s0_ps, 1)
                pe.wait_ge(h0_ok, at(pe, b, h0_ok, 3))
                for t in range(NT):
                    last = mm(banks(7, 1)[:, 0:D], ones[:], hx[:, t, 0:D], start=(t == 0), stop=(t == NT - 1))
                last.then_inc(hsum_ps, 1)
                pe.wait_ge(t_ok, at(pe, b, t_ok, 3))
                pe.wait_ge(v0_ok, at(pe, b, v0_ok, 2))
                for g in range(2):
                    if g == 1:
                        pe.wait_ge(hsum_ok, at(pe, b, hsum_ok, 1))
                    for t in range(NT):
                        pe.wait_ge(p0_ok, at(pe, b, p0_ok, 2 * (NT * g + t + 1)))
                        for half in range(2):
                            for q in range(2):
                                last = mm(banks(4 + 2 * g + half, 1)[C0 * q:C0 * (q + 1)], v0[:, t, 2 * g + q],
                                          ring[:, (2 * (NT * g + t) + q) % 8, half * HALF:(half + 1) * HALF],
                                          start=(t == 0), stop=(t == NT - 1))
                        last.then_inc(pv0, 1)
                pe.wait_ge(oT0_ok, at(pe, b, oT0_ok, 2)).then_inc(waits_alone, 1)
                pe.wait_ge(c_relu, at(pe, b, c_relu, H0)).then_inc(waits_alone, 1)
                for t in range(NT):
                    for g in range(2):
                        last = tr(T4[:, t, g * P:(g + 1) * P], oT[:, g, t * P:(t + 1) * P], ident[:])
                last.then_inc(o0_ps, 1)
                pe.wait_ge(ln_ok, at(pe, b, ln_ok, NT))
                turn_x(xT_ps)
                pe.wait_ge(xT_ok, at(pe, b, xT_ok, 2))
                for n, bank, t, k in threes(0):
                    for i in range(k):
                        out = bank[:, i * (D + 1):(i + 1) * (D + 1)]
                        mm(out, ones[0:1, :], b1x[:], start=True, stop=False)
                        last = mm(out, xT[:, (t + i) * P:(t + i + 1) * P], w1x[:], start=False, stop=True)
                last.then_inc(h1_ps, 1)
                for half in range(2):
                    last = mm(banks(6 + half, 1), w1s[:], xT[:, half * HALF:(half + 1) * HALF], start=True, stop=True)
                last.then_inc(s1_ps, 1)
                pe.wait_ge(nadj_ok, at(pe, b, nadj_ok, 1)).then_inc(waits_alone, 1)
                for g in range(G):
                    last = tr(banks(4, 1)[0:GN, g * GN:(g + 1) * GN], nadj[:, g], ident[0:GN, 0:GN])
                last.then_inc(nadjT_ps, 1)
                pe.wait_ge(h1_ok, at(pe, b, h1_ok, 3))
                pe.wait_ge(s2_ok, at(pe, b, s2_ok, 3))
                pe.wait_ge(p1_ok, at(pe, b, p1_ok, NT))
                for i in range(NT):
                    for j in range(NT):
                        last = mm(T4[:, i, 0:D + 1], ring[:, j, i * P:(i + 1) * P], hx[:, j],
                                  start=(j == 0), stop=(j == NT - 1))
                last.then_inc(pv1, 1)
                pe.wait_ge(ln_ok, at(pe, b, ln_ok, 2 * NT)).then_inc(waits_alone, 1)
                tr(banks(5, 1)[:, 0:GN], xr[0:GN, 0], ident[0:GN, 0:GN]).then_inc(x25_ps, 1)
                pe.wait_ge(x25_ok, at(pe, b, x25_ok, 1))
                for c in range(0, G * DH, HALF):
                    w = min(HALF, G * DH - c)
                    last = mm(banks(0, 3)[0:GN, c:c + w], x25T[:], w2a[:, c:c + w], start=True, stop=True)
                last.then_inc(sup1_ps, 1)
                pe.wait_ge(sup1_ok, at(pe, b, sup1_ok, 1))
                pe.wait_ge(nadjT_ok, at(pe, b, nadjT_ok, 1)).then_inc(waits_alone, 1)
                for n in range(2 * G):
                    last = mm(banks(3, 1)[:, n * GN:(n + 1) * GN], sup1[:, n * P:(n + 1) * P], nT[:, n // 2],
                              start=True, stop=True)
                last.then_inc(h25_ps, 1)
                pe.wait_ge(h25_ok, at(pe, b, h25_ok, 2))
                for n in range(2 * G):
                    last = mm(banks(6, 2)[0:GN, n // 2 * D:(n // 2 + 1) * D], h25[:, n], w2b[:, n],
                              start=(n % 2 == 0), stop=(n % 2 == 1))
                last.then_inc(sup2_ps, 1)
                pe.wait_ge(sup2_ok, at(pe, b, sup2_ok, 1)).then_inc(waits_alone, 1)
                for g in range(G):
                    out = banks(0, 2)[0:GN, g * D:(g + 1) * D]
                    mm(out, ones[0:1, 0:GN], b2b[:, g * D:(g + 1) * D], start=True, stop=False)
                    last = mm(out, nT[:, g], sup2[:, g * D:(g + 1) * D], start=False, stop=True)
                last.then_inc(o25_ps, 1)
                pe.wait_ge(ln_ok, at(pe, b, ln_ok, 3 * NT))
                turn_x(xT_ps)
                pe.wait_ge(xT_ok, at(pe, b, xT_ok, 3))
                for side in range(2):
                    for half in range(2):
                        last = mm(banks(2 * side + half, 1), wT[:, side], xT[:, half * HALF:(half + 1) * HALF],
                                  start=True, stop=True)
                    last.then_inc(qk_ps, 1)
                for t in range(NT):
                    last = mm(banks(6, 2)[:, t * P:(t + 1) * P], xT[:, t * P:(t + 1) * P], wT[:, 2], start=True, stop=True)
                last.then_inc(v_ps, 1)
                pe.wait_ge(rest_ok, at(pe, b, rest_ok, 2))
                pe.wait_ge(stack_in, at(pe, b, stack_in, PER[stack_in]))
                for n in range(H3 * NT):
                    h, t = n // NT, n % NT
                    if n >= 3:
                        pe.wait_ge(mx_ok, at(pe, b, mx_ok, n - 2))
                    for half in range(2):
                        last = mm(banks(2 * (n % 3) + half, 1), qs[0:KQ, h, t * P:(t + 1) * P],
                                  ks[0:KQ, h, half * HALF:(half + 1) * HALF], start=True, stop=True)
                    last.then_inc(mxs_ps, 1)
                pe.wait_ge(sh_ok, at(pe, b, sh_ok, 2))
                pe.wait_ge(v3_ok, at(pe, b, v3_ok, 1)).then_inc(waits_alone, 1)
                tr(banks(6, 1)[0:H3 * NT, 0:P], sh[:].rearrange("p h t -> p (h t)"), ident[:]).then_inc(shT_ps, 1)
                pe.wait_ge(shift_in, at(pe, b, shift_in, 16))
                pe.wait_ge(negT_ok, at(pe, b, negT_ok, 1))

                def scores(n):
                    g, t, q = n // (4 * NT), n // 4 % NT, n % 4
                    if n >= 2:
                        pe.wait_ge(p3_ok, at(pe, b, p3_ok, n - 1))
                    for half in range(2):
                        out, cols = banks(2 * (n % 2) + half, 1), slice(half * HALF, (half + 1) * HALF)
                        mm(out, identb[:], negT[:, t, cols], start=True, stop=False)
                        last = mm(out, ks[:, 4 * g + q, t * P:(t + 1) * P], qs[:, 4 * g + q, cols], start=False, stop=True)
                    last.then_inc(sc_ps, 1)

                def values(m):
                    g, t = m // NT, m % NT
                    pe.wait_ge(p3_ok, at(pe, b, p3_ok, 4 * (m + 1)))
                    for half in range(2):
                        for q in range(4):
                            last = mm(banks(4 + 2 * g + half, 1)[C3 * q:C3 * (q + 1)], v3[:, t, 4 * g + q],
                                      ring[:, (4 * m + q) % 8, half * HALF:(half + 1) * HALF],
                                      start=(t == 0), stop=(t == NT - 1))
                    last.then_inc(pv3, 1)

                for m in range(2 * NT):
                    for q in range(4):
                        scores(4 * m + q)
                    if m >= 1:
                        values(m - 1)
                values(2 * NT - 1)
                pe.wait_ge(oT3_ok, at(pe, b, oT3_ok, 2))
                for t in range(NT):
                    for g in range(2):
                        last = tr(T4[:, t, g * P:(g + 1) * P], oT[:, g, t * P:(t + 1) * P], ident[:])
                last.then_inc(o3_ps, 1)
                pe.wait_ge(on_ok, at(pe, b, on_ok, 1))
                for t in range(NT):
                    last = tr(banks(4, 2)[:, t * P:(t + 1) * P], yr[:, t], ident[:])
                last.then_inc(onT_ps, 1)
                pe.wait_ge(onT_ok, at(pe, b, onT_ok, 1))
                for t in range(NT):
                    last = mm(banks(6, 2)[:, t * P:(t + 1) * P], xT[:, t * P:(t + 1) * P], wT[:, 3], start=True, stop=True)
                last.then_inc(z_ps, 1)


_INS = ['x', 'adj', 'nodemask', 'L0_gnn_W', 'L0_gnn_a', 'L1_gnn_W', 'L1_gnn_b', 'L1_gnn_a1', 'L1_gnn_a2',
        'L1_gnn_att_b', 'L2_gnn_W1', 'L2_gnn_b1', 'L2_gnn_W2', 'L2_gnn_b2', 'L2_gnn_fusion_w', 'L3_gnn_W_q',
        'L3_gnn_W_k', 'L3_gnn_W_v', 'L3_gnn_W_e', 'L3_gnn_W_o']


def shape_constants():
    pair = np.zeros((GN, G, GN), np.float32)
    row = np.zeros((GN, G), np.float32)
    for g, nodes in enumerate(GROUPS):
        row[nodes, g] = 1.0
        pair[np.ix_(nodes, [g], nodes)] = 1.0
    return {"ident": np.eye(P, dtype=np.float32), "gpair": pair, "grow": row}


def kernel(**inputs):
    import concourse.bacc as _bacc
    from concourse.bass_utils import run_bass_kernel_spmd as _run

    nc = _bacc.Bacc("TRN2", target_bir_lowering=False, num_devices=1)
    arrays, aps = {}, {}
    for name in _INS:
        v = np.ascontiguousarray(inputs[name])
        arrays[name] = v.reshape(1) if v.ndim == 0 else v
    arrays.update(shape_constants())
    arrays = {f"in_{name}": v for name, v in arrays.items()}
    for name, v in arrays.items():
        aps[name[3:]] = nc.dram_tensor(name, v.shape, mybir.dt.from_np(v.dtype), kind="ExternalInput").ap()
    aps["out"] = nc.dram_tensor("out_nodes", (B, N, D), F32, kind="ExternalOutput").ap()
    build(nc, aps)
    return _run(nc, [arrays], core_ids=[0]).results[0]["out_nodes"]
```

```python
from contextlib import ExitStack

import concourse.bass as bass
import numpy as np
from concourse import mybir

ALU = mybir.AluOpType
ACT = mybir.ActivationFunctionType
F32 = mybir.dt.float32
BF16 = mybir.dt.bfloat16
AX_X = mybir.AxisListType.X
RMAX = bass.bass_isa.ReduceOp.max

P = 128
B, N, D = 8, 1024, 128
NT = N // P
HALF = 512
H0, D0 = 4, 32
C0 = 64
H3, D3 = 8, 16
C3 = 32
G, GN, DH = 5, 25, 256
GROUPS = [list(range(25)), [0, 1, 2, 3, 4, 5, 6, 7, 8], [0, 9, 10, 11, 12, 13, 14],
          [6, 7, 8, 12, 13, 14], [3, 4, 5, 9, 10, 11]]
SETUP_V = 24
BIG = float(2.0 ** 100)
EPS = 1e-5
TERMS = [(0, 0), (0, 1), (1, 0), (1, 1), (0, 2), (2, 0)]
KQ = D3 * len(TERMS)
SLOTS = 7

def stages_a():
    tiles, last = range(NT), NT - 1
    order = [("sp", "load"), ("sp", ("adj", 0)), ("sp", ("adj", 1)), ("pool", ("adj", 0))]
    for t in tiles:
        order += [("pe", ("adj", t)), ("act", ("adj", t))] + [("sp", ("adj", t + 2))] * (t + 2 <= last)
    order += [("pe", "h0"), ("act", "h0"), ("pe", "h0x"), ("dve", "h0x"), ("act", "h0x"), ("pool", "tall"),
              ("dve", "tall"), ("pe", "tB"), ("act", "v0"), ("pool", "v0")]
    for g in range(2):
        order += [("pe", ("c", g, 0)), ("dve", ("c", g, 0)), ("pe", ("c", g, 1)), ("act", ("c", g, 0)),
                  ("dve", ("c", g, 1)), ("act", ("c", g, 1)), ("dve", ("p0", g, 0))]
        for t in tiles:
            order += [("dve", ("p0", g, t + 1))] * (t < last) + [("pe", ("p0", g, t))]
        order += [("act", ("o", g)), ("pe", ("o", g)), ("dve", ("o", g)), ("pool", ("y0", g)), ("dve", ("y0", g))]
    order += [("dve", "mean0"), ("act", "mean0"), ("dve", "ln0"), ("pe", "h1"), ("act", "h1"), ("pe", "h1x"),
              ("dve", "h1x"), ("act", "h1x"), ("pe", "s1"), ("act", "s1"), ("dve", "s1"), ("pe", "nT"), ("dve", "nT"),
              ("act", ("att1", 0)), ("act", ("att1", 1)), ("dve", ("att1", 0))]
    for t in tiles:
        order += [("act", ("att1", t + 2))] * (t + 2 <= last) + [("dve", ("att1", t + 1))] * (t < last)
        order += [("pe", ("att1", t))]
    return order + [("dve", "y1"), ("dve", "mean1"), ("act", "mean1"), ("dve", "ln1"), ("pe", "x25"), ("act", "x25"),
                    ("pe", "sup1"), ("act", "sup1"), ("pe", "h25"), ("dve", "h25"), ("pe", "sup2"), ("act", "sup2"),
                    ("pe", "o25"), ("dve", "o25"), ("dve", "mean2"), ("act", "mean2"), ("dve", "ln2"), ("dve", "negT")]


def stages_b():
    def all_of(stage):
        return [(eng, stage) for eng in ("pe", "dve", "act", "sp", "pool")]

    order = [("pe", "x3"), ("act", "x3T"), ("sp", "x3"), ("pool", "x3"), ("pe", "qk"), ("act", "qk"), ("dve", "qk"),
             ("sp", "qk"), ("pool", "qk"), ("act", "rest"), ("pe", "parts"), ("pool", "parts"), ("act", "parts"),
             ("sp", "parts"), ("sp", "stack")]
    for t in range(NT):
        order += all_of(("max", t, 0)) + all_of(("max", t, 1))
    for g in range(2):
        order += [("dve", ("shift", g)), ("pe", ("shift", g)), ("act", ("shift", g)), ("sp", ("shift row", g))]
        for t in range(NT):
            order += all_of(("att", g, t, 0)) + all_of(("att", g, t, 1))
        order += [("pe", ("end", g)), ("act", ("end", g))]
    return order + [("pe", "o3"), ("dve", "o3"), ("pe", "on"), ("act", "on"), ("pe", "z"), ("dve", "z"), ("dve", "mean3"),
                    ("act", "mean3"), ("dve", "ln3"), ("sp", "ln3")]


A_STAGES, B_STAGES = stages_a(), stages_b()


PLACES = [
    0, 0, 9, 10, 10, 12, 14, 16, 20, 20, 21, 23, 28, 30, 30, 33, 33, 36, 38, 38,
    40, 40, 44, 45, 48, 53, 53, 53, 58, 60, 60, 63, 63, 63, 68, 68, 68, 70, 73, 80,
    81, 84, 84, 87, 90, 90, 90, 94, 96, 96, 99, 102, 104, 107, 109, 116, 118, 119, 119, 119,
    122, 124, 124, 129, 129, 129, 131, 133, 151, 151, 151, 151, 151, 151, 151, 151, 151, 153, 155, 157,
    161, 164, 167, 169, 174, 174, 177, 177, 179, 181, 183, 184, 185, 189, 190, 192, 192, 193, 198, 202,
    206, 207, 209, 209, 209, 212, 212, 220, 228, 228, 228, 228, 228, 230, 230, 230, 230, 230, 230, 230,
    230, 230, 230, 230, 246, 246, 246, 248, 260, 260, 265, 265, 265, 265, 266, 268, 270, 273, 274, 276,
    276, 276, 276, 276, 276,
]


def merged():
    order, b = [], 0
    for n, place in enumerate(PLACES):
        order += [("B", *s) for s in B_STAGES[b:place]] + [("A", *A_STAGES[n])]
        b = place
    return order + [("B", *s) for s in B_STAGES[b:]]


ORDER = merged()


def bank_plan():
    keys = [("max", k) for k in range(8 * NT)] + [("shift", 0)]
    for k in range(8 * NT):
        keys += [("score", k), ("max", 8 * NT + k)]
    keys += [("shift", 1)] + [("score", k) for k in range(8 * NT, 16 * NT)]
    return ({key: 5 + n % 3 for n, key in enumerate(keys)},
            {key: keys[n - 3] if n >= 3 else None for n, key in enumerate(keys)})


BANK, BEFORE = bank_plan()


def build(nc, a):
    with ExitStack() as ctx:
        def sb(name, shape, dt=F32):
            return ctx.enter_context(nc.sbuf_tensor(name, shape, dt))

        def sem(name):
            return ctx.enter_context(nc.semaphore(name))

        ps = ctx.enter_context(nc.psum_tensor("ps", [P, 8, 512], F32))

        def banks(first, count):
            return ps[:, first:first + count, :].rearrange("p b n -> p (b n)")

        ident = sb("ident", [P, P])
        identb = sb("identb", [P, P], BF16)
        ones = sb("ones", [P, P])
        w0x = sb("w0x", [P, D + H0])
        w0s = sb("w0s", [P, H0, P])
        w1x = sb("w1x", [P, D + 1])
        w1s = sb("w1s", [P, P])
        b1x = sb("b1x", [1, D + 1])
        w2a = sb("w2a", [P, G * DH])
        b2a = sb("b2a", [P, G * 2])
        w2b = sb("w2b", [P, G * 2, D])
        b2b = sb("b2b", [1, G * D])
        gpair = sb("gpair", [GN, G, GN])
        grow = sb("grow", [GN, G])
        gw = sb("gw", [GN, G])
        wT = sb("wT", [P, 4, P])
        web = sb("web", [P, H3])
        maskall = sb("maskall", [P, B * NT])
        small = sb("small", [P, 8])
        epst = sb("epst", [P, 1])

        adja = sb("adja", [P, 2, N])
        adjT = sb("adjT", [P, NT, N], BF16)
        xr = sb("xr", [P, NT, D])
        yr = sb("yr", [P, NT, D])
        xT = sb("xT", [P, N])
        cs = sb("cs", [P, 2, N])
        ringa = sb("ringa", [P, 4, N])
        oT = sb("oT", [P, 2, N])
        v0_all = sb("v0", [P, NT * H0 * (D0 + 1) + C0 - D0 - 1])
        v0 = v0_all[:, 0:NT * H0 * (D0 + 1)].rearrange("p (t h c) -> p t h c", t=NT, h=H0)
        hx = sb("hx", [P, NT, D + 1])
        eh = cs[:, 0, 0:NT * C0].rearrange("p (t c) -> p t c", t=NT)
        tt = sb("tt", [P, NT, H0])
        tB = sb("tB", [P, NT, H0])
        tE = sb("tE", [P, NT, H0])
        tmx = sb("tmx", [P, H0])
        tall = sb("tall", [P, H0])
        den = sb("den", [P, NT, H0])
        emp = sb("emp", [P, NT, H0])
        hsum = sb("hsum", [P, D])
        s2 = sb("s2", [P, NT])
        msk = sb("msk", [P, NT])
        fac = sb("fac", [P, NT])
        stats = sb("stats", [P, NT, 6])
        mv = sb("mv", [P, NT, 2])
        sd = sb("sd", [P, NT])
        a25 = sb("a25", [GN, GN])
        agr = sb("agr", [GN, G, GN])
        nT = sb("nT", [GN, G, GN])
        deg = sb("deg", [GN, 4, G])
        nadj = sb("nadj", [GN, G, GN])
        x25T = sb("x25T", [P, GN])
        h25 = oT[:, 0, 0:G * 2 * GN].rearrange("p (g n) -> p g n", g=G * 2)
        f25 = sb("f25", [GN, D])
        flata = ringa[:].rearrange("p a n -> p (a n)")
        sup1 = flata[0:GN, 0:G * DH]
        sup2 = flata[0:GN, 2 * N:2 * N + G * D]
        o25 = flata[0:GN, 3 * N:3 * N + G * D].rearrange("p (g d) -> p g d", g=G)

        adjb = sb("adjb", [P, 2, HALF])
        neg = sb("neg", [P, 2, N], BF16)
        negT = sb("negT", [P, NT, N], BF16)
        x3 = sb("x3", [P, NT, D])
        qk_all = sb("qk", [P, 2, H3 * N], BF16)
        qk = qk_all[0:KQ + 1].rearrange("p s (h n) -> p s h n", h=H3)
        qs, ks = qk[:, 0], qk[:, 1]
        ring = sb("ring", [P, SLOTS, N])
        flat = ring[:].rearrange("p a n -> p (a n)")
        parts = flat[:, 0:3 * N].bitcast(BF16).rearrange("p (s c n) -> p s c n", s=2, c=3)
        rest = ring[:, 3:5]
        junk = sb("junk", [P, 2, HALF], BF16)
        v3_all = sb("v3", [P, NT * H3 * (D3 + 1) + C3 - D3 - 1])
        v3 = v3_all[:, 0:NT * H3 * (D3 + 1)].rearrange("p (t h c) -> p t h c", t=NT, h=H3)
        mx = sb("mx", [P, 2, H3, NT])
        sh = sb("sh", [P, 2, H3 // 2, NT])
        shT = sb("shT", [H3 // 2 * NT, 2, P], BF16)
        oz = sb("oz", [P, 2, N])
        x3T, o3n = oz[:, 0], oz[:, 1].rearrange("p (t d) -> p t d", t=NT)
        den3 = sb("den3", [P, NT, H3])
        stat3 = sb("stat3", [P, NT, 6])
        mv3 = sb("mv3", [P, NT, 2])
        sd3 = sb("sd3", [P, NT])
        parts_d = nc.dram_tensor("qk_parts", [2, 3, P, N], BF16).ap()

        raw = ring[:, 5].rearrange("p (w n) -> p w n", w=NT)
        mrow = ring[0:B * NT, 6, 0:P]
        w0t = ring[:, 6, P:2 * P]
        ablk = ring[:, 6, 2 * P:2 * P + 2 * H0]
        acol = ring[:, 6, 3 * P:3 * P + 3]
        attb = ring[0:1, 6, 4 * P:4 * P + 1]
        fus = ring[0:GN, 6, 5 * P:5 * P + G]

        PER, HEAD = {}, {}

        def signal(name, per=1, head=0):
            s = sem(name)
            PER[s], HEAD[s] = per, head
            return s

        weights_in = sem("weights_in")
        waits_alone = sem("waits_alone")
        setup_t = sem("setup_t")
        setup_v = sem("setup_v")
        setup_a = sem("setup_a")
        setup_g = sem("setup_g")
        adja_in = [signal(f"adja_in_{n}", 8 * NT) for n in range(2)]
        x_in = signal("x_in", 16)
        adjT_ps = signal("adjT_ps", 2 * NT, head=3)
        adjT_ok = signal("adjT_ok", 2 * NT)
        agr_ok = signal("agr_ok", 2, head=1)
        mask_ok = signal("mask_ok")
        deg_ok = signal("deg_ok", 3)
        degroot_ok = signal("degroot_ok")
        dinv_ok = signal("dinv_ok", 3)
        nadj_ok = signal("nadj_ok")
        nadjT_ps = signal("nadjT_ps")
        nadjT_ok = signal("nadjT_ok")
        xT_ps = signal("xT_ps", 2)
        xT_ok = signal("xT_ok", 2)
        h0_ps = signal("h0_ps")
        h0_ok = signal("h0_ok", 3)
        t_ok = signal("t_ok", 3)
        tmax_ok = signal("tmax_ok")
        tall_ok = signal("tall_ok")
        td_ok = signal("td_ok")
        tBE_ok = signal("tBE_ok", 2)
        v0_ok = signal("v0_ok", 2)
        hsum_ps = signal("hsum_ps")
        hsum_ok = signal("hsum_ok")
        s0_ps = signal("s0_ps", H0)
        c_relu = signal("c_relu", H0)
        c_ok = signal("c_ok", H0)
        p0_ok = signal("p0_ok", H0 * NT)
        pv0 = signal("pv0", 2 * NT)
        oT0_ok = signal("oT0_ok", 2)
        o0_ps = signal("o0_ps", 2)
        emp_ok = signal("emp_ok", 2)
        den0_ok = signal("den0_ok", 4)
        eh_ok = signal("eh_ok", 2)
        y0_ok = signal("y0_ok", 5)
        y1_ok = signal("y1_ok", 4)
        ln_stats = signal("ln_stats", 3 * NT)
        ln_aggr = signal("ln_aggr", 3 * NT)
        ln_root = signal("ln_root", 3)
        ln_rec = signal("ln_rec", 3)
        ln_ok = signal("ln_ok", 3 * NT, head=1)
        h1_ps = signal("h1_ps")
        h1_ok = signal("h1_ok", 3)
        s2_ok = signal("s2_ok", 3)
        s1_ps = signal("s1_ps")
        s1_ok = signal("s1_ok")
        sig_ok = signal("sig_ok", NT)
        p1_ok = signal("p1_ok", NT)
        pv1 = signal("pv1", NT)
        negT_ok = signal("negT_ok", head=1)
        fac_ok = signal("fac_ok", 7)
        x25_ps = signal("x25_ps")
        x25_ok = signal("x25_ok")
        sup1_ps = signal("sup1_ps")
        sup1_ok = signal("sup1_ok")
        h25_ps = signal("h25_ps")
        h25_ok = signal("h25_ok", 2)
        sup2_ps = signal("sup2_ps")
        sup2_ok = signal("sup2_ok")
        o25_ps = signal("o25_ps")
        o25_ok = signal("o25_ok", G + 2)
        adjb_in = [signal(f"adjb_in_{n}", 32 * NT) for n in range(2)]
        neg_ok = signal("neg_ok", 4 * NT, head=2)
        x3T_ps = signal("x3T_ps")
        x3T_ok = signal("x3T_ok")
        qk_ps = signal("qk_ps", 2)
        v_ps = signal("v_ps")
        v3_ok = signal("v3_ok")
        part1_ok = signal("part1_ok", 2)
        rest_ok = signal("rest_ok", 2)
        part2_ok = signal("part2_ok", 2)
        part3_ok = signal("part3_ok", 2)
        parts_out = signal("parts_out", 32)
        stack_in = [signal(f"stack_in_{g}", 16 * 2 * len(TERMS), head=1) for g in range(2)]
        mxs_ps = signal("mxs_ps", 2 * H3 * NT)
        mx_ok = signal("mx_ok", 2 * H3 * NT, head=1)
        sh_ok = signal("sh_ok", 6)
        shT_ps = signal("shT_ps", 2)
        shT_ok = signal("shT_ok", 2)
        shift_in = signal("shift_in", 32)
        sc_ps = signal("sc_ps", 2 * H3 * NT, head=1)
        p3_ok = signal("p3_ok", 2 * H3 * NT)
        pv3 = signal("pv3", 4 * NT)
        oT3_ok = signal("oT3_ok", 2)
        o3_ps = signal("o3_ps", 2)
        den3_ok = signal("den3_ok", 2)
        on_ok = signal("on_ok", 2)
        onT_ps = signal("onT_ps")
        onT_ok = signal("onT_ok")
        z_ps = signal("z_ps")
        y3_ok = signal("y3_ok", head=1)
        ln3_stats = signal("ln3_stats", NT)
        ln3_aggr = signal("ln3_aggr", NT)
        ln3_root = signal("ln3_root")
        ln3_rec = signal("ln3_rec")
        ln3_ok = signal("ln3_ok", NT)
        stored = signal("stored", 16, head=1)

        def at(eng, b, s, k):
            if isinstance(b, int):
                return PER[s] * b + k + HEAD[s]
            value = registers[eng]
            eng.reg_mul(value, b[0], PER[s])
            eng.reg_add(value, value, PER[s] * b[1] + k + HEAD[s])
            return value

        def of(array, b):
            return array[b] if isinstance(b, int) else array[b[0] + b[1]]

        x_d = a["x"].rearrange("b (t p) d -> b p t d", p=P)
        out_d = a["out"].rearrange("b (t p) d -> b p t d", p=P)
        names = ["L0_gnn_W", "L1_gnn_W", "L3_gnn_W_q", "L3_gnn_W_k", "L3_gnn_W_v", "L3_gnn_W_o"]

        def tiles(first):
            return banks(first, 2).rearrange("p (t n) -> p t n", t=NT)

        def threes():
            return [(n, ps[:, n, :], 3 * n, min(3, NT - 3 * n)) for n in range(3)]

        def unit(k):
            return k // (8 * NT), k // 8 % NT, k // 2 % 4, k % 2

        registers = {eng: ctx.enter_context(eng.register(f"wait_value_{n}"))
                     for n, eng in enumerate([nc.sync, nc.gpsimd, nc.scalar, nc.vector, nc.tensor])}
        block = ctx.enter_context(nc.Block())

        def turns(eng, name, early, late):
            for _ in early(0):
                pass
            with eng.Fori(0, B - 1) as r:
                work = {"A": early((r, 1)), "B": late((r, 0))}
                coming = {which: next(work[which]) for which in work}
                for which, whose, stage in ORDER:
                    if whose == name and coming[which] == stage:
                        coming[which] = next(work[which], None)
                assert coming == {"A": None, "B": None}
            for _ in late(B - 1):
                pass

        @block.sync
        def _(sp):
            def load(dst, src, **how):
                sp.dma_start(dst, src, **how).then_inc(weights_in, 16)

            for n, name in enumerate(names):
                load(raw[:, n, :], a[name])
            load(ident[:], a["ident"])
            load(gpair[:], a["gpair"])
            load(grow[:], a["grow"])
            sp.wait_ge(setup_g, 1)
            for h in range(H0):
                for half in range(2):
                    load(ablk[D0 * h:D0 * h + D0, H0 * half + h:H0 * half + h + 1],
                         a["L0_gnn_a"][h, D0 * half:D0 * half + D0].rearrange("(d o) -> d o", o=1))
            for n, name in enumerate(["L1_gnn_a1", "L1_gnn_a2", "L1_gnn_b"]):
                load(acol[:, n:n + 1], a[name].rearrange("(d o) -> d o", o=1))
            load(b1x[:, 0:D], a["L1_gnn_b"].rearrange("(o d) -> o d", o=1))
            load(attb, a["L1_gnn_att_b"].rearrange("(o d) -> o d", o=1))
            load(w2a[:].rearrange("p (g e) -> p g e", g=G), a["L2_gnn_W1"].rearrange("g d e -> d g e"))
            load(b2a[:], a["L2_gnn_b1"].rearrange("g (c e) -> e (g c)", e=P), allow_slow_non_contiguous=True)
            load(w2b[:].rearrange("p (g c) d -> p g c d", g=G), a["L2_gnn_W2"].rearrange("g (c e) d -> e g c d", e=P))
            load(b2b[:], a["L2_gnn_b2"].rearrange("(o g) d -> o (g d)", o=1))
            load(fus, a["L2_gnn_fusion_w"].rearrange("(o g) -> o g", o=1).broadcast_to([GN, G]))
            load(web[:], a["L3_gnn_W_e"].rearrange("h o -> o h").broadcast_to([P, H3]))
            load(mrow, a["nodemask"].rearrange("b (t p) -> (b t) p", p=P))
            for s in (adjT_ps, agr_ok, ln_ok, negT_ok, neg_ok, mx_ok, sc_ps, y3_ok, stored, *stack_in):
                sp.wait_ge(setup_v, SETUP_V).then_inc(s, HEAD[s])

            def early(b):
                yield "load"
                sp.wait_ge(ln_ok, at(sp, b, ln_ok, 0))
                sp.dma_start(xr[:], of(x_d, b)).then_inc(x_in, 16)
                for t in range(NT):
                    yield "adj", t
                    sp.wait_ge(adjT_ps, at(sp, b, adjT_ps, 2 * t - 2))
                    sp.wait_ge(agr_ok, at(sp, b, agr_ok, 1 if t >= 2 else 0))
                    sp.dma_start(adja[:, t % 2], of(a["adj"], b)[t * P:(t + 1) * P]).then_inc(adja_in[t % 2], 16)

            def late(b):
                yield "x3"
                def load_adj(m):
                    t = m % NT
                    for half in range(2):
                        sp.wait_ge(neg_ok, at(sp, b, neg_ok, 2 * m + half - 1))
                        sp.dma_start(adjb[:, half], of(a["adj"], b)[t * P:(t + 1) * P, half * HALF:(half + 1) * HALF])\
                            .then_inc(adjb_in[half], 16)

                load_adj(0)
                yield "qk"
                load_adj(1)
                yield "parts"
                load_adj(2)
                yield "stack"
                for g in range(2):
                    sp.wait_ge(stack_in[g], at(sp, b, stack_in[g], 0))
                for side in range(2):
                    sp.wait_ge(part3_ok, at(sp, b, part3_ok, side + 1))
                    sp.dma_start(parts_d[side].rearrange("c p n -> p c n"), parts[:, side]).then_inc(parts_out, 16)
                sp.wait_ge(parts_out, at(sp, b, parts_out, 32))
                for g in range(2):
                    heads = slice(4 * g, 4 * g + 4)
                    for side in range(2):
                        for t, pair in enumerate(TERMS):
                            sp.dma_start(qk[D3 * t:D3 * t + D3, side, heads, :],
                                         parts_d[side, pair[side]].rearrange("(h d) n -> d h n", h=H3)[:, heads])\
                                .then_inc(stack_in[g], 16)
                for t in range(NT):
                    yield "max", t, 1
                    load_adj(t + 3)
                for g in range(2):
                    yield "shift row", g
                    sp.wait_ge(shT_ok, at(sp, b, shT_ok, g + 1))
                    sp.dma_start(qs[KQ:KQ + 1, 4 * g:4 * g + 4].rearrange("o h (t n) -> o (h t) n", n=P), shT[:, g])\
                        .then_inc(shift_in, 16)
                    for t in range(NT - 3):
                        if g == 0:
                            yield "att", 0, t, 1
                            load_adj(NT + t + 3)
                yield "ln3"
                sp.wait_ge(ln3_ok, at(sp, b, ln3_ok, NT))
                sp.dma_start(of(out_d, b), o3n).then_inc(stored, 16)

            turns(sp, "sp", early, late)
            sp.wait_ge(stored, at(sp, B, stored, 0))

        W_ALL = 16 * (len(names) + 3 + 2 * H0 + 3 + 1 + 1 + 4 + 2 + 1)

        @block.gpsimd
        def _(pool):
            pool.memset(ablk, 0.0).then_inc(setup_g, 1)
            pool.memset(ones[:], 1.0).then_inc(setup_g, 1)
            pool.memset(v0_all[:], 0.0).then_inc(setup_g, 1)
            pool.memset(v3_all[:], 0.0).then_inc(setup_g, 1)
            pool.memset(epst[:], EPS).then_inc(setup_g, 1)
            pool.memset(hx[:], 1.0).then_inc(setup_g, 1)
            pool.wait_ge(setup_g, 6)
            pool.memset(v3[:, :, :, D3:D3 + 1], 1.0).then_inc(setup_g, 1)
            pool.wait_ge(setup_v, SETUP_V)

            def early(b):
                yield "adj", 0
                pool.wait_ge(adja_in[0], at(pool, b, adja_in[0], 16))
                pool.wait_ge(ln_ok, at(pool, b, ln_ok, 0))
                pool.tensor_tensor(a25[:], adja[0:GN, 0, 0:GN], ident[0:GN, 0:GN], ALU.add).then_inc(agr_ok, 1)
                pool.wait_ge(agr_ok, at(pool, b, agr_ok, 1))
                pool.tensor_tensor(agr[:], a25[:].unsqueeze(1).broadcast_to([GN, G, GN]), gpair[:], ALU.mult)\
                    .then_inc(agr_ok, 1)
                first = b * NT if isinstance(b, int) else (b[0] + b[1]) * NT
                pool.tensor_copy(msk[:], maskall[:, bass.ds(first, NT)]).then_inc(mask_ok, 1)
                yield "tall"
                pool.wait_ge(tmax_ok, at(pool, b, tmax_ok, 1)).then_inc(waits_alone, 1)
                pool.partition_all_reduce(tall[:], tmx[:], P, RMAX).then_inc(tall_ok, 1)
                yield "v0"
                pool.wait_ge(tBE_ok, at(pool, b, tBE_ok, 2))
                pool.wait_ge(h0_ok, at(pool, b, h0_ok, 3))
                pool.tensor_tensor(v0[:, :, :, 0:D0], hx[:, :, 0:D].rearrange("p t (h d) -> p t h d", h=H0),
                                   tB[:].unsqueeze(3).broadcast_to([P, NT, H0, D0]), ALU.mult).then_inc(v0_ok, 1)
                pool.tensor_copy(v0[:, :, :, D0:D0 + 1], tB[:].unsqueeze(3)).then_inc(v0_ok, 1)
                for g in range(2):
                    yield "y0", g
                    pool.wait_ge(emp_ok, at(pool, b, emp_ok, g + 1))
                    pool.wait_ge(hsum_ok, at(pool, b, hsum_ok, 1))
                    if g == 1:
                        pool.wait_ge(y0_ok, at(pool, b, y0_ok, 1))
                    pool.tensor_tensor(
                        eh.rearrange("p t (h d) -> p t h d", h=2),
                        emp[:, :, 2 * g:2 * g + 2].unsqueeze(3).broadcast_to([P, NT, 2, D0]),
                        hsum[:, C0 * g:C0 * g + C0].rearrange("p (h d) -> p h d", h=2).unsqueeze(1)
                        .broadcast_to([P, NT, 2, D0]), ALU.mult).then_inc(eh_ok, 1)

            def late(b):
                def mask(m):
                    for half in range(2):
                        pool.wait_ge(adjb_in[half], at(pool, b, adjb_in[half], 16 * (m + 1)))
                        pool.wait_ge(mx_ok, at(pool, b, mx_ok, 8 * max(m - 1, 0))).then_inc(waits_alone, 1)
                        pool.tensor_scalar(neg[:, m % 2, half * HALF:(half + 1) * HALF], adjb[:, half], -1.0, BIG,
                                           ALU.add, ALU.mult).then_inc(neg_ok, 1)

                yield "x3"
                mask(0)
                yield "qk"
                mask(1)
                yield "parts"
                for side in range(2):
                    pool.wait_ge(part2_ok, at(pool, b, part2_ok, side + 1))
                    pool.tensor_tensor(parts[:, side, 2], rest[:, side], parts[:, side, 1], ALU.subtract)\
                        .then_inc(part3_ok, 1)
                for t in range(NT):
                    yield "max", t, 1
                    mask(t + 2)
                for t in range(NT - 2):
                    yield "att", 0, t, 1
                    mask(NT + t + 2)

            turns(pool, "pool", early, late)

        @block.scalar
        def _(act):
            act.wait_ge(setup_v, 5)
            nc.scalar.activation(gw[:], gw[:], ACT.Exp).then_inc(setup_a, 1)
            act.wait_ge(setup_v, SETUP_V)

            def copy(out, in_, s, scale=1.0):
                nc.scalar.activation(out, in_, ACT.Copy, scale=scale).then_inc(s, 1)

            def early(b):
                def root(layer):
                    act.wait_ge(ln_aggr, at(act, b, ln_aggr, NT * (layer + 1)))
                    nc.scalar.activation(sd[:], mv[:, :, 1], ACT.Sqrt, bias=epst[:, 0:1]).then_inc(ln_root, 1)

                act.wait_ge(negT_ok, at(act, b, negT_ok, 0))
                for t in range(NT):
                    yield "adj", t
                    for part in range(2):
                        u = 2 * t + part
                        act.wait_ge(adjT_ps, at(act, b, adjT_ps, u + 1))
                        copy(adjT[:, 4 * part:4 * part + 4, t * P:(t + 1) * P],
                             banks(u % 3, 1).rearrange("p (j n) -> p j n", j=4), adjT_ok)
                yield "h0"
                act.wait_ge(xT_ps, at(act, b, xT_ps, 1))
                copy(xT[:], banks(0, 2), xT_ok)
                yield "h0x"
                act.wait_ge(t_ok, at(act, b, t_ok, 3))
                for _, bank, t, k in threes():
                    copy(hx[:, t:t + k, 0:D],
                         bank[:, 0:k * (D + H0)].rearrange("p (t n) -> p t n", t=k)[:, :, 0:D], h0_ok)
                yield "v0"
                act.wait_ge(hsum_ps, at(act, b, hsum_ps, 1))
                copy(hsum[:], banks(2, 1)[:, 0:D], hsum_ok)
                act.wait_ge(td_ok, at(act, b, td_ok, 1))
                nc.scalar.activation(tB[:], tt[:], ACT.Exp, scale=0.2).then_inc(tBE_ok, 1)
                nc.scalar.activation(tE[:], tt[:], ACT.Exp, scale=0.8).then_inc(tBE_ok, 1)
                for g in range(2):
                    for q in range(2):
                        yield "c", g, q
                        act.wait_ge(c_relu, at(act, b, c_relu, 2 * g + q + 1))
                        nc.scalar.activation(cs[:, q], cs[:, q], ACT.Exp, scale=-0.8).then_inc(c_ok, 1)
                    yield "o", g
                    act.wait_ge(pv0, at(act, b, pv0, NT * (g + 1)))
                    copy(oT[:, g], banks(0, 2), oT0_ok)
                yield "mean0"
                root(0)
                yield "h1"
                act.wait_ge(xT_ps, at(act, b, xT_ps, 2))
                copy(xT[:], banks(0, 2), xT_ok)
                yield "h1x"
                act.wait_ge(s2_ok, at(act, b, s2_ok, 3))
                for _, bank, t, k in threes():
                    copy(hx[:, t:t + k, 0:D],
                         bank[:, 0:k * (D + 1)].rearrange("p (t n) -> p t n", t=k)[:, :, 0:D], h1_ok)
                yield "s1"
                act.wait_ge(s1_ps, at(act, b, s1_ps, 1))
                copy(cs[:, 0], banks(0, 2), s1_ok)
                act.wait_ge(deg_ok, at(act, b, deg_ok, 3))
                nc.scalar.activation(deg[:, 3], deg[:, 2], ACT.Sqrt).then_inc(degroot_ok, 1)
                for t in range(NT):
                    yield "att1", t
                    if t == 0:
                        act.wait_ge(s1_ok, at(act, b, s1_ok, 1))
                    if t >= 2:
                        act.wait_ge(p1_ok, at(act, b, p1_ok, t - 1))
                    nc.scalar.activation(oT[:, t % 2], cs[:, 0], ACT.Sigmoid, bias=s2[:, t:t + 1]).then_inc(sig_ok, 1)
                yield "mean1"
                root(1)
                yield "x25"
                act.wait_ge(x25_ps, at(act, b, x25_ps, 1))
                copy(x25T[:], banks(0, 1)[:, 0:GN], x25_ok)
                yield "sup1"
                act.wait_ge(sup1_ps, at(act, b, sup1_ps, 1))
                copy(sup1, banks(0, 3)[0:GN, 0:G * DH], sup1_ok)
                yield "sup2"
                act.wait_ge(sup2_ps, at(act, b, sup2_ps, 1))
                copy(sup2, banks(1, 2)[0:GN, 0:G * D], sup2_ok)
                yield "mean2"
                root(2)

            def late(b):
                yield "x3T"
                act.wait_ge(x3T_ps, at(act, b, x3T_ps, 1))
                copy(x3T, banks(3, 2), x3T_ok)
                yield "qk"
                for side, scale in enumerate([0.25, 1.0]):
                    act.wait_ge(qk_ps, at(act, b, qk_ps, side + 1))
                    copy(parts[:, side, 0], banks(5 - 2 * side, 2), part1_ok, scale)
                yield "rest"
                for side in range(2):
                    act.wait_ge(rest_ok, at(act, b, rest_ok, side + 1))
                    copy(parts[:, side, 1], rest[:, side], part2_ok)
                yield "parts"
                act.wait_ge(v_ps, at(act, b, v_ps, 1))
                copy(v3[:, :, :, 0:D3], banks(5, 2).rearrange("p (t h d) -> p t h d", t=NT, h=H3), v3_ok)
                for g in range(2):
                    yield "shift", g
                    act.wait_ge(shT_ps, at(act, b, shT_ps, g + 1))
                    copy(shT[:, g], banks(BANK["shift", g], 1)[0:H3 // 2 * NT, 0:P], shT_ok)
                    for t in range(NT):
                        for k in range(8 * (NT * g + t), 8 * (NT * g + t + 1)):
                            if k % 4 == 0:
                                yield "att", g, t, k % 8 // 4
                            n, half = k // 2, k % 2
                            act.wait_ge(sc_ps, at(act, b, sc_ps, k + 1))
                            if n >= SLOTS and half == 0:
                                act.wait_ge(pv3, at(act, b, pv3, 2 * ((n - SLOTS) // 4 + 1)))
                            nc.scalar.activation(ring[:, n % SLOTS, half * HALF:(half + 1) * HALF],
                                                 banks(BANK["score", k], 1), ACT.Exp).then_inc(p3_ok, 1)
                    yield "end", g
                    act.wait_ge(pv3, at(act, b, pv3, 2 * NT * (g + 1)))
                    if g == 1:
                        act.wait_ge(stored, at(act, b, stored, 0))
                    copy(oz[:, g], banks(3, 2), oT3_ok)
                yield "on"
                act.wait_ge(onT_ps, at(act, b, onT_ps, 1))
                copy(oz[:, 0], banks(3, 2), onT_ok)
                yield "mean3"
                act.wait_ge(ln3_aggr, at(act, b, ln3_aggr, NT))
                nc.scalar.activation(sd3[:], mv3[:, :, 1], ACT.Sqrt, bias=epst[:, 0:1]).then_inc(ln3_root, 1)

            turns(act, "act", early, late)

        @block.vector
        def _(dve):
            steps = [0]

            def step(ins):
                ins.then_inc(setup_v, 1)
                steps[0] += 1
                dve.wait_ge(setup_v, steps[0])

            dve.wait_ge(weights_in, W_ALL)
            step(nc.vector.tensor_copy(identb[:], ident[:]))
            step(nc.vector.tensor_copy(w0x[:, 0:D], raw[:, 0]))
            step(nc.vector.tensor_copy(gw[:], fus))
            step(nc.vector.reduce_max(small[0:GN, 0:1], gw[:], AX_X))
            step(nc.vector.tensor_scalar(gw[:], gw[:], small[0:GN, 0:1], None, ALU.subtract))
            dve.wait_ge(setup_t, 1)
            step(nc.vector.tensor_copy(w0t, banks(0, 1)[:, 0:P]))
            step(nc.vector.tensor_copy(w1x[:, 0:D], banks(0, 1)[:, P:2 * P]))
            step(nc.vector.tensor_copy(wT[:], banks(0, 2)[:, 2 * P:6 * P].rearrange("p (w n) -> p w n", w=4)))
            step(nc.vector.tensor_copy(maskall[:], banks(2, 1)[:, 0:B * NT]))
            dve.wait_ge(setup_t, 2)
            step(nc.vector.tensor_copy(w0x[:, D:D + H0], banks(3, 1)[:, H0:2 * H0]))
            step(nc.vector.tensor_copy(small[:, 0:H0], banks(3, 1)[:, 0:H0]))
            step(nc.vector.tensor_copy(small[:, H0:H0 + 2], banks(3, 1)[:, 16:18]))
            dve.wait_ge(setup_g, 7)
            for h in range(H0):
                step(nc.vector.tensor_scalar(w0s[:, h], ones[:], small[:, h:h + 1], None, ALU.mult))
            step(nc.vector.tensor_scalar(w1s[:], ones[:], small[:, H0:H0 + 1], None, ALU.mult))
            step(nc.vector.tensor_copy(w1x[:, D:D + 1], small[:, H0 + 1:H0 + 2]))
            step(nc.vector.reduce_sum(b1x[:, D:D + 1], banks(3, 1)[0:1, 32:34], AX_X))
            step(nc.vector.tensor_tensor(b1x[:, D:D + 1], b1x[:, D:D + 1], attb, ALU.add))
            dve.wait_ge(setup_a, 1)
            step(nc.vector.reduce_sum(small[0:GN, 6:7], gw[:], AX_X))
            step(nc.vector.reciprocal(small[0:GN, 7:8], small[0:GN, 6:7]))
            step(nc.vector.scalar_tensor_tensor(out=gw[:], in0=gw[:], scalar=small[0:GN, 7:8], in1=grow[:],
                                                op0=ALU.mult, op1=ALU.mult))
            step(nc.vector.memset(qk[KQ:KQ + 1, :], 1.0))
            assert steps[0] == SETUP_V

            def early(b):
                def means(layer, src):
                    for t in range(NT):
                        nc.vector.bn_stats(stats[:, t], src[:, t]).then_inc(ln_stats, 1)
                    dve.wait_ge(ln_stats, at(dve, b, ln_stats, NT * (layer + 1))).then_inc(waits_alone, 1)
                    for t in range(NT):
                        nc.vector.bn_aggr(mv[:, t], stats[:, t]).then_inc(ln_aggr, 1)

                def norm(layer, src, out):
                    dve.wait_ge(ln_root, at(dve, b, ln_root, layer + 1))
                    nc.vector.reciprocal(sd[:], sd[:]).then_inc(ln_rec, 1)
                    dve.wait_ge(ln_rec, at(dve, b, ln_rec, layer + 1))
                    for t in range(NT):
                        nc.vector.tensor_scalar(out[:, t], src[:, t], mv[:, t, 0:1], sd[:, t:t + 1],
                                                ALU.subtract, ALU.mult).then_inc(ln_ok, 1)

                yield "h0x"
                dve.wait_ge(h0_ps, at(dve, b, h0_ps, 1))
                for _, bank, t, k in threes():
                    nc.vector.tensor_copy(tt[:, t:t + k], bank[:, 0:k * (D + H0)].rearrange(
                        "p (t n) -> p t n", t=k)[:, :, D:D + H0]).then_inc(t_ok, 1)
                dve.wait_ge(t_ok, at(dve, b, t_ok, 3))
                nc.vector.reduce_max(tmx[:], tt[:].rearrange("p t h -> p h t"), AX_X).then_inc(tmax_ok, 1)
                yield "tall"
                dve.wait_ge(tall_ok, at(dve, b, tall_ok, 1))
                nc.vector.tensor_tensor(tt[:], tt[:], tall[:].unsqueeze(1).broadcast_to([P, NT, H0]), ALU.subtract)\
                    .then_inc(td_ok, 1)
                for g in range(2):
                    for q in range(2):
                        yield "c", g, q
                        h = 2 * g + q
                        dve.wait_ge(s0_ps, at(dve, b, s0_ps, h + 1))
                        nc.vector.tensor_scalar(cs[:, q], banks(0, 2), tall[:, h:h + 1], 0.0, ALU.add, ALU.max)\
                            .then_inc(c_relu, 1)
                    if g == 0:
                        dve.wait_ge(tBE_ok, at(dve, b, tBE_ok, 2))
                    for t in range(NT):
                        yield "p0", g, t
                        for q in range(2):
                            m, h = NT * g + t, 2 * g + q
                            if t == 0:
                                dve.wait_ge(c_ok, at(dve, b, c_ok, h + 1))
                            if m >= 2 and q == 0:
                                dve.wait_ge(pv0, at(dve, b, pv0, m - 1))
                            nc.vector.scalar_tensor_tensor(
                                out=ringa[:, 2 * (m % 2) + q], in0=cs[:, q], scalar=tE[:, t, h:h + 1], in1=adjT[:, t],
                                op0=ALU.max, op1=ALU.mult).then_inc(p0_ok, 1)
                    yield "o", g
                    O0 = tiles(0).rearrange("p t (h c) -> p t h c", c=C0)
                    mine = slice(2 * g, 2 * g + 2)
                    y4 = yr[:, :, C0 * g:C0 * g + C0].rearrange("p t (h d) -> p t h d", h=2)
                    dve.wait_ge(o0_ps, at(dve, b, o0_ps, g + 1))
                    nc.vector.tensor_scalar(emp[:, :, mine], O0[:, :, :, D0], 0.0, None, ALU.is_equal)\
                        .then_inc(emp_ok, 1)
                    dve.wait_ge(emp_ok, at(dve, b, emp_ok, g + 1))
                    nc.vector.scalar_tensor_tensor(out=den[:, :, mine], in0=emp[:, :, mine], scalar=float(N),
                                                   in1=O0[:, :, :, D0], op0=ALU.mult, op1=ALU.add).then_inc(den0_ok, 1)
                    dve.wait_ge(den0_ok, at(dve, b, den0_ok, 2 * g + 1))
                    nc.vector.reciprocal(den[:, :, mine], den[:, :, mine]).then_inc(den0_ok, 1)
                    yield "y0", g
                    dve.wait_ge(eh_ok, at(dve, b, eh_ok, g + 1))
                    nc.vector.tensor_tensor(y4, O0[:, :, :, 0:D0], eh.rearrange("p t (h d) -> p t h d", h=2),
                                            ALU.add).then_inc(y0_ok, 1)
                    dve.wait_ge(den0_ok, at(dve, b, den0_ok, 2 * g + 2))
                    dve.wait_ge(y0_ok, at(dve, b, y0_ok, 2 * g + 1))
                    nc.vector.tensor_tensor(y4, y4, den[:, :, mine].unsqueeze(3).broadcast_to([P, NT, 2, D0]), ALU.mult)\
                        .then_inc(y0_ok, 1)
                yield "mean0"
                dve.wait_ge(x_in, at(dve, b, x_in, 16))
                dve.wait_ge(y0_ok, at(dve, b, y0_ok, 4))
                nc.vector.tensor_tensor(yr[:], yr[:], xr[:], ALU.add).then_inc(y0_ok, 1)
                dve.wait_ge(y0_ok, at(dve, b, y0_ok, 5))
                means(0, yr)
                yield "ln0"
                norm(0, yr, xr)
                yield "h1x"
                dve.wait_ge(h1_ps, at(dve, b, h1_ps, 1))
                for _, bank, t, k in threes():
                    nc.vector.tensor_copy(s2[:, t:t + k], bank[:, 0:k * (D + 1)].rearrange(
                        "p (t n) -> p t n", t=k)[:, :, D]).then_inc(s2_ok, 1)
                dve.wait_ge(agr_ok, at(dve, b, agr_ok, 2))
                nc.vector.reduce_sum(deg[:, 0], agr[:], AX_X).then_inc(deg_ok, 1)
                dve.wait_ge(deg_ok, at(dve, b, deg_ok, 1))
                nc.vector.tensor_scalar(deg[:, 1], deg[:, 0], 0.0, None, ALU.is_equal).then_inc(deg_ok, 1)
                dve.wait_ge(deg_ok, at(dve, b, deg_ok, 2))
                nc.vector.tensor_tensor(deg[:, 2], deg[:, 0], deg[:, 1], ALU.add).then_inc(deg_ok, 1)
                yield "s1"
                dve.wait_ge(degroot_ok, at(dve, b, degroot_ok, 1))
                nc.vector.reciprocal(deg[:, 2], deg[:, 3]).then_inc(dinv_ok, 1)
                nc.vector.tensor_scalar(deg[:, 0], deg[:, 1], -1.0, 1.0, ALU.mult, ALU.add).then_inc(dinv_ok, 1)
                dve.wait_ge(dinv_ok, at(dve, b, dinv_ok, 2))
                nc.vector.tensor_tensor(deg[:, 3], deg[:, 2], deg[:, 0], ALU.mult).then_inc(dinv_ok, 1)
                dve.wait_ge(dinv_ok, at(dve, b, dinv_ok, 3))
                dinv = deg[:, 3].unsqueeze(2).broadcast_to([GN, G, GN])
                nc.vector.tensor_tensor(nadj[:], agr[:], dinv, ALU.mult).then_inc(nadj_ok, 1)
                yield "nT"
                dve.wait_ge(nadjT_ps, at(dve, b, nadjT_ps, 1))
                nc.vector.tensor_tensor(nT[:], banks(2, 1)[0:GN, 0:G * GN].rearrange("p (g n) -> p g n", g=G), dinv,
                                        ALU.mult).then_inc(nadjT_ok, 1)
                for t in range(NT):
                    yield "att1", t
                    if t == 0:
                        dve.wait_ge(mask_ok, at(dve, b, mask_ok, 1))
                    dve.wait_ge(sig_ok, at(dve, b, sig_ok, t + 1))
                    if t >= 4:
                        dve.wait_ge(pv1, at(dve, b, pv1, t - 3))
                    nc.vector.scalar_tensor_tensor(out=ringa[:, t % 4], in0=oT[:, t % 2], scalar=msk[:, t:t + 1],
                                                   in1=adjT[:, t], op0=ALU.mult, op1=ALU.mult).then_inc(p1_ok, 1)
                yield "y1"
                dve.wait_ge(pv1, at(dve, b, pv1, NT))
                sums = [(bank[:, 0:k * (D + 1)].rearrange("p (t n) -> p t n", t=k), slice(t, t + k))
                        for _, bank, t, k in threes()]
                for o, t in sums:
                    nc.vector.tensor_tensor(fac[:, t], o[:, :, D], msk[:, t], ALU.mult).then_inc(fac_ok, 1)
                dve.wait_ge(fac_ok, at(dve, b, fac_ok, 3))
                nc.vector.tensor_scalar(fac[:], fac[:], 1e-8, None, ALU.add).then_inc(fac_ok, 1)
                dve.wait_ge(fac_ok, at(dve, b, fac_ok, 4))
                nc.vector.reciprocal(fac[:], fac[:]).then_inc(fac_ok, 1)
                dve.wait_ge(fac_ok, at(dve, b, fac_ok, 5))
                nc.vector.tensor_tensor(fac[:], fac[:], msk[:], ALU.mult).then_inc(fac_ok, 1)
                dve.wait_ge(fac_ok, at(dve, b, fac_ok, 6))
                nc.vector.tensor_tensor(fac[:], fac[:], msk[:], ALU.mult).then_inc(fac_ok, 1)
                dve.wait_ge(fac_ok, at(dve, b, fac_ok, 7))
                for o, t in sums:
                    nc.vector.tensor_tensor(yr[:, t], o[:, :, 0:D],
                                            fac[:, t].unsqueeze(2).broadcast_to([P, t.stop - t.start, D]), ALU.mult)\
                        .then_inc(y1_ok, 1)
                yield "mean1"
                dve.wait_ge(y1_ok, at(dve, b, y1_ok, 3))
                nc.vector.tensor_tensor(yr[:], yr[:], xr[:], ALU.add).then_inc(y1_ok, 1)
                dve.wait_ge(y1_ok, at(dve, b, y1_ok, 4))
                means(1, yr)
                yield "ln1"
                norm(1, yr, xr)
                yield "h25"
                dve.wait_ge(h25_ps, at(dve, b, h25_ps, 1))
                nc.vector.tensor_tensor(h25, banks(0, 1)[:, 0:2 * G * GN].rearrange("p (g n) -> p g n", n=GN),
                                        b2a[:].unsqueeze(2).broadcast_to([P, 2 * G, GN]), ALU.add).then_inc(h25_ok, 1)
                dve.wait_ge(h25_ok, at(dve, b, h25_ok, 1))
                nc.vector.tensor_scalar(h25, h25, 0.0, None, ALU.max).then_inc(h25_ok, 1)
                yield "o25"
                dve.wait_ge(o25_ps, at(dve, b, o25_ps, 1))
                for g in range(G):
                    nc.vector.tensor_scalar(o25[:, g], banks(0, 2)[0:GN, g * D:(g + 1) * D], 0.0, gw[:, g:g + 1],
                                            ALU.max, ALU.mult).then_inc(o25_ok, 1)
                dve.wait_ge(o25_ok, at(dve, b, o25_ok, G))
                nc.vector.tensor_reduce(f25[:], o25[:].rearrange("p g d -> p d g"), AX_X, ALU.add).then_inc(o25_ok, 1)
                dve.wait_ge(o25_ok, at(dve, b, o25_ok, G + 1))
                nc.vector.tensor_tensor(xr[0:GN, 0], xr[0:GN, 0], f25[:], ALU.add).then_inc(o25_ok, 1)
                yield "mean2"
                dve.wait_ge(o25_ok, at(dve, b, o25_ok, G + 2))
                means(2, xr)
                yield "ln2"
                dve.wait_ge(y3_ok, at(dve, b, y3_ok, 0))
                norm(2, xr, x3)
                yield "negT"
                dve.wait_ge(sc_ps, at(dve, b, sc_ps, 0))
                nc.vector.tensor_scalar(negT[:], adjT[:], -1.0, BIG, ALU.add, ALU.mult).then_inc(negT_ok, 1)

            def late(b):
                def maximum(k):
                    g, t, q, half = unit(k)
                    if k % 8 == 0:
                        dve.wait_ge(neg_ok, at(dve, b, neg_ok, 2 * (k // 8) + 2))
                    dve.wait_ge(mx_ok, at(dve, b, mx_ok, max(k - 1, 0)))
                    dve.wait_ge(mxs_ps, at(dve, b, mxs_ps, k + 1)).then_inc(waits_alone, 1)
                    nc.vector.tensor_tensor_reduce(
                        out=junk[:, k % 2], in0=banks(BANK["max", k], 1), in1=neg[:, t % 2, half * HALF:(half + 1) * HALF],
                        scale=1.0, scalar=-3e38, op0=ALU.add, op1=ALU.max,
                        accum_out=mx[:, half, 4 * g + q, t:t + 1]).then_inc(mx_ok, 1)

                def shift(g):
                    heads = slice(4 * g, 4 * g + 4)
                    wb = web[:, heads].unsqueeze(2).broadcast_to([P, 4, NT])
                    dve.wait_ge(mx_ok, at(dve, b, mx_ok, 8 * NT * (g + 1)))
                    nc.vector.tensor_tensor(sh[:, g], mx[:, 0, heads], mx[:, 1, heads], ALU.max).then_inc(sh_ok, 1)
                    dve.wait_ge(sh_ok, at(dve, b, sh_ok, 3 * g + 1))
                    nc.vector.tensor_tensor(sh[:, g], sh[:, g], wb, ALU.add).then_inc(sh_ok, 1)
                    dve.wait_ge(sh_ok, at(dve, b, sh_ok, 3 * g + 2))
                    nc.vector.tensor_tensor(sh[:, g], wb, sh[:, g], ALU.subtract).then_inc(sh_ok, 1)

                yield "qk"
                for side, scale in enumerate([0.25, 1.0]):
                    dve.wait_ge(part1_ok, at(dve, b, part1_ok, side + 1))
                    nc.vector.scalar_tensor_tensor(out=rest[:, side], in0=banks(5 - 2 * side, 2), scalar=scale,
                                                   in1=parts[:, side, 0], op0=ALU.mult, op1=ALU.subtract)\
                        .then_inc(rest_ok, 1)
                for t in range(NT):
                    for c in range(2):
                        yield "max", t, c
                        for k in range(8 * t + 4 * c, 8 * t + 4 * c + 4):
                            maximum(k)
                yield "shift", 0
                shift(0)
                for t in range(NT):
                    for c in range(2):
                        yield "att", 0, t, c
                        for k in range(8 * (NT + t) + 4 * c, 8 * (NT + t) + 4 * c + 4):
                            maximum(k)
                yield "shift", 1
                shift(1)
                yield "o3"
                for g in range(2):
                    O3 = tiles(3 + 2 * g).rearrange("p t (h c) -> p t h c", c=C3)
                    heads = slice(4 * g, 4 * g + 4)
                    dve.wait_ge(o3_ps, at(dve, b, o3_ps, 2))
                    nc.vector.reciprocal(den3[:, :, heads], O3[:, :, :, D3]).then_inc(den3_ok, 1)
                    dve.wait_ge(den3_ok, at(dve, b, den3_ok, g + 1))
                    nc.vector.tensor_tensor(
                        o3n[:, :, C0 * g:C0 * g + C0].rearrange("p t (h d) -> p t h d", h=4), O3[:, :, :, 0:D3],
                        den3[:, :, heads].unsqueeze(3).broadcast_to([P, NT, 4, D3]), ALU.mult).then_inc(on_ok, 1)
                yield "z"
                dve.wait_ge(z_ps, at(dve, b, z_ps, 1))
                nc.vector.tensor_tensor(o3n, tiles(5), x3[:], ALU.add).then_inc(y3_ok, 1)
                yield "mean3"
                dve.wait_ge(y3_ok, at(dve, b, y3_ok, 1))
                for t in range(NT):
                    nc.vector.bn_stats(stat3[:, t], o3n[:, t]).then_inc(ln3_stats, 1)
                dve.wait_ge(ln3_stats, at(dve, b, ln3_stats, NT)).then_inc(waits_alone, 1)
                for t in range(NT):
                    nc.vector.bn_aggr(mv3[:, t], stat3[:, t]).then_inc(ln3_aggr, 1)
                yield "ln3"
                dve.wait_ge(ln3_root, at(dve, b, ln3_root, 1))
                nc.vector.reciprocal(sd3[:], sd3[:]).then_inc(ln3_rec, 1)
                dve.wait_ge(ln3_rec, at(dve, b, ln3_rec, 1))
                for t in range(NT):
                    nc.vector.tensor_scalar(o3n[:, t], o3n[:, t], mv3[:, t, 0:1], sd3[:, t:t + 1],
                                            ALU.subtract, ALU.mult).then_inc(ln3_ok, 1)

            turns(dve, "dve", early, late)

        @block.tensor
        def _(pe):
            mm, tr = nc.tensor.matmul, nc.tensor.transpose
            pe.wait_ge(weights_in, W_ALL)
            for n in range(len(names)):
                tr(banks(0, 2)[:, n * P:(n + 1) * P], raw[:, n], ident[:])
            tr(banks(2, 1)[:, 0:B * NT], mrow, ident[0:B * NT, 0:B * NT]).then_inc(setup_t, 1)
            pe.wait_ge(setup_v, 6)
            mm(banks(3, 1)[:, 0:2 * H0], w0t, ablk, start=True, stop=True)
            mm(banks(3, 1)[:, 16:18], raw[:, 1], acol[:, 0:2], start=True, stop=True)
            mm(banks(3, 1)[0:1, 32:34], acol[:, 2:3], acol[:, 0:2], start=True, stop=True).then_inc(setup_t, 1)
            pe.wait_ge(setup_v, SETUP_V)
            pe.wait_ge(setup_g, 7)

            def turn_x(first, x, s):
                for t in range(NT):
                    last = tr(banks(first, 2)[:, t * P:(t + 1) * P], x[:, t], ident[:])
                last.then_inc(s, 1)

            def early(b):
                pe.wait_ge(ln_ok, at(pe, b, ln_ok, 0))
                for i in range(NT):
                    yield "adj", i
                    pe.wait_ge(adja_in[i % 2], at(pe, b, adja_in[i % 2], 16 * (i // 2 + 1)))
                    for part in range(2):
                        u = 2 * i + part
                        if u >= 3:
                            pe.wait_ge(adjT_ok, at(pe, b, adjT_ok, u - 2))
                        for j in range(4):
                            c = (4 * part + j) * P
                            last = tr(banks(u % 3, 1)[:, j * P:(j + 1) * P], adja[:, i % 2, c:c + P], ident[:])
                        last.then_inc(adjT_ps, 1)
                yield "h0"
                pe.wait_ge(x_in, at(pe, b, x_in, 16))
                pe.wait_ge(adjT_ok, at(pe, b, adjT_ok, 2 * NT))
                turn_x(0, xr, xT_ps)
                yield "h0x"
                pe.wait_ge(xT_ok, at(pe, b, xT_ok, 1))
                for _, bank, t, k in threes():
                    for i in range(k):
                        last = mm(bank[:, i * (D + H0):(i + 1) * (D + H0)], xT[:, (t + i) * P:(t + i + 1) * P], w0x[:],
                                  start=True, stop=True)
                last.then_inc(h0_ps, 1)
                yield "tB"
                pe.wait_ge(h0_ok, at(pe, b, h0_ok, 3))
                for t in range(NT):
                    last = mm(banks(2, 1)[:, 0:D], ones[:], hx[:, t, 0:D], start=(t == 0), stop=(t == NT - 1))
                last.then_inc(hsum_ps, 1)
                for g in range(2):
                    for q in range(2):
                        yield "c", g, q
                        h = 2 * g + q
                        if q == 1:
                            pe.wait_ge(c_relu, at(pe, b, c_relu, h))
                        elif g == 1:
                            pe.wait_ge(y0_ok, at(pe, b, y0_ok, 1))
                        for half in range(2):
                            last = mm(banks(half, 1), w0s[:, h], xT[:, half * HALF:(half + 1) * HALF],
                                      start=True, stop=True)
                        last.then_inc(s0_ps, 1)
                    for t in range(NT):
                        yield "p0", g, t
                        m = NT * g + t
                        if t == 0:
                            pe.wait_ge(c_relu, at(pe, b, c_relu, 2 * g + 2))
                            pe.wait_ge(v0_ok, at(pe, b, v0_ok, 2))
                        pe.wait_ge(p0_ok, at(pe, b, p0_ok, 2 * (m + 1)))
                        for half in range(2):
                            for q in range(2):
                                first = (H0 * t + 2 * g + q) * (D0 + 1)
                                last = mm(banks(half, 1)[C0 * q:C0 * (q + 1)], v0_all[:, first:first + C0],
                                          ringa[:, 2 * (m % 2) + q, half * HALF:(half + 1) * HALF],
                                          start=(t == 0), stop=(t == NT - 1))
                        last.then_inc(pv0, 1)
                    yield "o", g
                    pe.wait_ge(oT0_ok, at(pe, b, oT0_ok, g + 1)).then_inc(waits_alone, 1)
                    for t in range(NT):
                        last = tr(tiles(0)[:, t], oT[:, g, t * P:(t + 1) * P], ident[:])
                    last.then_inc(o0_ps, 1)
                yield "h1"
                pe.wait_ge(ln_ok, at(pe, b, ln_ok, NT))
                turn_x(0, xr, xT_ps)
                yield "h1x"
                pe.wait_ge(xT_ok, at(pe, b, xT_ok, 2))
                for _, bank, t, k in threes():
                    for i in range(k):
                        out = bank[:, i * (D + 1):(i + 1) * (D + 1)]
                        mm(out, ones[0:1, :], b1x[:], start=True, stop=False)
                        last = mm(out, xT[:, (t + i) * P:(t + i + 1) * P], w1x[:], start=False, stop=True)
                last.then_inc(h1_ps, 1)
                yield "s1"
                pe.wait_ge(s2_ok, at(pe, b, s2_ok, 3))
                pe.wait_ge(h1_ok, at(pe, b, h1_ok, 3))
                for half in range(2):
                    last = mm(banks(half, 1), w1s[:], xT[:, half * HALF:(half + 1) * HALF], start=True, stop=True)
                last.then_inc(s1_ps, 1)
                yield "nT"
                pe.wait_ge(nadj_ok, at(pe, b, nadj_ok, 1)).then_inc(waits_alone, 1)
                for g in range(G):
                    last = tr(banks(2, 1)[0:GN, g * GN:(g + 1) * GN], nadj[:, g], ident[0:GN, 0:GN])
                last.then_inc(nadjT_ps, 1)
                for j in range(NT):
                    yield "att1", j
                    if j == 0:
                        pe.wait_ge(s1_ok, at(pe, b, s1_ok, 1))
                        pe.wait_ge(nadjT_ok, at(pe, b, nadjT_ok, 1))
                    pe.wait_ge(p1_ok, at(pe, b, p1_ok, j + 1))
                    for _, bank, t, k in threes():
                        for i in range(k):
                            last = mm(bank[:, i * (D + 1):(i + 1) * (D + 1)], ringa[:, j % 4, (t + i) * P:(t + i + 1) * P],
                                      hx[:, j], start=(j == 0 and i == 0), stop=(j == NT - 1), skip_group_check=True)
                    last.then_inc(pv1, 1)
                yield "x25"
                pe.wait_ge(ln_ok, at(pe, b, ln_ok, 2 * NT)).then_inc(waits_alone, 1)
                tr(banks(0, 1)[:, 0:GN], xr[0:GN, 0], ident[0:GN, 0:GN]).then_inc(x25_ps, 1)
                yield "sup1"
                pe.wait_ge(x25_ok, at(pe, b, x25_ok, 1))
                for c in range(0, G * DH, HALF):
                    w = min(HALF, G * DH - c)
                    last = mm(banks(0, 3)[0:GN, c:c + w], x25T[:], w2a[:, c:c + w], start=True, stop=True)
                last.then_inc(sup1_ps, 1)
                yield "h25"
                pe.wait_ge(sup1_ok, at(pe, b, sup1_ok, 1)).then_inc(waits_alone, 1)
                for n in range(2 * G):
                    last = mm(banks(0, 1)[:, n * GN:(n + 1) * GN], sup1[:, n * P:(n + 1) * P], nT[:, n // 2],
                              start=True, stop=True)
                last.then_inc(h25_ps, 1)
                yield "sup2"
                pe.wait_ge(h25_ok, at(pe, b, h25_ok, 2))
                for n in range(2 * G):
                    last = mm(banks(1, 2)[0:GN, n // 2 * D:(n // 2 + 1) * D], h25[:, n], w2b[:, n],
                              start=(n % 2 == 0), stop=(n % 2 == 1))
                last.then_inc(sup2_ps, 1)
                yield "o25"
                pe.wait_ge(sup2_ok, at(pe, b, sup2_ok, 1)).then_inc(waits_alone, 1)
                for g in range(G):
                    out = banks(0, 2)[0:GN, g * D:(g + 1) * D]
                    mm(out, ones[0:1, 0:GN], b2b[:, g * D:(g + 1) * D], start=True, stop=False)
                    last = mm(out, nT[:, g], sup2[:, g * D:(g + 1) * D], start=False, stop=True)
                last.then_inc(o25_ps, 1)

            def late(b):
                yield "x3"
                def free(key):
                    if BEFORE[key]:
                        what, k = BEFORE[key]
                        reader = {"max": mx_ok, "score": p3_ok, "shift": shT_ok}[what]
                        pe.wait_ge(reader, at(pe, b, reader, k + 1))
                    return banks(BANK[key], 1)

                def for_max(k):
                    g, t, q, half = unit(k)
                    mm(free(("max", k)), qs[0:KQ, 4 * g + q, t * P:(t + 1) * P],
                       ks[0:KQ, 4 * g + q, half * HALF:(half + 1) * HALF], start=True, stop=True).then_inc(mxs_ps, 1)

                def scores(k):
                    g, t, q, half = unit(k)
                    out, cols = free(("score", k)), slice(half * HALF, (half + 1) * HALF)
                    mm(out, identb[:], negT[:, t, cols], start=True, stop=False)
                    mm(out, ks[:, 4 * g + q, t * P:(t + 1) * P], qs[:, 4 * g + q, cols], start=False, stop=True)\
                        .then_inc(sc_ps, 1)

                def values(m, half):
                    g, t = m // NT, m % NT
                    if m == NT:
                        pe.wait_ge(oT3_ok, at(pe, b, oT3_ok, 1))
                    pe.wait_ge(p3_ok, at(pe, b, p3_ok, 8 * (m + 1)))
                    for q in range(4):
                        first = (H3 * t + 4 * g + q) * (D3 + 1)
                        last = mm(banks(3 + half, 1)[C3 * q:C3 * (q + 1)], v3_all[:, first:first + C3],
                                  ring[:, (4 * m + q) % SLOTS, half * HALF:(half + 1) * HALF],
                                  start=(t == 0), stop=(t == NT - 1))
                    last.then_inc(pv3, 1)

                pe.wait_ge(ln_ok, at(pe, b, ln_ok, 3 * NT))
                turn_x(3, x3, x3T_ps)
                yield "qk"
                pe.wait_ge(x3T_ok, at(pe, b, x3T_ok, 1))
                for side in range(2):
                    for half in range(2):
                        last = mm(banks(5 - 2 * side + half, 1), wT[:, side], x3T[:, half * HALF:(half + 1) * HALF],
                                  start=True, stop=True)
                    last.then_inc(qk_ps, 1)
                yield "parts"
                pe.wait_ge(rest_ok, at(pe, b, rest_ok, 1))
                for t in range(NT):
                    last = mm(banks(5, 2)[:, t * P:(t + 1) * P], x3T[:, t * P:(t + 1) * P], wT[:, 2], start=True, stop=True)
                last.then_inc(v_ps, 1)
                for t in range(NT):
                    for c in range(2):
                        yield "max", t, c
                        if (t, c) == (0, 0):
                            pe.wait_ge(v3_ok, at(pe, b, v3_ok, 1))
                            pe.wait_ge(rest_ok, at(pe, b, rest_ok, 2))
                            pe.wait_ge(stack_in[0], at(pe, b, stack_in[0], PER[stack_in[0]]))
                        for k in range(8 * t + 4 * c, 8 * t + 4 * c + 4):
                            for_max(k)
                for g in range(2):
                    yield "shift", g
                    bank = free(("shift", g))
                    pe.wait_ge(sh_ok, at(pe, b, sh_ok, 3 * g + 3)).then_inc(waits_alone, 1)
                    tr(bank[0:H3 // 2 * NT, 0:P], sh[:, g].rearrange("p h t -> p (h t)"), ident[:]).then_inc(shT_ps, 1)
                    for t in range(NT):
                        for k in range(8 * (NT * g + t), 8 * (NT * g + t + 1)):
                            if k % 4 == 0:
                                yield "att", g, t, k % 8 // 4
                            if k % (8 * NT) == 0:
                                pe.wait_ge(shift_in, at(pe, b, shift_in, 16 * (g + 1)))
                            if k == 0:
                                pe.wait_ge(stack_in[1], at(pe, b, stack_in[1], PER[stack_in[1]]))
                                pe.wait_ge(negT_ok, at(pe, b, negT_ok, 1))
                            scores(k)
                            if g == 0:
                                for_max(8 * NT + k)
                            if t >= 1 and k % 8 in (2, 4):
                                values(NT * g + t - 1, k % 8 // 4)
                    yield "end", g
                    values(NT * g + NT - 1, 0)
                    values(NT * g + NT - 1, 1)
                yield "o3"
                pe.wait_ge(oT3_ok, at(pe, b, oT3_ok, 2))
                pe.wait_ge(p3_ok, at(pe, b, p3_ok, 16 * NT))
                for g in range(2):
                    for t in range(NT):
                        last = tr(tiles(3 + 2 * g)[:, t], oz[:, g, t * P:(t + 1) * P], ident[:])
                    last.then_inc(o3_ps, 1)
                yield "on"
                pe.wait_ge(on_ok, at(pe, b, on_ok, 2))
                turn_x(3, o3n, onT_ps)
                yield "z"
                pe.wait_ge(onT_ok, at(pe, b, onT_ok, 1))
                for t in range(NT):
                    last = mm(banks(5, 2)[:, t * P:(t + 1) * P], oz[:, 0, t * P:(t + 1) * P], wT[:, 3],
                              start=True, stop=True)
                last.then_inc(z_ps, 1)

            turns(pe, "pe", early, late)

_INS = ['x', 'adj', 'nodemask', 'L0_gnn_W', 'L0_gnn_a', 'L1_gnn_W', 'L1_gnn_b', 'L1_gnn_a1', 'L1_gnn_a2',
        'L1_gnn_att_b', 'L2_gnn_W1', 'L2_gnn_b1', 'L2_gnn_W2', 'L2_gnn_b2', 'L2_gnn_fusion_w', 'L3_gnn_W_q',
        'L3_gnn_W_k', 'L3_gnn_W_v', 'L3_gnn_W_e', 'L3_gnn_W_o']


def shape_constants():
    pair = np.zeros((GN, G, GN), np.float32)
    row = np.zeros((GN, G), np.float32)
    for g, nodes in enumerate(GROUPS):
        row[nodes, g] = 1.0
        pair[np.ix_(nodes, [g], nodes)] = 1.0
    return {"ident": np.eye(P, dtype=np.float32), "gpair": pair, "grow": row}


def kernel(**inputs):
    import concourse.bacc as _bacc
    from concourse.bass_utils import run_bass_kernel_spmd as _run

    nc = _bacc.Bacc("TRN2", target_bir_lowering=False, num_devices=1)
    arrays, aps = {}, {}
    for name in _INS:
        v = np.ascontiguousarray(inputs[name])
        arrays[name] = v.reshape(1) if v.ndim == 0 else v
    arrays.update(shape_constants())
    arrays = {f"in_{name}": v for name, v in arrays.items()}
    for name, v in arrays.items():
        aps[name[3:]] = nc.dram_tensor(name, v.shape, mybir.dt.from_np(v.dtype), kind="ExternalInput").ap()
    aps["out"] = nc.dram_tensor("out_nodes", (B, N, D), F32, kind="ExternalOutput").ap()
    build(nc, aps)
    return _run(nc, [arrays], core_ids=[0]).results[0]["out_nodes"]
```

```python
from contextlib import ExitStack

import concourse.bass as bass
import numpy as np
from concourse import mybir

ALU = mybir.AluOpType
ACT = mybir.ActivationFunctionType
F32 = mybir.dt.float32
BF16 = mybir.dt.bfloat16
AX_X = mybir.AxisListType.X
RMAX = bass.bass_isa.ReduceOp.max

P = 128
B, N, D = 8, 1024, 128
NT = N // P
HALF = 512
H0, D0 = 4, 32
C0 = 64
H3, D3 = 8, 16
C3 = 32
AHEAD = 4
G, GN, DH = 5, 25, 256
GROUPS = [list(range(25)), [0, 1, 2, 3, 4, 5, 6, 7, 8], [0, 9, 10, 11, 12, 13, 14],
          [6, 7, 8, 12, 13, 14], [3, 4, 5, 9, 10, 11]]
SETUP_V = 25
BIG = float(2.0 ** 100)
EPS = 1e-5
TERMS = [(0, 0), (1, 0), (2, 0), (0, 1), (1, 1), (0, 2)]
RUNS = [[(0, 3, 0), (3, 2, 0), (5, 1, 0)],
        [(0, 1, 0), (1, 1, 0), (2, 2, 0), (4, 2, 1)]]
KQ = D3 * len(TERMS)
SLOTS = 10
QUARTERS = 4
UNITS = 4 * NT
QT = NT // 2

def stages_a():
    tiles, last = range(NT), NT - 1
    order = [("sp", "load")] + [("sp", ("adj", t)) for t in range(AHEAD)] + [("pool", ("adj", 0))]
    for t in tiles:
        order += [("pe", ("adj", t)), ("act", ("adj", t))] + [("sp", ("adj", t + AHEAD))] * (t + AHEAD <= last)
    order += [("pe", "h0"), ("act", "h0"), ("pe", "h0x"), ("dve", "h0x"), ("act", "h0x"), ("pool", "tall"),
              ("dve", "tall"), ("pe", "tB"), ("act", "v0"), ("pool", "v0")]
    for g in range(2):
        order += [("pe", ("c", g, 0)), ("dve", ("c", g, 0)), ("pe", ("c", g, 1)), ("act", ("c", g, 0)),
                  ("dve", ("c", g, 1)), ("act", ("c", g, 1)), ("dve", ("p0", g, 0))]
        for t in tiles:
            order += [("dve", ("p0", g, t + 1))] * (t < last) + [("pe", ("p0", g, t))]
        order += [("act", ("o", g)), ("pe", ("o", g)), ("dve", ("o", g)), ("pool", ("y0", g)), ("dve", ("y0", g))]
    order += [("dve", "mean0"), ("act", "mean0"), ("dve", "ln0"), ("pe", "h1"), ("act", "h1"), ("pe", "h1x"),
              ("dve", "h1x"), ("act", "h1x"), ("pe", "s1"), ("act", "s1"), ("dve", "s1"), ("pe", "nT"), ("dve", "nT"),
              ("act", ("att1", 0)), ("act", ("att1", 1)), ("dve", ("att1", 0))]
    for t in tiles:
        order += [("act", ("att1", t + 2))] * (t + 2 <= last) + [("dve", ("att1", t + 1))] * (t < last)
        order += [("pe", ("att1", t))]
    return order + [("dve", "y1"), ("dve", "mean1"), ("act", "mean1"), ("dve", "ln1"), ("pe", "x25"), ("act", "x25"),
                    ("pe", "sup1"), ("act", "sup1"), ("pe", "h25"), ("dve", "h25"), ("pe", "sup2"), ("act", "sup2"),
                    ("pe", "o25"), ("dve", "o25"), ("dve", "mean2"), ("act", "mean2"), ("dve", "ln2"), ("dve", "negT")]


def stages_b():
    def all_of(stage):
        return [(eng, stage) for eng in ("pe", "dve", "act", "sp", "pool")]

    order = [("pe", "x3"), ("act", "x3T"), ("sp", "x3"), ("pool", "x3"), ("pe", "qk"), ("act", "qk"), ("dve", "qk"),
             ("sp", "qk"), ("pool", "qk"), ("act", "rest"), ("pe", "parts"), ("dve", "parts"), ("act", "parts"),
             ("sp", ("parts", 0)), ("sp", ("parts", 1)), ("sp", ("stack", 0)), ("sp", ("stack", 1))]
    for t in range(NT):
        order += all_of(("max", t))
    for u in range(QUARTERS):
        order += [("dve", ("shift", u)), ("pe", ("shift", u)), ("act", ("shift", u)), ("sp", ("shift row", u))]
        for t in range(NT):
            order += all_of(("att", u, t))
        order += [("pe", ("end", u)), ("act", ("end", u))]
    return order + [("pe", "o3"), ("dve", "o3"), ("pe", "on"), ("act", "on"), ("pe", "z"), ("dve", "z"), ("dve", "mean3"),
                    ("act", "mean3"), ("dve", "ln3"), ("sp", "ln3")]


A_STAGES, B_STAGES = stages_a(), stages_b()


PLACES = [
    0, 1, 1, 1, 4, 4, 7, 6, 6, 7, 6, 6, 7, 8, 6, 8, 11, 7, 12, 13,
    13, 15, 13, 18, 15, 18, 15, 19, 17, 15, 20, 18, 16, 17, 22, 22, 17, 17, 18, 22,
    29, 38, 51, 55, 54, 59, 60, 62, 61, 79, 78, 83, 85, 103, 102, 107, 106, 106, 107, 108,
    110, 109, 117, 119, 122, 126, 128, 126, 137, 137, 150, 151, 152, 153, 160, 165, 168, 165, 169, 165,
    169, 167, 169, 167, 168, 169, 169, 177, 182, 181, 182, 187, 189, 191, 192, 193, 197, 193, 196, 195,
    199, 196, 200, 196, 196, 205, 196, 211, 197, 196, 214, 198, 199, 217, 201, 199, 220, 201, 204, 224,
    203, 206, 225, 203, 227, 203, 203, 227, 228, 212, 229, 217, 219, 224, 223, 225, 237, 237, 237, 243,
    243, 246, 246, 246, 250,
]


def merged():
    order = []
    for b in range(len(B_STAGES) + 1):
        order += [("A", *A_STAGES[n]) for n in range(len(PLACES)) if PLACES[n] == b]
        order += [("B", *s) for s in B_STAGES[b:b + 1]]
    return order


ORDER = merged()


def bank_plan():
    keys = [("max", k) for k in range(UNITS)]
    for u in range(QUARTERS):
        keys.append(("shift", u))
        for k in range(UNITS * u, UNITS * (u + 1)):
            keys += [("score", k)] + [("max", UNITS + k)] * (u < QUARTERS - 1)
    return ({key: 4 + n % 4 for n, key in enumerate(keys)},
            {key: keys[n - 4] if n >= 4 else None for n, key in enumerate(keys)})


BANK, BEFORE = bank_plan()


def build(nc, a):
    with ExitStack() as ctx:
        def sb(name, shape, dt=F32):
            return ctx.enter_context(nc.sbuf_tensor(name, shape, dt))

        def sem(name):
            return ctx.enter_context(nc.semaphore(name))

        ps = ctx.enter_context(nc.psum_tensor("ps", [P, 8, 512], F32))

        def banks(first, count):
            return ps[:, first:first + count, :].rearrange("p b n -> p (b n)")

        ident = sb("ident", [P, P])
        identb = sb("identb", [P, P], BF16)
        ones = sb("ones", [P, P])
        w0x = sb("w0x", [P, D + H0])
        w0s = sb("w0s", [P, H0, P])
        w1x = sb("w1x", [P, D + 1])
        w1s = sb("w1s", [P, P])
        b1x = sb("b1x", [1, D + 1])
        w2a = sb("w2a", [P, G * DH])
        b2a = sb("b2a", [P, G * 2])
        w2b = sb("w2b", [P, G * 2, D])
        b2b = sb("b2b", [1, G * D])
        gpair = sb("gpair", [GN, G, GN])
        grow = sb("grow", [GN, G])
        gw = sb("gw", [GN, G])
        wT = sb("wT", [P, 4, P])
        web = sb("web", [P, H3])
        maskall = sb("maskall", [P, B * NT])
        small = sb("small", [P, 8])
        epst = sb("epst", [P, 1])

        adja = sb("adja", [P, AHEAD, N])
        adjT = sb("adjT", [P, NT, N], BF16)
        xr = sb("xr", [P, NT, D])
        yr = sb("yr", [P, NT, D])
        xT = sb("xT", [P, N])
        cs = sb("cs", [P, 2, N])
        ringa = sb("ringa", [P, 4, N])
        oT = sb("oT", [P, 2, N])
        v0_all = sb("v0", [P, NT * H0 * (D0 + 1) + C0 - D0 - 1])
        v0 = v0_all[:, 0:NT * H0 * (D0 + 1)].rearrange("p (t h c) -> p t h c", t=NT, h=H0)
        hx = sb("hx", [P, NT, D + 1])
        eh = cs[:, 0, 0:NT * C0].rearrange("p (t c) -> p t c", t=NT)
        tt = sb("tt", [P, NT, H0])
        tB = sb("tB", [P, NT, H0])
        tE = sb("tE", [P, NT, H0])
        tmx = sb("tmx", [P, H0])
        tall = sb("tall", [P, H0])
        den = sb("den", [P, NT, H0])
        emp = sb("emp", [P, NT, H0])
        hsum = sb("hsum", [P, D])
        s2 = sb("s2", [P, NT])
        msk = sb("msk", [P, NT])
        fac = sb("fac", [P, NT])
        stats = sb("stats", [P, NT, 6])
        mv = sb("mv", [P, NT, 2])
        sd = sb("sd", [P, NT])
        a25 = sb("a25", [GN, GN])
        agr = sb("agr", [GN, G, GN])
        nT = sb("nT", [GN, G, GN])
        deg = sb("deg", [GN, 4, G])
        nadj = sb("nadj", [GN, G, GN])
        x25T = sb("x25T", [P, GN])
        h25 = oT[:, 0, 0:G * 2 * GN].rearrange("p (g n) -> p g n", g=G * 2)
        f25 = sb("f25", [GN, D])
        flata = ringa[:].rearrange("p a n -> p (a n)")
        sup1 = flata[0:GN, 0:G * DH]
        sup2 = flata[0:GN, 2 * N:2 * N + G * D]
        o25 = flata[0:GN, 3 * N:3 * N + G * D].rearrange("p (g d) -> p g d", g=G)

        adjb = sb("adjb", [P, 2, HALF])
        neg = sb("neg", [P, 2, N], BF16)
        negT = sb("negT", [P, NT, N], BF16)
        x3 = sb("x3", [P, NT, D])
        qk_all = sb("qk", [P, 2, H3 * N], BF16)
        qk = qk_all[0:KQ + 1].rearrange("p s (h n) -> p s h n", h=H3)
        qs = qk_all[0:KQ + 1, 0].rearrange("p (u h n) -> p u h n", u=QUARTERS, h=4)
        ks = qk[:, 1]
        ring = sb("ring", [P, SLOTS, HALF])
        flat = ring[:].rearrange("p a n -> p (a n)")
        parts = flat[:, 0:3 * N].bitcast(BF16).rearrange("p (s c n) -> p s c n", s=2, c=3)
        rest = flat[:, 3 * N:5 * N].rearrange("p (s n) -> p s n", s=2)
        junk = sb("junk", [P, 2, HALF], BF16)
        v3_all = sb("v3", [P, NT * H3 * (D3 + 1) + C3 - D3 - 1])
        v3 = v3_all[:, 0:NT * H3 * (D3 + 1)].rearrange("p (t h c) -> p t h c", t=NT, h=H3)
        mx = sb("mx", [P, 2, QUARTERS, 4, QT])
        sh = sb("sh", [P, QUARTERS, 4, QT])
        shT = sb("shT", [4 * QT, QUARTERS, P], BF16)
        oz = sb("oz", [P, 2, N])
        x3T, o3n = oz[:, 0], oz[:, 1].rearrange("p (t d) -> p t d", t=NT)
        den3 = sb("den3", [P, NT, H3])
        stat3 = sb("stat3", [P, NT, 6])
        mv3 = sb("mv3", [P, NT, 2])
        sd3 = sb("sd3", [P, NT])
        q_parts = nc.dram_tensor("q_parts", [2, 3, P, HALF], BF16).ap()
        k_parts = nc.dram_tensor("k_parts", [3, P, N], BF16).ap()

        raw = x3
        spare = oz[:, 0].rearrange("p (w n) -> p w n", w=NT)
        mrow = spare[0:B * NT, 0]
        w0t = spare[:, 1]
        ablk = spare[:, 2, 0:2 * H0]
        acol = spare[:, 3, 0:3]
        attb = spare[0:1, 4, 0:1]
        fus = spare[0:GN, 5, 0:G]

        PER, HEAD = {}, {}

        def signal(name, per=1, head=0):
            s = sem(name)
            PER[s], HEAD[s] = per, head
            return s

        first_in = sem("first_in")
        weights_in = sem("weights_in")
        waits_alone = sem("waits_alone")
        setup_t = sem("setup_t")
        setup_v = sem("setup_v")
        setup_a = sem("setup_a")
        setup_g = sem("setup_g")
        adja_in = [signal(f"adja_in_{n}", 16 * NT // AHEAD) for n in range(AHEAD)]
        x_in = signal("x_in", 16)
        adjT_ps = signal("adjT_ps", 2 * NT, head=2 * AHEAD - 1)
        adjT_ok = signal("adjT_ok", 2 * NT)
        agr_ok = signal("agr_ok", 2, head=1)
        mask_ok = signal("mask_ok")
        deg_ok = signal("deg_ok", 3)
        degroot_ok = signal("degroot_ok")
        dinv_ok = signal("dinv_ok", 3)
        nadj_ok = signal("nadj_ok")
        nadjT_ps = signal("nadjT_ps")
        nadjT_ok = signal("nadjT_ok")
        xT_ps = signal("xT_ps", 2)
        xT_ok = signal("xT_ok", 2)
        h0_ps = signal("h0_ps")
        h0_ok = signal("h0_ok", 3)
        t_ok = signal("t_ok", 3)
        tmax_ok = signal("tmax_ok")
        tall_ok = signal("tall_ok")
        td_ok = signal("td_ok")
        tBE_ok = signal("tBE_ok", 2)
        v0_ok = signal("v0_ok", 2)
        hsum_ps = signal("hsum_ps")
        hsum_ok = signal("hsum_ok")
        s0_ps = signal("s0_ps", H0)
        c_relu = signal("c_relu", H0)
        c_ok = signal("c_ok", H0)
        p0_ok = signal("p0_ok", H0 * NT)
        pv0 = signal("pv0", 2 * NT)
        oT0_ok = signal("oT0_ok", 2)
        o0_ps = signal("o0_ps", 2)
        emp_ok = signal("emp_ok", 2)
        den0_ok = signal("den0_ok", 4)
        eh_ok = signal("eh_ok", 2)
        y0_ok = signal("y0_ok", 5)
        y1_ok = signal("y1_ok", 4)
        ln_stats = signal("ln_stats", 3 * NT)
        ln_aggr = signal("ln_aggr", 3 * NT)
        ln_root = signal("ln_root", 3)
        ln_rec = signal("ln_rec", 3)
        ln_ok = signal("ln_ok", 3 * NT, head=1)
        h1_ps = signal("h1_ps")
        h1_ok = signal("h1_ok", 3)
        s2_ok = signal("s2_ok", 3)
        s1_ps = signal("s1_ps")
        s1_ok = signal("s1_ok")
        sig_ok = signal("sig_ok", NT)
        p1_ok = signal("p1_ok", NT)
        pv1 = signal("pv1", NT)
        negT_ok = signal("negT_ok", head=1)
        fac_ok = signal("fac_ok", 7)
        x25_ps = signal("x25_ps")
        x25_ok = signal("x25_ok")
        sup1_ps = signal("sup1_ps")
        sup1_ok = signal("sup1_ok")
        h25_ps = signal("h25_ps")
        h25_ok = signal("h25_ok", 2)
        sup2_ps = signal("sup2_ps")
        sup2_ok = signal("sup2_ok")
        o25_ps = signal("o25_ps")
        o25_ok = signal("o25_ok", G + 2)
        adjb_in = [signal(f"adjb_in_{n}", 32 * NT) for n in range(2)]
        neg_ok = signal("neg_ok", 4 * NT, head=2)
        x3T_ps = signal("x3T_ps", head=1)
        x3_ok = signal("x3_ok", head=1)
        x3T_ok = signal("x3T_ok")
        qk_ps = signal("qk_ps", 2)
        v_ps = signal("v_ps")
        v3_ok = signal("v3_ok")
        part1_ok = signal("part1_ok", 2)
        rest_ok = signal("rest_ok", 2)
        part2_ok = signal("part2_ok", 2)
        part3_ok = signal("part3_ok", 2)
        parts_out = signal("parts_out", 48)
        stack_in = [signal(f"stack_in_{g}", 16 * (len(RUNS[0]) + len(RUNS[1])), head=1) for g in range(2)]
        mxs_ps = signal("mxs_ps", 2 * H3 * NT)
        mx_ok = signal("mx_ok", 2 * H3 * NT, head=1)
        sh_ok = signal("sh_ok", 3 * QUARTERS)
        shT_ps = signal("shT_ps", QUARTERS)
        shT_ok = signal("shT_ok", QUARTERS)
        shift_in = signal("shift_in", 16 * QUARTERS)
        sc_ps = signal("sc_ps", 2 * H3 * NT, head=1)
        p3_ok = signal("p3_ok", 2 * H3 * NT)
        pv3 = signal("pv3", QUARTERS * NT)
        oT3_ok = signal("oT3_ok", QUARTERS)
        o3_ps = signal("o3_ps", 2)
        den3_ok = signal("den3_ok", 2)
        on_ok = signal("on_ok", 2)
        onT_ps = signal("onT_ps")
        onT_ok = signal("onT_ok")
        z_ps = signal("z_ps")
        y3_ok = signal("y3_ok", head=1)
        ln3_stats = signal("ln3_stats", NT)
        ln3_aggr = signal("ln3_aggr", NT)
        ln3_root = signal("ln3_root")
        ln3_rec = signal("ln3_rec")
        ln3_ok = signal("ln3_ok", NT)
        stored = signal("stored", 16, head=1)

        def at(eng, b, s, k):
            if isinstance(b, int):
                return PER[s] * b + k + HEAD[s]
            value = registers[eng]
            if eng is nc.sync:
                eng.reg_mul(value, b[0], PER[s])
                eng.reg_add(value, value, PER[s] * b[1] + k + HEAD[s])
            else:
                eng.reg_add(value, rises[eng, PER[s]], PER[s] * b[1] + k + HEAD[s])
            return value

        def of(array, b):
            return array[b] if isinstance(b, int) else array[b[0] + b[1]]

        x_d = a["x"].rearrange("b (t p) d -> b p t d", p=P)
        out_d = a["out"].rearrange("b (t p) d -> b p t d", p=P)
        names = ["L0_gnn_W", "L1_gnn_W", "L3_gnn_W_q", "L3_gnn_W_k", "L3_gnn_W_v", "L3_gnn_W_o"]

        def tiles(first):
            return banks(first, 2).rearrange("p (t n) -> p t n", t=NT)

        def threes():
            return [(n, ps[:, n, :], 3 * n, min(3, NT - 3 * n)) for n in range(3)]

        def max_unit(k):
            return k // UNITS, k // 8 % QT, k // 2 % 4, k % 2

        def score_unit(k):
            return k // UNITS, k // 4 % NT, k % 4

        registers = {eng: ctx.enter_context(eng.register(f"wait_value_{n}"))
                     for n, eng in enumerate([nc.sync, nc.gpsimd, nc.scalar, nc.vector, nc.tensor])}
        rises = {(eng, per): ctx.enter_context(eng.register(f"rises_{per}_{n}"))
                 for n, eng in enumerate(registers) if eng is not nc.sync for per in sorted(set(PER.values()))}
        block = ctx.enter_context(nc.Block())

        def advance(work, stages):
            for _ in range(stages):
                next(work)

        def turns(eng, name, early, late, first=None):
            for _ in first or early(0):
                pass
            with eng.Fori(0, B - 1) as r:
                for per in sorted(set(PER.values())) if eng is not nc.sync else []:
                    eng.reg_mul(rises[eng, per], r, per)
                work = {"A": early((r, 1)), "B": late((r, 0))}
                coming = {which: next(work[which]) for which in work}
                for which, whose, stage in ORDER:
                    if whose == name and coming[which] == stage:
                        coming[which] = next(work[which], None)
                assert coming == {"A": None, "B": None}
            for _ in late(B - 1):
                pass

        @block.sync
        def _(sp):
            def early(b):
                yield "load"
                sp.wait_ge(x3_ok, at(sp, b, x3_ok, 0))
                sp.wait_ge(x3T_ps, at(sp, b, x3T_ps, 0))
                sp.dma_start(xr[:], of(x_d, b)).then_inc(x_in, 16)
                for t in range(NT):
                    yield "adj", t
                    sp.wait_ge(adjT_ps, at(sp, b, adjT_ps, 2 * (t + 1 - AHEAD)))
                    sp.wait_ge(agr_ok, at(sp, b, agr_ok, 1 if t >= AHEAD else 0))
                    sp.dma_start(adja[:, t % AHEAD], of(a["adj"], b)[t * P:(t + 1) * P])\
                        .then_inc(adja_in[t % AHEAD], 16)

            def load(dst, src, **how):
                sp.dma_start(dst, src, **how).then_inc(weights_in, 16)

            sp.dma_start(ident[:], a["ident"]).then_inc(first_in, 16)
            sp.dma_start(gpair[:], a["gpair"]).then_inc(first_in, 16)
            for s in (x3T_ps, x3_ok, adjT_ps, agr_ok, ln_ok, negT_ok, neg_ok, mx_ok, sc_ps, y3_ok, stored, *stack_in):
                sp.wait_ge(setup_g, 1).then_inc(s, HEAD[s])
            first = early(0)
            advance(first, 2 + AHEAD)
            for n, name in enumerate(names):
                load(raw[:, n, :], a[name])
            load(grow[:], a["grow"])
            sp.wait_ge(setup_g, 1)
            for h in range(H0):
                for half in range(2):
                    load(ablk[D0 * h:D0 * h + D0, H0 * half + h:H0 * half + h + 1],
                         a["L0_gnn_a"][h, D0 * half:D0 * half + D0].rearrange("(d o) -> d o", o=1))
            for n, name in enumerate(["L1_gnn_a1", "L1_gnn_a2", "L1_gnn_b"]):
                load(acol[:, n:n + 1], a[name].rearrange("(d o) -> d o", o=1))
            load(b1x[:, 0:D], a["L1_gnn_b"].rearrange("(o d) -> o d", o=1))
            load(attb, a["L1_gnn_att_b"].rearrange("(o d) -> o d", o=1))
            load(w2a[:].rearrange("p (g e) -> p g e", g=G), a["L2_gnn_W1"].rearrange("g d e -> d g e"))
            load(b2a[:], a["L2_gnn_b1"].rearrange("g (c e) -> e (g c)", e=P), allow_slow_non_contiguous=True)
            load(w2b[:].rearrange("p (g c) d -> p g c d", g=G), a["L2_gnn_W2"].rearrange("g (c e) d -> e g c d", e=P))
            load(b2b[:], a["L2_gnn_b2"].rearrange("(o g) d -> o (g d)", o=1))
            load(fus, a["L2_gnn_fusion_w"].rearrange("(o g) -> o g", o=1).broadcast_to([GN, G]))
            load(web[:], a["L3_gnn_W_e"].rearrange("h o -> o h").broadcast_to([P, H3]))
            load(mrow, a["nodemask"].rearrange("b (t p) -> (b t) p", p=P))

            def late(b):
                yield "x3"
                def load_adj(m):
                    t = m % NT
                    for half in range(2):
                        sp.wait_ge(neg_ok, at(sp, b, neg_ok, 2 * m + half - 1))
                        sp.dma_start(adjb[:, half], of(a["adj"], b)[t * P:(t + 1) * P, half * HALF:(half + 1) * HALF])\
                            .then_inc(adjb_in[half], 16)

                load_adj(0)
                yield "qk"
                load_adj(1)
                for side in range(2):
                    yield "parts", side
                    sp.wait_ge(stack_in[side], at(sp, b, stack_in[side], 0))
                    sp.wait_ge(part3_ok, at(sp, b, part3_ok, side + 1))
                    if side == 0:
                        for half in range(2):
                            sp.dma_start(q_parts[half].rearrange("c p n -> p c n"),
                                         parts[:, 0, :, half * HALF:(half + 1) * HALF]).then_inc(parts_out, 16)
                    else:
                        sp.dma_start(k_parts.rearrange("c p n -> p c n"), parts[:, 1]).then_inc(parts_out, 16)
                for g in range(2):
                    yield "stack", g
                    sp.wait_ge(parts_out, at(sp, b, parts_out, 48))
                    heads = slice(4 * g, 4 * g + 4)
                    for t, k, part in RUNS[0]:
                        sp.dma_start(qs[D3 * t:D3 * (t + k), 2 * g:2 * g + 2].rearrange("p u h n -> p u (h n)"),
                                     q_parts[:, part:part + k].rearrange("u c (d h) n -> (c d) u h n", h=H3)[:, :, heads]
                                     .rearrange("p u h n -> p u (h n)")).then_inc(stack_in[g], 16)
                    for t, k, part in RUNS[1]:
                        sp.dma_start(ks[D3 * t:D3 * (t + k), heads],
                                     k_parts[part:part + k].rearrange("c (d h) n -> (c d) h n", h=H3)[:, heads])\
                            .then_inc(stack_in[g], 16)
                load_adj(2)
                for t in range(QT):
                    yield "max", 2 * t + 1
                    load_adj(t + 3)
                for u in range(QUARTERS):
                    yield "shift row", u
                    sp.wait_ge(shT_ok, at(sp, b, shT_ok, u + 1))
                    sp.dma_start(qs[KQ:KQ + 1, u].rearrange("o h (t n) -> o (h t) n", n=P), shT[:, u])\
                        .then_inc(shift_in, 16)
                    for t in range(QT):
                        m = QT * (u + 1) + t + 3
                        if m < 2 * NT:
                            yield "att", u, 2 * t + 1
                            load_adj(m)
                yield "ln3"
                sp.wait_ge(ln3_ok, at(sp, b, ln3_ok, NT))
                sp.dma_start(of(out_d, b), o3n).then_inc(stored, 16)

            turns(sp, "sp", early, late, first)
            sp.wait_ge(stored, at(sp, B, stored, 0))

        W_ALL = 16 * (len(names) + 1 + 2 * H0 + 3 + 1 + 1 + 4 + 2 + 1)

        @block.gpsimd
        def _(pool):
            def early(b):
                yield "adj", 0
                pool.wait_ge(adja_in[0], at(pool, b, adja_in[0], 16))
                pool.wait_ge(ln_ok, at(pool, b, ln_ok, 0))
                pool.tensor_tensor(a25[:], adja[0:GN, 0, 0:GN], ident[0:GN, 0:GN], ALU.add).then_inc(agr_ok, 1)
                pool.wait_ge(agr_ok, at(pool, b, agr_ok, 1))
                pool.tensor_tensor(agr[:], a25[:].unsqueeze(1).broadcast_to([GN, G, GN]), gpair[:], ALU.mult)\
                    .then_inc(agr_ok, 1)
                yield "tall"
                pool.wait_ge(tmax_ok, at(pool, b, tmax_ok, 1)).then_inc(waits_alone, 1)
                pool.partition_all_reduce(tall[:], tmx[:], P, RMAX).then_inc(tall_ok, 1)
                yield "v0"
                pool.wait_ge(tBE_ok, at(pool, b, tBE_ok, 2))
                pool.wait_ge(h0_ok, at(pool, b, h0_ok, 3))
                pool.tensor_tensor(v0[:, :, :, 0:D0], hx[:, :, 0:D].rearrange("p t (h d) -> p t h d", h=H0),
                                   tB[:].unsqueeze(3).broadcast_to([P, NT, H0, D0]), ALU.mult).then_inc(v0_ok, 1)
                pool.tensor_copy(v0[:, :, :, D0:D0 + 1], tB[:].unsqueeze(3)).then_inc(v0_ok, 1)
                first = b * NT if isinstance(b, int) else (b[0] + b[1]) * NT
                pool.tensor_copy(msk[:], maskall[:, bass.ds(first, NT)]).then_inc(mask_ok, 1)
                for g in range(2):
                    yield "y0", g
                    pool.wait_ge(emp_ok, at(pool, b, emp_ok, g + 1))
                    pool.wait_ge(hsum_ok, at(pool, b, hsum_ok, 1))
                    if g == 1:
                        pool.wait_ge(y0_ok, at(pool, b, y0_ok, 1))
                    pool.tensor_tensor(
                        eh.rearrange("p t (h d) -> p t h d", h=2),
                        emp[:, :, 2 * g:2 * g + 2].unsqueeze(3).broadcast_to([P, NT, 2, D0]),
                        hsum[:, C0 * g:C0 * g + C0].rearrange("p (h d) -> p h d", h=2).unsqueeze(1)
                        .broadcast_to([P, NT, 2, D0]), ALU.mult).then_inc(eh_ok, 1)

            pool.memset(ablk, 0.0).then_inc(setup_g, 1)
            pool.memset(ones[:], 1.0).then_inc(setup_g, 1)
            pool.memset(v0_all[:], 0.0).then_inc(setup_g, 1)
            pool.memset(v3_all[:], 0.0).then_inc(setup_g, 1)
            pool.memset(epst[:], EPS).then_inc(setup_g, 1)
            pool.memset(hx[:], 1.0).then_inc(setup_g, 1)
            pool.wait_ge(setup_g, 6)
            pool.memset(v3[:, :, :, D3:D3 + 1], 1.0).then_inc(setup_g, 1)
            pool.wait_ge(first_in, 32)
            first = early(0)
            advance(first, 2)
            pool.wait_ge(setup_v, SETUP_V)

            def late(b):
                def mask(m):
                    for half in range(2):
                        pool.wait_ge(adjb_in[half], at(pool, b, adjb_in[half], 16 * (m + 1)))
                        pool.wait_ge(mx_ok, at(pool, b, mx_ok, 8 * max(m - 1, 0))).then_inc(waits_alone, 1)
                        pool.tensor_scalar(neg[:, m % 2, half * HALF:(half + 1) * HALF], adjb[:, half], -1.0, BIG,
                                           ALU.add, ALU.mult).then_inc(neg_ok, 1)

                yield "x3"
                pool.wait_ge(ln_ok, at(pool, b, ln_ok, 3 * NT))
                pool.wait_ge(y3_ok, at(pool, b, y3_ok, 0)).then_inc(waits_alone, 1)
                pool.tensor_copy(x3[:], xr[:]).then_inc(x3_ok, 1)
                mask(0)
                yield "qk"
                mask(1)
                for t in range(QT):
                    yield "max", 2 * t + 1
                    mask(t + 2)
                for m in range(QT + 2, 2 * NT):
                    yield "att", (m - 2) // QT - 1, 2 * ((m - 2) % QT) + 1
                    mask(m)

            turns(pool, "pool", early, late, first)

        @block.scalar
        def _(act):
            def copy(out, in_, s, scale=1.0):
                nc.scalar.activation(out, in_, ACT.Copy, scale=scale).then_inc(s, 1)

            def early(b):
                def root(layer):
                    act.wait_ge(ln_aggr, at(act, b, ln_aggr, NT * (layer + 1)))
                    nc.scalar.activation(sd[:], mv[:, :, 1], ACT.Sqrt, bias=epst[:, 0:1]).then_inc(ln_root, 1)

                act.wait_ge(negT_ok, at(act, b, negT_ok, 0))
                for t in range(NT):
                    yield "adj", t
                    for part in range(2):
                        u = 2 * t + part
                        act.wait_ge(adjT_ps, at(act, b, adjT_ps, u + 1))
                        copy(adjT[:, 4 * part:4 * part + 4, t * P:(t + 1) * P],
                             banks(u % 3, 1).rearrange("p (j n) -> p j n", j=4), adjT_ok)
                yield "h0"
                act.wait_ge(xT_ps, at(act, b, xT_ps, 1))
                copy(xT[:], banks(0, 2), xT_ok)
                yield "h0x"
                act.wait_ge(t_ok, at(act, b, t_ok, 3))
                for _, bank, t, k in threes():
                    copy(hx[:, t:t + k, 0:D],
                         bank[:, 0:k * (D + H0)].rearrange("p (t n) -> p t n", t=k)[:, :, 0:D], h0_ok)
                yield "v0"
                act.wait_ge(hsum_ps, at(act, b, hsum_ps, 1))
                copy(hsum[:], banks(2, 1)[:, 0:D], hsum_ok)
                act.wait_ge(td_ok, at(act, b, td_ok, 1))
                nc.scalar.activation(tB[:], tt[:], ACT.Exp, scale=0.2).then_inc(tBE_ok, 1)
                nc.scalar.activation(tE[:], tt[:], ACT.Exp, scale=0.8).then_inc(tBE_ok, 1)
                for g in range(2):
                    for q in range(2):
                        yield "c", g, q
                        act.wait_ge(c_relu, at(act, b, c_relu, 2 * g + q + 1))
                        nc.scalar.activation(cs[:, q], cs[:, q], ACT.Exp, scale=-0.8).then_inc(c_ok, 1)
                    yield "o", g
                    act.wait_ge(pv0, at(act, b, pv0, NT * (g + 1)))
                    copy(oT[:, g], banks(0, 2), oT0_ok)
                yield "mean0"
                root(0)
                yield "h1"
                act.wait_ge(xT_ps, at(act, b, xT_ps, 2))
                copy(xT[:], banks(0, 2), xT_ok)
                yield "h1x"
                act.wait_ge(s2_ok, at(act, b, s2_ok, 3))
                for _, bank, t, k in threes():
                    copy(hx[:, t:t + k, 0:D],
                         bank[:, 0:k * (D + 1)].rearrange("p (t n) -> p t n", t=k)[:, :, 0:D], h1_ok)
                yield "s1"
                act.wait_ge(s1_ps, at(act, b, s1_ps, 1))
                copy(cs[:, 0], banks(0, 2), s1_ok)
                act.wait_ge(deg_ok, at(act, b, deg_ok, 3))
                nc.scalar.activation(deg[:, 3], deg[:, 2], ACT.Sqrt).then_inc(degroot_ok, 1)
                for t in range(NT):
                    yield "att1", t
                    if t == 0:
                        act.wait_ge(s1_ok, at(act, b, s1_ok, 1))
                    if t >= 2:
                        act.wait_ge(p1_ok, at(act, b, p1_ok, t - 1))
                    nc.scalar.activation(oT[:, t % 2], cs[:, 0], ACT.Sigmoid, bias=s2[:, t:t + 1]).then_inc(sig_ok, 1)
                yield "mean1"
                root(1)
                yield "x25"
                act.wait_ge(x25_ps, at(act, b, x25_ps, 1))
                copy(x25T[:], banks(0, 1)[:, 0:GN], x25_ok)
                yield "sup1"
                act.wait_ge(sup1_ps, at(act, b, sup1_ps, 1))
                copy(sup1, banks(0, 3)[0:GN, 0:G * DH], sup1_ok)
                yield "sup2"
                act.wait_ge(sup2_ps, at(act, b, sup2_ps, 1))
                copy(sup2, banks(1, 2)[0:GN, 0:G * D], sup2_ok)
                yield "mean2"
                root(2)

            first = early(0)
            advance(first, 1 + AHEAD)
            act.wait_ge(setup_v, 5)
            nc.scalar.activation(gw[:], gw[:], ACT.Exp).then_inc(setup_a, 1)
            advance(first, NT - AHEAD)
            act.wait_ge(setup_v, SETUP_V)

            def late(b):
                yield "x3T"
                act.wait_ge(x3T_ps, at(act, b, x3T_ps, 1))
                copy(x3T, banks(3, 2), x3T_ok)
                yield "qk"
                for side, scale in enumerate([0.25, 1.0]):
                    act.wait_ge(qk_ps, at(act, b, qk_ps, side + 1))
                    copy(parts[:, side, 0], banks(5 - 2 * side, 2), part1_ok, scale)
                yield "rest"
                for side in range(2):
                    act.wait_ge(rest_ok, at(act, b, rest_ok, side + 1))
                    copy(parts[:, side, 1], rest[:, side], part2_ok)
                yield "parts"
                act.wait_ge(v_ps, at(act, b, v_ps, 1))
                copy(v3[:, :, :, 0:D3], banks(5, 2).rearrange("p (t h d) -> p t h d", t=NT, h=H3), v3_ok)
                for u in range(QUARTERS):
                    yield "shift", u
                    act.wait_ge(shT_ps, at(act, b, shT_ps, u + 1))
                    copy(shT[:, u], banks(BANK["shift", u], 1)[0:4 * QT, 0:P], shT_ok)
                    for t in range(NT):
                        yield "att", u, t
                        for k in range(UNITS * u + 4 * t, UNITS * u + 4 * t + 4):
                            act.wait_ge(sc_ps, at(act, b, sc_ps, k + 1))
                            if k >= SLOTS:
                                act.wait_ge(pv3, at(act, b, pv3, (k - SLOTS) // 4 + 1))
                            nc.scalar.activation(ring[:, k % SLOTS], banks(BANK["score", k], 1), ACT.Exp)\
                                .then_inc(p3_ok, 1)
                    yield "end", u
                    act.wait_ge(pv3, at(act, b, pv3, NT * (u + 1)))
                    if u == 2:
                        act.wait_ge(stored, at(act, b, stored, 0))
                    copy(oz[:, u // 2, u % 2 * HALF:(u % 2 + 1) * HALF], banks(3, 1), oT3_ok)
                yield "on"
                act.wait_ge(onT_ps, at(act, b, onT_ps, 1))
                copy(oz[:, 0], banks(3, 2), onT_ok)
                yield "mean3"
                act.wait_ge(ln3_aggr, at(act, b, ln3_aggr, NT))
                nc.scalar.activation(sd3[:], mv3[:, :, 1], ACT.Sqrt, bias=epst[:, 0:1]).then_inc(ln3_root, 1)

            turns(act, "act", early, late, first)

        @block.vector
        def _(dve):
            steps = [0]

            def step(ins):
                ins.then_inc(setup_v, 1)
                steps[0] += 1
                dve.wait_ge(setup_v, steps[0])

            dve.wait_ge(weights_in, W_ALL)
            step(nc.vector.tensor_copy(identb[:], ident[:]))
            step(nc.vector.tensor_copy(w0x[:, 0:D], raw[:, 0]))
            step(nc.vector.tensor_copy(gw[:], fus))
            step(nc.vector.reduce_max(small[0:GN, 0:1], gw[:], AX_X))
            step(nc.vector.tensor_scalar(gw[:], gw[:], small[0:GN, 0:1], None, ALU.subtract))
            dve.wait_ge(setup_t, 1)
            step(nc.vector.tensor_copy(w0t, banks(4, 1)[:, 0:P]))
            step(nc.vector.tensor_copy(w1x[:, 0:D], banks(4, 1)[:, P:2 * P]))
            step(nc.vector.tensor_copy(wT[:, 0:2].rearrange("p w (d h) -> p w h d", h=H3),
                                       banks(4, 2)[:, 2 * P:4 * P].rearrange("p (w h d) -> p w h d", w=2, h=H3)))
            step(nc.vector.tensor_copy(wT[:, 2:4], banks(4, 2)[:, 4 * P:6 * P].rearrange("p (w n) -> p w n", w=2)))
            step(nc.vector.tensor_copy(maskall[:], banks(6, 1)[:, 0:B * NT]))
            dve.wait_ge(setup_t, 2)
            step(nc.vector.tensor_copy(w0x[:, D:D + H0], banks(7, 1)[:, H0:2 * H0]))
            step(nc.vector.tensor_copy(small[:, 0:H0], banks(7, 1)[:, 0:H0]))
            step(nc.vector.tensor_copy(small[:, H0:H0 + 2], banks(7, 1)[:, 16:18]))
            dve.wait_ge(setup_g, 7)
            for h in range(H0):
                step(nc.vector.tensor_scalar(w0s[:, h], ones[:], small[:, h:h + 1], None, ALU.mult))
            step(nc.vector.tensor_scalar(w1s[:], ones[:], small[:, H0:H0 + 1], None, ALU.mult))
            step(nc.vector.tensor_copy(w1x[:, D:D + 1], small[:, H0 + 1:H0 + 2]))
            step(nc.vector.reduce_sum(b1x[:, D:D + 1], banks(7, 1)[0:1, 32:34], AX_X))
            step(nc.vector.tensor_tensor(b1x[:, D:D + 1], b1x[:, D:D + 1], attb, ALU.add))
            dve.wait_ge(setup_a, 1)
            step(nc.vector.reduce_sum(small[0:GN, 6:7], gw[:], AX_X))
            step(nc.vector.reciprocal(small[0:GN, 7:8], small[0:GN, 6:7]))
            step(nc.vector.scalar_tensor_tensor(out=gw[:], in0=gw[:], scalar=small[0:GN, 7:8], in1=grow[:],
                                                op0=ALU.mult, op1=ALU.mult))
            step(nc.vector.memset(qk[KQ:KQ + 1, :], 1.0))
            assert steps[0] == SETUP_V

            def early(b):
                def means(layer, src):
                    for t in range(NT):
                        nc.vector.bn_stats(stats[:, t], src[:, t]).then_inc(ln_stats, 1)
                    dve.wait_ge(ln_stats, at(dve, b, ln_stats, NT * (layer + 1))).then_inc(waits_alone, 1)
                    for t in range(NT):
                        nc.vector.bn_aggr(mv[:, t], stats[:, t]).then_inc(ln_aggr, 1)

                def norm(layer, src, out):
                    dve.wait_ge(ln_root, at(dve, b, ln_root, layer + 1))
                    nc.vector.reciprocal(sd[:], sd[:]).then_inc(ln_rec, 1)
                    dve.wait_ge(ln_rec, at(dve, b, ln_rec, layer + 1))
                    for t in range(NT):
                        nc.vector.tensor_scalar(out[:, t], src[:, t], mv[:, t, 0:1], sd[:, t:t + 1],
                                                ALU.subtract, ALU.mult).then_inc(ln_ok, 1)

                yield "h0x"
                dve.wait_ge(h0_ps, at(dve, b, h0_ps, 1))
                for _, bank, t, k in threes():
                    nc.vector.tensor_copy(tt[:, t:t + k], bank[:, 0:k * (D + H0)].rearrange(
                        "p (t n) -> p t n", t=k)[:, :, D:D + H0]).then_inc(t_ok, 1)
                dve.wait_ge(t_ok, at(dve, b, t_ok, 3))
                nc.vector.reduce_max(tmx[:], tt[:].rearrange("p t h -> p h t"), AX_X).then_inc(tmax_ok, 1)
                yield "tall"
                dve.wait_ge(tall_ok, at(dve, b, tall_ok, 1))
                nc.vector.tensor_tensor(tt[:], tt[:], tall[:].unsqueeze(1).broadcast_to([P, NT, H0]), ALU.subtract)\
                    .then_inc(td_ok, 1)
                for g in range(2):
                    for q in range(2):
                        yield "c", g, q
                        h = 2 * g + q
                        dve.wait_ge(s0_ps, at(dve, b, s0_ps, h + 1))
                        nc.vector.tensor_scalar(cs[:, q], banks(0, 2), tall[:, h:h + 1], 0.0, ALU.add, ALU.max)\
                            .then_inc(c_relu, 1)
                    if g == 0:
                        dve.wait_ge(tBE_ok, at(dve, b, tBE_ok, 2))
                    for t in range(NT):
                        yield "p0", g, t
                        for q in range(2):
                            m, h = NT * g + t, 2 * g + q
                            if t == 0:
                                dve.wait_ge(c_ok, at(dve, b, c_ok, h + 1))
                            if m >= 2 and q == 0:
                                dve.wait_ge(pv0, at(dve, b, pv0, m - 1))
                            nc.vector.scalar_tensor_tensor(
                                out=ringa[:, 2 * (m % 2) + q], in0=cs[:, q], scalar=tE[:, t, h:h + 1], in1=adjT[:, t],
                                op0=ALU.max, op1=ALU.mult).then_inc(p0_ok, 1)
                    yield "o", g
                    O0 = tiles(0).rearrange("p t (h c) -> p t h c", c=C0)
                    mine = slice(2 * g, 2 * g + 2)
                    y4 = yr[:, :, C0 * g:C0 * g + C0].rearrange("p t (h d) -> p t h d", h=2)
                    dve.wait_ge(o0_ps, at(dve, b, o0_ps, g + 1))
                    nc.vector.tensor_scalar(emp[:, :, mine], O0[:, :, :, D0], 0.0, None, ALU.is_equal)\
                        .then_inc(emp_ok, 1)
                    dve.wait_ge(emp_ok, at(dve, b, emp_ok, g + 1))
                    nc.vector.scalar_tensor_tensor(out=den[:, :, mine], in0=emp[:, :, mine], scalar=float(N),
                                                   in1=O0[:, :, :, D0], op0=ALU.mult, op1=ALU.add).then_inc(den0_ok, 1)
                    dve.wait_ge(den0_ok, at(dve, b, den0_ok, 2 * g + 1))
                    nc.vector.reciprocal(den[:, :, mine], den[:, :, mine]).then_inc(den0_ok, 1)
                    yield "y0", g
                    dve.wait_ge(eh_ok, at(dve, b, eh_ok, g + 1))
                    nc.vector.tensor_tensor(y4, O0[:, :, :, 0:D0], eh.rearrange("p t (h d) -> p t h d", h=2),
                                            ALU.add).then_inc(y0_ok, 1)
                    dve.wait_ge(den0_ok, at(dve, b, den0_ok, 2 * g + 2))
                    dve.wait_ge(y0_ok, at(dve, b, y0_ok, 2 * g + 1))
                    nc.vector.tensor_tensor(y4, y4, den[:, :, mine].unsqueeze(3).broadcast_to([P, NT, 2, D0]), ALU.mult)\
                        .then_inc(y0_ok, 1)
                yield "mean0"
                dve.wait_ge(x_in, at(dve, b, x_in, 16))
                dve.wait_ge(y0_ok, at(dve, b, y0_ok, 4))
                nc.vector.tensor_tensor(yr[:], yr[:], xr[:], ALU.add).then_inc(y0_ok, 1)
                dve.wait_ge(y0_ok, at(dve, b, y0_ok, 5))
                means(0, yr)
                yield "ln0"
                norm(0, yr, xr)
                yield "h1x"
                dve.wait_ge(h1_ps, at(dve, b, h1_ps, 1))
                for _, bank, t, k in threes():
                    nc.vector.tensor_copy(s2[:, t:t + k], bank[:, 0:k * (D + 1)].rearrange(
                        "p (t n) -> p t n", t=k)[:, :, D]).then_inc(s2_ok, 1)
                dve.wait_ge(agr_ok, at(dve, b, agr_ok, 2))
                nc.vector.reduce_sum(deg[:, 0], agr[:], AX_X).then_inc(deg_ok, 1)
                dve.wait_ge(deg_ok, at(dve, b, deg_ok, 1))
                nc.vector.tensor_scalar(deg[:, 1], deg[:, 0], 0.0, None, ALU.is_equal).then_inc(deg_ok, 1)
                dve.wait_ge(deg_ok, at(dve, b, deg_ok, 2))
                nc.vector.tensor_tensor(deg[:, 2], deg[:, 0], deg[:, 1], ALU.add).then_inc(deg_ok, 1)
                yield "s1"
                dve.wait_ge(degroot_ok, at(dve, b, degroot_ok, 1))
                nc.vector.reciprocal(deg[:, 2], deg[:, 3]).then_inc(dinv_ok, 1)
                nc.vector.tensor_scalar(deg[:, 0], deg[:, 1], -1.0, 1.0, ALU.mult, ALU.add).then_inc(dinv_ok, 1)
                dve.wait_ge(dinv_ok, at(dve, b, dinv_ok, 2))
                nc.vector.tensor_tensor(deg[:, 3], deg[:, 2], deg[:, 0], ALU.mult).then_inc(dinv_ok, 1)
                dve.wait_ge(dinv_ok, at(dve, b, dinv_ok, 3))
                dinv = deg[:, 3].unsqueeze(2).broadcast_to([GN, G, GN])
                nc.vector.tensor_tensor(nadj[:], agr[:], dinv, ALU.mult).then_inc(nadj_ok, 1)
                yield "nT"
                dve.wait_ge(nadjT_ps, at(dve, b, nadjT_ps, 1))
                nc.vector.tensor_tensor(nT[:], banks(2, 1)[0:GN, 0:G * GN].rearrange("p (g n) -> p g n", g=G), dinv,
                                        ALU.mult).then_inc(nadjT_ok, 1)
                for t in range(NT):
                    yield "att1", t
                    if t == 0:
                        dve.wait_ge(mask_ok, at(dve, b, mask_ok, 1))
                    dve.wait_ge(sig_ok, at(dve, b, sig_ok, t + 1))
                    if t >= 4:
                        dve.wait_ge(pv1, at(dve, b, pv1, t - 3))
                    nc.vector.scalar_tensor_tensor(out=ringa[:, t % 4], in0=oT[:, t % 2], scalar=msk[:, t:t + 1],
                                                   in1=adjT[:, t], op0=ALU.mult, op1=ALU.mult).then_inc(p1_ok, 1)
                yield "y1"
                dve.wait_ge(pv1, at(dve, b, pv1, NT))
                sums = [(bank[:, 0:k * (D + 1)].rearrange("p (t n) -> p t n", t=k), slice(t, t + k))
                        for _, bank, t, k in threes()]
                for o, t in sums:
                    nc.vector.tensor_tensor(fac[:, t], o[:, :, D], msk[:, t], ALU.mult).then_inc(fac_ok, 1)
                dve.wait_ge(fac_ok, at(dve, b, fac_ok, 3))
                nc.vector.tensor_scalar(fac[:], fac[:], 1e-8, None, ALU.add).then_inc(fac_ok, 1)
                dve.wait_ge(fac_ok, at(dve, b, fac_ok, 4))
                nc.vector.reciprocal(fac[:], fac[:]).then_inc(fac_ok, 1)
                dve.wait_ge(fac_ok, at(dve, b, fac_ok, 5))
                nc.vector.tensor_tensor(fac[:], fac[:], msk[:], ALU.mult).then_inc(fac_ok, 1)
                dve.wait_ge(fac_ok, at(dve, b, fac_ok, 6))
                nc.vector.tensor_tensor(fac[:], fac[:], msk[:], ALU.mult).then_inc(fac_ok, 1)
                dve.wait_ge(fac_ok, at(dve, b, fac_ok, 7))
                for o, t in sums:
                    nc.vector.tensor_tensor(yr[:, t], o[:, :, 0:D],
                                            fac[:, t].unsqueeze(2).broadcast_to([P, t.stop - t.start, D]), ALU.mult)\
                        .then_inc(y1_ok, 1)
                yield "mean1"
                dve.wait_ge(y1_ok, at(dve, b, y1_ok, 3))
                nc.vector.tensor_tensor(yr[:], yr[:], xr[:], ALU.add).then_inc(y1_ok, 1)
                dve.wait_ge(y1_ok, at(dve, b, y1_ok, 4))
                means(1, yr)
                yield "ln1"
                norm(1, yr, xr)
                yield "h25"
                dve.wait_ge(h25_ps, at(dve, b, h25_ps, 1))
                nc.vector.tensor_tensor(h25, banks(0, 1)[:, 0:2 * G * GN].rearrange("p (g n) -> p g n", n=GN),
                                        b2a[:].unsqueeze(2).broadcast_to([P, 2 * G, GN]), ALU.add).then_inc(h25_ok, 1)
                dve.wait_ge(h25_ok, at(dve, b, h25_ok, 1))
                nc.vector.tensor_scalar(h25, h25, 0.0, None, ALU.max).then_inc(h25_ok, 1)
                yield "o25"
                dve.wait_ge(o25_ps, at(dve, b, o25_ps, 1))
                for g in range(G):
                    nc.vector.tensor_scalar(o25[:, g], banks(0, 2)[0:GN, g * D:(g + 1) * D], 0.0, gw[:, g:g + 1],
                                            ALU.max, ALU.mult).then_inc(o25_ok, 1)
                dve.wait_ge(o25_ok, at(dve, b, o25_ok, G))
                nc.vector.tensor_reduce(f25[:], o25[:].rearrange("p g d -> p d g"), AX_X, ALU.add).then_inc(o25_ok, 1)
                dve.wait_ge(o25_ok, at(dve, b, o25_ok, G + 1))
                nc.vector.tensor_tensor(xr[0:GN, 0], xr[0:GN, 0], f25[:], ALU.add).then_inc(o25_ok, 1)
                yield "mean2"
                dve.wait_ge(o25_ok, at(dve, b, o25_ok, G + 2))
                means(2, xr)
                yield "ln2"
                norm(2, xr, xr)
                yield "negT"
                dve.wait_ge(sc_ps, at(dve, b, sc_ps, 0))
                nc.vector.tensor_scalar(negT[:], adjT[:], -1.0, BIG, ALU.add, ALU.mult).then_inc(negT_ok, 1)

            def late(b):
                def maximum(k):
                    u, t, q, half = max_unit(k)
                    if k % 8 == 0:
                        dve.wait_ge(neg_ok, at(dve, b, neg_ok, 2 * (k // 8) + 2))
                    dve.wait_ge(mx_ok, at(dve, b, mx_ok, max(k - 1, 0)))
                    dve.wait_ge(mxs_ps, at(dve, b, mxs_ps, k + 1)).then_inc(waits_alone, 1)
                    nc.vector.tensor_tensor_reduce(
                        out=junk[:, k % 2], in0=banks(BANK["max", k], 1), in1=neg[:, t % 2, half * HALF:(half + 1) * HALF],
                        scale=1.0, scalar=-3e38, op0=ALU.add, op1=ALU.max,
                        accum_out=mx[:, half, u, q, t:t + 1]).then_inc(mx_ok, 1)

                def shift(u):
                    wb = web[:, 4 * (u // 2):4 * (u // 2) + 4].unsqueeze(2).broadcast_to([P, 4, QT])
                    dve.wait_ge(mx_ok, at(dve, b, mx_ok, UNITS * (u + 1)))
                    nc.vector.tensor_tensor(sh[:, u], mx[:, 0, u], mx[:, 1, u], ALU.max).then_inc(sh_ok, 1)
                    dve.wait_ge(sh_ok, at(dve, b, sh_ok, 3 * u + 1))
                    nc.vector.tensor_tensor(sh[:, u], sh[:, u], wb, ALU.add).then_inc(sh_ok, 1)
                    dve.wait_ge(sh_ok, at(dve, b, sh_ok, 3 * u + 2))
                    nc.vector.tensor_tensor(sh[:, u], wb, sh[:, u], ALU.subtract).then_inc(sh_ok, 1)

                yield "qk"
                for side, scale in enumerate([0.25, 1.0]):
                    dve.wait_ge(part1_ok, at(dve, b, part1_ok, side + 1))
                    nc.vector.scalar_tensor_tensor(out=rest[:, side], in0=banks(5 - 2 * side, 2), scalar=scale,
                                                   in1=parts[:, side, 0], op0=ALU.mult, op1=ALU.subtract)\
                        .then_inc(rest_ok, 1)
                yield "parts"
                for side in range(2):
                    dve.wait_ge(part2_ok, at(dve, b, part2_ok, side + 1))
                    nc.vector.tensor_tensor(parts[:, side, 2], rest[:, side], parts[:, side, 1], ALU.subtract)\
                        .then_inc(part3_ok, 1)
                for t in range(NT):
                    yield "max", t
                    for k in range(4 * t, 4 * t + 4):
                        maximum(k)
                for u in range(QUARTERS):
                    yield "shift", u
                    shift(u)
                    if u < QUARTERS - 1:
                        for t in range(NT):
                            yield "att", u, t
                            for k in range(UNITS * (u + 1) + 4 * t, UNITS * (u + 1) + 4 * t + 4):
                                maximum(k)
                yield "o3"
                for g in range(2):
                    O3 = tiles(3 + 2 * g).rearrange("p t (h c) -> p t h c", c=C3)
                    heads = slice(4 * g, 4 * g + 4)
                    dve.wait_ge(o3_ps, at(dve, b, o3_ps, 2))
                    nc.vector.reciprocal(den3[:, :, heads], O3[:, :, :, D3]).then_inc(den3_ok, 1)
                    dve.wait_ge(den3_ok, at(dve, b, den3_ok, g + 1))
                    nc.vector.tensor_tensor(
                        o3n[:, :, C0 * g:C0 * g + C0].rearrange("p t (h d) -> p t h d", h=4), O3[:, :, :, 0:D3],
                        den3[:, :, heads].unsqueeze(3).broadcast_to([P, NT, 4, D3]), ALU.mult).then_inc(on_ok, 1)
                yield "z"
                dve.wait_ge(z_ps, at(dve, b, z_ps, 1))
                dve.wait_ge(x3_ok, at(dve, b, x3_ok, 1))
                nc.vector.tensor_tensor(o3n, tiles(5), x3[:], ALU.add).then_inc(y3_ok, 1)
                yield "mean3"
                dve.wait_ge(y3_ok, at(dve, b, y3_ok, 1))
                for t in range(NT):
                    nc.vector.bn_stats(stat3[:, t], o3n[:, t]).then_inc(ln3_stats, 1)
                dve.wait_ge(ln3_stats, at(dve, b, ln3_stats, NT)).then_inc(waits_alone, 1)
                for t in range(NT):
                    nc.vector.bn_aggr(mv3[:, t], stat3[:, t]).then_inc(ln3_aggr, 1)
                yield "ln3"
                dve.wait_ge(ln3_root, at(dve, b, ln3_root, 1))
                nc.vector.reciprocal(sd3[:], sd3[:]).then_inc(ln3_rec, 1)
                dve.wait_ge(ln3_rec, at(dve, b, ln3_rec, 1))
                for t in range(NT):
                    nc.vector.tensor_scalar(o3n[:, t], o3n[:, t], mv3[:, t, 0:1], sd3[:, t:t + 1],
                                            ALU.subtract, ALU.mult).then_inc(ln3_ok, 1)

            turns(dve, "dve", early, late)

        @block.tensor
        def _(pe):
            mm, tr = nc.tensor.matmul, nc.tensor.transpose
            def turn_x(first, x, s):
                for t in range(NT):
                    last = tr(banks(first, 2)[:, t * P:(t + 1) * P], x[:, t], ident[:])
                last.then_inc(s, 1)

            def early(b):
                pe.wait_ge(ln_ok, at(pe, b, ln_ok, 0))
                for i in range(NT):
                    yield "adj", i
                    pe.wait_ge(adja_in[i % AHEAD], at(pe, b, adja_in[i % AHEAD], 16 * (i // AHEAD + 1)))
                    for part in range(2):
                        u = 2 * i + part
                        if u >= 3:
                            pe.wait_ge(adjT_ok, at(pe, b, adjT_ok, u - 2))
                        for j in range(4):
                            c = (4 * part + j) * P
                            last = tr(banks(u % 3, 1)[:, j * P:(j + 1) * P], adja[:, i % AHEAD, c:c + P], ident[:])
                        last.then_inc(adjT_ps, 1)
                yield "h0"
                pe.wait_ge(x_in, at(pe, b, x_in, 16))
                pe.wait_ge(adjT_ok, at(pe, b, adjT_ok, 2 * NT))
                turn_x(0, xr, xT_ps)
                yield "h0x"
                pe.wait_ge(xT_ok, at(pe, b, xT_ok, 1))
                for _, bank, t, k in threes():
                    for i in range(k):
                        last = mm(bank[:, i * (D + H0):(i + 1) * (D + H0)], xT[:, (t + i) * P:(t + i + 1) * P], w0x[:],
                                  start=True, stop=True)
                last.then_inc(h0_ps, 1)
                yield "tB"
                pe.wait_ge(h0_ok, at(pe, b, h0_ok, 3))
                for t in range(NT):
                    last = mm(banks(2, 1)[:, 0:D], ones[:], hx[:, t, 0:D], start=(t == 0), stop=(t == NT - 1))
                last.then_inc(hsum_ps, 1)
                for g in range(2):
                    for q in range(2):
                        yield "c", g, q
                        h = 2 * g + q
                        if q == 1:
                            pe.wait_ge(c_relu, at(pe, b, c_relu, h))
                        elif g == 1:
                            pe.wait_ge(y0_ok, at(pe, b, y0_ok, 1))
                        for half in range(2):
                            last = mm(banks(half, 1), w0s[:, h], xT[:, half * HALF:(half + 1) * HALF],
                                      start=True, stop=True)
                        last.then_inc(s0_ps, 1)
                    for t in range(NT):
                        yield "p0", g, t
                        m = NT * g + t
                        if t == 0:
                            pe.wait_ge(c_relu, at(pe, b, c_relu, 2 * g + 2))
                            pe.wait_ge(v0_ok, at(pe, b, v0_ok, 2))
                        pe.wait_ge(p0_ok, at(pe, b, p0_ok, 2 * (m + 1)))
                        for half in range(2):
                            for q in range(2):
                                first = (H0 * t + 2 * g + q) * (D0 + 1)
                                last = mm(banks(half, 1)[C0 * q:C0 * (q + 1)], v0_all[:, first:first + C0],
                                          ringa[:, 2 * (m % 2) + q, half * HALF:(half + 1) * HALF],
                                          start=(t == 0), stop=(t == NT - 1))
                        last.then_inc(pv0, 1)
                    yield "o", g
                    pe.wait_ge(oT0_ok, at(pe, b, oT0_ok, g + 1)).then_inc(waits_alone, 1)
                    for t in range(NT):
                        last = tr(tiles(0)[:, t], oT[:, g, t * P:(t + 1) * P], ident[:])
                    last.then_inc(o0_ps, 1)
                yield "h1"
                pe.wait_ge(ln_ok, at(pe, b, ln_ok, NT))
                turn_x(0, xr, xT_ps)
                yield "h1x"
                pe.wait_ge(xT_ok, at(pe, b, xT_ok, 2))
                for _, bank, t, k in threes():
                    for i in range(k):
                        out = bank[:, i * (D + 1):(i + 1) * (D + 1)]
                        mm(out, ones[0:1, :], b1x[:], start=True, stop=False)
                        last = mm(out, xT[:, (t + i) * P:(t + i + 1) * P], w1x[:], start=False, stop=True)
                last.then_inc(h1_ps, 1)
                yield "s1"
                pe.wait_ge(s2_ok, at(pe, b, s2_ok, 3))
                pe.wait_ge(h1_ok, at(pe, b, h1_ok, 3))
                for half in range(2):
                    last = mm(banks(half, 1), w1s[:], xT[:, half * HALF:(half + 1) * HALF], start=True, stop=True)
                last.then_inc(s1_ps, 1)
                yield "nT"
                pe.wait_ge(nadj_ok, at(pe, b, nadj_ok, 1)).then_inc(waits_alone, 1)
                for g in range(G):
                    last = tr(banks(2, 1)[0:GN, g * GN:(g + 1) * GN], nadj[:, g], ident[0:GN, 0:GN])
                last.then_inc(nadjT_ps, 1)
                for j in range(NT):
                    yield "att1", j
                    if j == 0:
                        pe.wait_ge(s1_ok, at(pe, b, s1_ok, 1))
                        pe.wait_ge(nadjT_ok, at(pe, b, nadjT_ok, 1))
                    pe.wait_ge(p1_ok, at(pe, b, p1_ok, j + 1))
                    for _, bank, t, k in threes():
                        for i in range(k):
                            last = mm(bank[:, i * (D + 1):(i + 1) * (D + 1)], ringa[:, j % 4, (t + i) * P:(t + i + 1) * P],
                                      hx[:, j], start=(j == 0 and i == 0), stop=(j == NT - 1), skip_group_check=True)
                    last.then_inc(pv1, 1)
                yield "x25"
                pe.wait_ge(ln_ok, at(pe, b, ln_ok, 2 * NT)).then_inc(waits_alone, 1)
                tr(banks(0, 1)[:, 0:GN], xr[0:GN, 0], ident[0:GN, 0:GN]).then_inc(x25_ps, 1)
                yield "sup1"
                pe.wait_ge(x25_ok, at(pe, b, x25_ok, 1))
                for c in range(0, G * DH, HALF):
                    w = min(HALF, G * DH - c)
                    last = mm(banks(0, 3)[0:GN, c:c + w], x25T[:], w2a[:, c:c + w], start=True, stop=True)
                last.then_inc(sup1_ps, 1)
                yield "h25"
                pe.wait_ge(sup1_ok, at(pe, b, sup1_ok, 1)).then_inc(waits_alone, 1)
                for n in range(2 * G):
                    last = mm(banks(0, 1)[:, n * GN:(n + 1) * GN], sup1[:, n * P:(n + 1) * P], nT[:, n // 2],
                              start=True, stop=True)
                last.then_inc(h25_ps, 1)
                yield "sup2"
                pe.wait_ge(h25_ok, at(pe, b, h25_ok, 2))
                for n in range(2 * G):
                    last = mm(banks(1, 2)[0:GN, n // 2 * D:(n // 2 + 1) * D], h25[:, n], w2b[:, n],
                              start=(n % 2 == 0), stop=(n % 2 == 1))
                last.then_inc(sup2_ps, 1)
                yield "o25"
                pe.wait_ge(sup2_ok, at(pe, b, sup2_ok, 1)).then_inc(waits_alone, 1)
                for g in range(G):
                    out = banks(0, 2)[0:GN, g * D:(g + 1) * D]
                    mm(out, ones[0:1, 0:GN], b2b[:, g * D:(g + 1) * D], start=True, stop=False)
                    last = mm(out, nT[:, g], sup2[:, g * D:(g + 1) * D], start=False, stop=True)
                last.then_inc(o25_ps, 1)

            pe.wait_ge(first_in, 32)
            first = early(0)
            advance(first, 1 + AHEAD)
            pe.wait_ge(weights_in, W_ALL)
            for n in range(len(names)):
                tr(banks(4, 2)[:, n * P:(n + 1) * P], raw[:, n], ident[:])
            tr(banks(6, 1)[:, 0:B * NT], mrow, ident[0:B * NT, 0:B * NT]).then_inc(setup_t, 1)
            pe.wait_ge(setup_v, 6)
            mm(banks(7, 1)[:, 0:2 * H0], w0t, ablk, start=True, stop=True)
            mm(banks(7, 1)[:, 16:18], raw[:, 1], acol[:, 0:2], start=True, stop=True)
            mm(banks(7, 1)[0:1, 32:34], acol[:, 2:3], acol[:, 0:2], start=True, stop=True).then_inc(setup_t, 1)
            advance(first, NT - AHEAD)
            pe.wait_ge(setup_v, SETUP_V)
            pe.wait_ge(setup_g, 7)

            def late(b):
                yield "x3"
                def free(key):
                    if BEFORE[key]:
                        what, k = BEFORE[key]
                        reader = {"max": mx_ok, "score": p3_ok, "shift": shT_ok}[what]
                        pe.wait_ge(reader, at(pe, b, reader, k + 1))
                    return banks(BANK[key], 1)

                def for_max(k):
                    u, t, q, half = max_unit(k)
                    mm(free(("max", k)), qs[0:KQ, u, q, t * P:(t + 1) * P],
                       ks[0:KQ, 4 * (u // 2) + q, half * HALF:(half + 1) * HALF], start=True, stop=True)\
                        .then_inc(mxs_ps, 1)

                def scores(k):
                    u, t, q = score_unit(k)
                    out, half = free(("score", k)), u % 2
                    mm(out, identb[:], negT[:, t, half * HALF:(half + 1) * HALF], start=True, stop=False)
                    mm(out, ks[:, 4 * (u // 2) + q, t * P:(t + 1) * P], qs[:, u, q], start=False, stop=True)\
                        .then_inc(sc_ps, 1)

                def values(u, t):
                    if u >= 1 and t == 0:
                        pe.wait_ge(oT3_ok, at(pe, b, oT3_ok, u))
                    pe.wait_ge(p3_ok, at(pe, b, p3_ok, UNITS * u + 4 * t + 4))
                    for q in range(4):
                        first = (H3 * t + 4 * (u // 2) + q) * (D3 + 1)
                        last = mm(banks(3, 1)[C3 * q:C3 * (q + 1)], v3_all[:, first:first + C3],
                                  ring[:, (UNITS * u + 4 * t + q) % SLOTS], start=(t == 0), stop=(t == NT - 1))
                    last.then_inc(pv3, 1)

                pe.wait_ge(ln_ok, at(pe, b, ln_ok, 3 * NT))
                turn_x(3, xr, x3T_ps)
                yield "qk"
                pe.wait_ge(x3T_ok, at(pe, b, x3T_ok, 1))
                for side in range(2):
                    for half in range(2):
                        last = mm(banks(5 - 2 * side + half, 1), wT[:, side], x3T[:, half * HALF:(half + 1) * HALF],
                                  start=True, stop=True)
                    last.then_inc(qk_ps, 1)
                yield "parts"
                pe.wait_ge(rest_ok, at(pe, b, rest_ok, 1))
                for t in range(NT):
                    last = mm(banks(5, 2)[:, t * P:(t + 1) * P], x3T[:, t * P:(t + 1) * P], wT[:, 2], start=True, stop=True)
                last.then_inc(v_ps, 1)
                for t in range(NT):
                    yield "max", t
                    if t == 0:
                        pe.wait_ge(v3_ok, at(pe, b, v3_ok, 1))
                        pe.wait_ge(rest_ok, at(pe, b, rest_ok, 2))
                        pe.wait_ge(stack_in[0], at(pe, b, stack_in[0], PER[stack_in[0]]))
                    for k in range(4 * t, 4 * t + 4):
                        for_max(k)
                for u in range(QUARTERS):
                    yield "shift", u
                    bank = free(("shift", u))
                    pe.wait_ge(sh_ok, at(pe, b, sh_ok, 3 * u + 3)).then_inc(waits_alone, 1)
                    tr(bank[0:4 * QT, 0:P], sh[:, u].rearrange("p h t -> p (h t)"), ident[:]).then_inc(shT_ps, 1)
                    for t in range(NT):
                        yield "att", u, t
                        if t == 0:
                            pe.wait_ge(shift_in, at(pe, b, shift_in, 16 * (u + 1)))
                            if u == 0:
                                pe.wait_ge(negT_ok, at(pe, b, negT_ok, 1))
                            if u == 1:
                                pe.wait_ge(stack_in[1], at(pe, b, stack_in[1], PER[stack_in[1]]))
                        for k in range(UNITS * u + 4 * t, UNITS * u + 4 * t + 4):
                            scores(k)
                            if u < QUARTERS - 1:
                                for_max(UNITS + k)
                            if t >= 1 and k % 4 == 1:
                                values(u, t - 1)
                    yield "end", u
                    values(u, NT - 1)
                yield "o3"
                pe.wait_ge(oT3_ok, at(pe, b, oT3_ok, QUARTERS))
                pe.wait_ge(p3_ok, at(pe, b, p3_ok, 16 * NT))
                for g in range(2):
                    for t in range(NT):
                        last = tr(tiles(3 + 2 * g)[:, t], oz[:, g, t * P:(t + 1) * P], ident[:])
                    last.then_inc(o3_ps, 1)
                yield "on"
                pe.wait_ge(on_ok, at(pe, b, on_ok, 2))
                turn_x(3, o3n, onT_ps)
                yield "z"
                pe.wait_ge(onT_ok, at(pe, b, onT_ok, 1))
                for t in range(NT):
                    last = mm(banks(5, 2)[:, t * P:(t + 1) * P], oz[:, 0, t * P:(t + 1) * P], wT[:, 3],
                              start=True, stop=True)
                last.then_inc(z_ps, 1)

            turns(pe, "pe", early, late, first)

_INS = ['x', 'adj', 'nodemask', 'L0_gnn_W', 'L0_gnn_a', 'L1_gnn_W', 'L1_gnn_b', 'L1_gnn_a1', 'L1_gnn_a2',
        'L1_gnn_att_b', 'L2_gnn_W1', 'L2_gnn_b1', 'L2_gnn_W2', 'L2_gnn_b2', 'L2_gnn_fusion_w', 'L3_gnn_W_q',
        'L3_gnn_W_k', 'L3_gnn_W_v', 'L3_gnn_W_e', 'L3_gnn_W_o']


def shape_constants():
    pair = np.zeros((GN, G, GN), np.float32)
    row = np.zeros((GN, G), np.float32)
    for g, nodes in enumerate(GROUPS):
        row[nodes, g] = 1.0
        pair[np.ix_(nodes, [g], nodes)] = 1.0
    return {"ident": np.eye(P, dtype=np.float32), "gpair": pair, "grow": row}


def kernel(**inputs):
    import concourse.bacc as _bacc
    from concourse.bass_utils import run_bass_kernel_spmd as _run

    nc = _bacc.Bacc("TRN2", target_bir_lowering=False, num_devices=1)
    arrays, aps = {}, {}
    for name in _INS:
        v = np.ascontiguousarray(inputs[name])
        arrays[name] = v.reshape(1) if v.ndim == 0 else v
    arrays.update(shape_constants())
    arrays = {f"in_{name}": v for name, v in arrays.items()}
    for name, v in arrays.items():
        aps[name[3:]] = nc.dram_tensor(name, v.shape, mybir.dt.from_np(v.dtype), kind="ExternalInput").ap()
    aps["out"] = nc.dram_tensor("out_nodes", (B, N, D), F32, kind="ExternalOutput").ap()
    build(nc, aps)
    return _run(nc, [arrays], core_ids=[0]).results[0]["out_nodes"]
```
